# Optimizing a Trainium2 kernel written in Bass

```python
import numpy as np
import jax
import jax.numpy as jnp

def _softmax(x, axis=-1):
    return jax.nn.softmax(x, axis=axis)

def _gelu(x):
    return jax.nn.gelu(x, approximate=True)

def _silu(x):
    return jax.nn.silu(x)

def _sigmoid(x):
    return jax.nn.sigmoid(x)

def _layernorm(x, axis=-1, eps=1e-05):
    m = jnp.mean(x, axis=axis, keepdims=True)
    v = jnp.var(x, axis=axis, keepdims=True)
    return (x - m) / jnp.sqrt(v + eps)

def _scatter_add(tgt, idx, src, axis=0):
    return tgt.at[idx].add(src)

def _segment_sum(src, seg, n):
    return jax.ops.segment_sum(src, seg, n)
kernel_name = 'mk_gnn_resnorm_d2_gnn_r8_8ad2d4'

def setup_inputs(seed: int=0):
    np.random.seed(seed)
    _w = jnp.asarray

    def _rec_inputs():
        import jax
        import jax.numpy as jnp
        _gk = jax.random.key(seed)
        x = -0.0003713 + 1 * jax.random.normal(jax.random.fold_in(_gk, 1), (6250, 256), jnp.float32)
        src = jax.random.randint(jax.random.fold_in(_gk, 2), (200000,), 0, 6250, jnp.int32)
        dst = jax.random.randint(jax.random.fold_in(_gk, 3), (200000,), 0, 6250, jnp.int32)
        _o = jnp.argsort(dst, stable=True)
        src = src[_o]
        dst = dst[_o]
        edge_weight = jax.random.uniform(jax.random.fold_in(_gk, 12), (200000,), jnp.float32, 0.0, 1)
        return (x, src, dst, edge_weight)
    x, src, dst, edge_weight = _rec_inputs()

    def _L0_gnn_setup():
        import jax, jax.numpy as jnp
        import numpy as np
        N_NODES = 6250
        N_EDGES = 200000
        IN_DIM = 256
        OUT_DIM = 256
        key = jax.random.key(seed)
        k1, k2, k3, k4, k5 = jax.random.split(key, 5)
        x = jax.random.normal(k1, (N_NODES, IN_DIM), dtype=jnp.float32)
        edge_row = jax.random.randint(k2, (N_EDGES,), 0, N_NODES, dtype=jnp.int32)
        edge_col = jax.random.randint(k3, (N_EDGES,), 0, N_NODES, dtype=jnp.int32)
        edge_val = jax.random.uniform(k4, (N_EDGES,), dtype=jnp.float32)
        limit = float(np.sqrt(6.0 / (IN_DIM + OUT_DIM)))
        W = jax.random.uniform(k5, (OUT_DIM, IN_DIM), dtype=jnp.float32, minval=-limit, maxval=limit)
        return {'x': x, 'edge_row': edge_row, 'edge_col': edge_col, 'edge_val': edge_val, 'W': W}
    _L0_gnn_all = _L0_gnn_setup()
    _L0_gnn_in = {k: v for k, v in _L0_gnn_all.items() if k in ('W',)}
    del _L0_gnn_all

    def _L1_gnn_setup():
        import jax, jax.numpy as jnp
        import numpy as np
        V = 6250
        E = 75000
        D = 256
        K = 20
        OUT = 256

        def layer_norm(x, g, b, eps=1e-05):
            mu = jnp.mean(x, axis=-1, keepdims=True)
            var = jnp.var(x, axis=-1, keepdims=True)
            return (x - mu) * jax.lax.rsqrt(var + eps) * g + b
        key = jax.random.key(seed)
        ks = jax.random.split(key, 12)

        def rn(k, shape, s=0.05):
            return jax.random.normal(k, shape, dtype=jnp.float32) * s
        return dict(node_feats=jax.random.normal(ks[0], (V, D), dtype=jnp.float32), src=jax.random.randint(ks[1], (E,), 0, V), dst=jax.random.randint(ks[2], (E,), 0, V), Wp=rn(ks[3], (D, K)), bp=jnp.zeros((K,), jnp.float32), gp=jnp.ones((K,), jnp.float32), betap=jnp.zeros((K,), jnp.float32), Wk=rn(ks[4], (K * K, OUT)), bk=jnp.zeros((OUT,), jnp.float32), gk=jnp.ones((OUT,), jnp.float32), betak=jnp.zeros((OUT,), jnp.float32), We=rn(ks[5], (2 * D, 1)), be=jnp.zeros((1,), jnp.float32), Wn=rn(ks[6], (D, D)), bn=jnp.zeros((D,), jnp.float32), W_ih=rn(ks[7], (3 * D, D)), W_hh=rn(ks[8], (3 * D, D)), b_ih=jnp.zeros((3 * D,), jnp.float32), b_hh=jnp.zeros((3 * D,), jnp.float32), g_ln=jnp.ones((D,), jnp.float32), beta_ln=jnp.zeros((D,), jnp.float32), Wc=rn(ks[9], (D + OUT, D)), bc=jnp.zeros((D,), jnp.float32), gc=jnp.ones((D,), jnp.float32), betac=jnp.zeros((D,), jnp.float32))
    _L1_gnn_all = _L1_gnn_setup()
    _L1_gnn_in = {k: v for k, v in _L1_gnn_all.items() if k in ('Wp', 'bp', 'gp', 'betap', 'Wk', 'bk', 'gk', 'betak', 'We', 'be', 'Wn', 'bn', 'W_ih', 'W_hh', 'b_ih', 'b_hh', 'g_ln', 'beta_ln', 'Wc', 'bc', 'gc', 'betac')}
    del _L1_gnn_all
    return {'x': x, 'src': src, 'dst': dst, 'edge_weight': edge_weight, 'L0_gnn_W': _L0_gnn_in['W'], 'L1_gnn_Wp': _L1_gnn_in['Wp'], 'L1_gnn_bp': _L1_gnn_in['bp'], 'L1_gnn_gp': _L1_gnn_in['gp'], 'L1_gnn_betap': _L1_gnn_in['betap'], 'L1_gnn_Wk': _L1_gnn_in['Wk'], 'L1_gnn_bk': _L1_gnn_in['bk'], 'L1_gnn_gk': _L1_gnn_in['gk'], 'L1_gnn_betak': _L1_gnn_in['betak'], 'L1_gnn_We': _L1_gnn_in['We'], 'L1_gnn_be': _L1_gnn_in['be'], 'L1_gnn_Wn': _L1_gnn_in['Wn'], 'L1_gnn_bn': _L1_gnn_in['bn'], 'L1_gnn_W_ih': _L1_gnn_in['W_ih'], 'L1_gnn_W_hh': _L1_gnn_in['W_hh'], 'L1_gnn_b_ih': _L1_gnn_in['b_ih'], 'L1_gnn_b_hh': _L1_gnn_in['b_hh'], 'L1_gnn_g_ln': _L1_gnn_in['g_ln'], 'L1_gnn_beta_ln': _L1_gnn_in['beta_ln'], 'L1_gnn_Wc': _L1_gnn_in['Wc'], 'L1_gnn_bc': _L1_gnn_in['bc'], 'L1_gnn_gc': _L1_gnn_in['gc'], 'L1_gnn_betac': _L1_gnn_in['betac']}

def reference(x, src, dst, edge_weight, L0_gnn_W, L1_gnn_Wp, L1_gnn_bp, L1_gnn_gp, L1_gnn_betap, L1_gnn_Wk, L1_gnn_bk, L1_gnn_gk, L1_gnn_betak, L1_gnn_We, L1_gnn_be, L1_gnn_Wn, L1_gnn_bn, L1_gnn_W_ih, L1_gnn_W_hh, L1_gnn_b_ih, L1_gnn_b_hh, L1_gnn_g_ln, L1_gnn_beta_ln, L1_gnn_Wc, L1_gnn_bc, L1_gnn_gc, L1_gnn_betac):
    import jax
    import jax.numpy as jnp

    def _L0_gnn_ref(x, edge_row, edge_col, edge_val, W):
        import jax, jax.numpy as jnp
        import numpy as np
        N_NODES = 6250
        N_EDGES = 200000
        IN_DIM = 256
        OUT_DIM = 256
        msgs = edge_val[:, None] * x[edge_col]
        agg = jax.ops.segment_sum(msgs, edge_row, num_segments=N_NODES)
        out = jnp.einsum('ni,oi->no', agg, W)
        return jax.nn.relu(out)

    def _L1_gnn_ref(node_feats, src, dst, Wp, bp, gp, betap, Wk, bk, gk, betak, We, be, Wn, bn, W_ih, W_hh, b_ih, b_hh, g_ln, beta_ln, Wc, bc, gc, betac):
        import jax, jax.numpy as jnp
        import numpy as np
        V = 6250
        E = 75000
        D = 256
        K = 20
        OUT = 256

        def layer_norm(x, g, b, eps=1e-05):
            mu = jnp.mean(x, axis=-1, keepdims=True)
            var = jnp.var(x, axis=-1, keepdims=True)
            return (x - mu) * jax.lax.rsqrt(var + eps) * g + b
        Vn = node_feats.shape[0]
        En = src.shape[0]
        npj = jax.nn.relu(layer_norm(node_feats @ Wp + bp, gp, betap))
        kron = jnp.einsum('ea,ek->eak', npj[src], npj[dst]).reshape(En, -1)
        kron = jax.nn.relu(layer_norm(kron @ Wk + bk, gk, betak))
        kron_feat = jax.ops.segment_sum(kron, dst, num_segments=Vn)
        he = jnp.concatenate([node_feats[dst], node_feats[src]], axis=1)
        logits = jax.nn.relu(he @ We + be)
        m = jax.ops.segment_max(logits, dst, num_segments=Vn)
        ex = jnp.exp(logits - m[dst])
        denom = jax.ops.segment_sum(ex, dst, num_segments=Vn)
        a = ex / denom[dst]
        hv = node_feats @ Wn + bn
        context = jax.nn.relu(jax.ops.segment_sum(hv[src] * a, dst, num_segments=Vn))
        gi = context @ W_ih.T + b_ih
        gh = node_feats @ W_hh.T + b_hh
        i_r, i_z, i_n = jnp.split(gi, 3, axis=1)
        h_r, h_z, h_n = jnp.split(gh, 3, axis=1)
        r = jax.nn.sigmoid(i_r + h_r)
        z = jax.nn.sigmoid(i_z + h_z)
        n = jnp.tanh(i_n + r * h_n)
        h = (1.0 - z) * n + z * node_feats
        gru_out = layer_norm(jax.nn.relu(h), g_ln, beta_ln)
        cat = jnp.concatenate([gru_out, kron_feat], axis=1)
        return jax.nn.relu(layer_norm(cat @ Wc + bc, gc, betac))
    x = _layernorm(x + _L0_gnn_ref(x, src, dst, edge_weight, L0_gnn_W), axis=-1)
    x = _layernorm(x + _L1_gnn_ref(x, src, dst, L1_gnn_Wp, L1_gnn_bp, L1_gnn_gp, L1_gnn_betap, L1_gnn_Wk, L1_gnn_bk, L1_gnn_gk, L1_gnn_betak, L1_gnn_We, L1_gnn_be, L1_gnn_Wn, L1_gnn_bn, L1_gnn_W_ih, L1_gnn_W_hh, L1_gnn_b_ih, L1_gnn_b_hh, L1_gnn_g_ln, L1_gnn_beta_ln, L1_gnn_Wc, L1_gnn_bc, L1_gnn_gc, L1_gnn_betac), axis=-1)
    return x

_drawn_inputs = setup_inputs


def setup_inputs(seed=0):
    import zlib

    import numpy as np

    out = dict(_drawn_inputs(seed))
    spreads = {'L1_gnn_bp': (0.0, 0.1),
     'L1_gnn_gp': (1.0, 0.2),
     'L1_gnn_betap': (0.0, 0.1),
     'L1_gnn_bk': (0.0, 0.1),
     'L1_gnn_gk': (1.0, 0.2),
     'L1_gnn_betak': (0.0, 0.1),
     'L1_gnn_bn': (0.0, 2.0),
     'L1_gnn_b_ih': (0.0, 2.0),
     'L1_gnn_b_hh': (0.0, 2.0),
     'L1_gnn_g_ln': (1.0, 0.6),
     'L1_gnn_beta_ln': (0.0, 2.0),
     'L1_gnn_bc': (0.0, 0.8),
     'L1_gnn_gc': (1.0, 0.2),
     'L1_gnn_betac': (0.0, 0.1)}
    factors = {'L1_gnn_We': 8.0, 'L1_gnn_Wn': 8.0, 'L1_gnn_W_ih': 8.0, 'L1_gnn_W_hh': 14.853}
    for name, (base, spread) in spreads.items():
        noise = np.random.default_rng([zlib.crc32(name.encode()), seed]).standard_normal(out[name].shape)
        drawn = base * np.exp(spread * noise) if base else spread * noise
        out[name] = jnp.asarray(drawn.astype(out[name].dtype))
    for name, factor in factors.items():
        out[name] = (out[name] * factor).astype(out[name].dtype)
    return out
```

```python
from contextlib import ExitStack

import concourse.bass as bass
from concourse import mybir

P = 128
D = 256
K = 20
G = 4
GE = G * P
EPS = 1e-5
FAR = 1 << 24

ROW = D + 1 + K + 1
MSG = D + 1
KC = 101
HC = D + 1

ALU = mybir.AluOpType
ACT = mybir.ActivationFunctionType
AX_X = mybir.AxisListType.X
F32 = mybir.dt.float32
I32 = mybir.dt.int32
U32 = mybir.dt.uint32
U8 = mybir.dt.uint8
ENG = mybir.EngineType


class Chain:

    def __init__(self, eng, sem):
        self.eng, self.sem, self.done, self.taken = eng, sem, 0, 0

    def __call__(self, ins):
        ins.then_inc(self.sem, 1)
        self.done = self.done + 1
        self.taken += 1
        self.eng.wait_ge(self.sem, self.done)

    def loop(self, start, i, per):
        self.done, self.taken = start + i * per, 0

    def loop_ended(self, start, n, per):
        assert self.taken == per, (self.taken, per)
        self.done = start + n * per


def at(a, i, n=1, step=1):
    if isinstance(i, int):
        return a[:, i * step:i * step + n]
    return a[:, bass.ds(i * step, n)]


def is_zero(i):
    return isinstance(i, int) and i == 0


def rows(a, i, n=P):
    return a[i * P:i * P + n, :] if isinstance(i, int) else a[bass.ds(i * P, n), :]


def gnn_program(nc, io, V, E, EP):
    NT = -(-V // P)
    VL = V - (NT - 1) * P
    NB = NT + NT % 2
    ET = E // EP
    NG = -(-((E + (GE - 1) * NT) // GE) // 4) * 4
    NX = NG + 4
    GP = NX // 4
    SC = 16
    SL = ET // (2 * SC)
    NA = NT * MSG
    MASKW = -(-NB * ET // 4)
    assert E == EP * ET and ET == SL * 2 * SC and GP <= P and EP <= P and NB <= P

    with ExitStack() as ctx:
        def sb(name, shape, dt=F32):
            return ctx.enter_context(nc.sbuf_tensor(name, shape, dt))

        def sem(name):
            return ctx.enter_context(nc.semaphore(name))

        rec_dram = nc.dram_tensor("rec_dram", [NX * GE, 4], F32).ap()
        msg_dram = nc.dram_tensor("msg_dram", [NX * GE, MSG], F32).ap()
        tab_dram = nc.dram_tensor("tab_dram", [NT * P, ROW], F32).ap()
        x1_dram = nc.dram_tensor("x1_dram", [NT * P, D], F32).ap()
        map_dram = nc.dram_tensor("map_dram", [2, NX], I32).ap()

        ps = ctx.enter_context(nc.psum_tensor("ps", [P, 8, 512], F32))

        arena_n = sb("arena_n", [P, max(2 * NA, MASKW + P + 4 * NB)])
        arena_r = sb("arena_r", [P, max(6 * ET, NX * 16 + 4 * GE + 2 * G * (K + 1), 7200)])
        arena_e = sb("arena_e", [P, max(6 * ET, 8200 + NT * (K + 1))])

        def cutter(arena):
            used = [0]

            def cut(*shape):
                n = 1
                for s in shape:
                    n *= s
                v = arena[:, used[0]:used[0] + n]
                used[0] += n
                if len(shape) == 2:
                    v = v.rearrange("p (a b) -> p a b", a=shape[0])
                if len(shape) == 3:
                    v = v.rearrange("p (a b c) -> p a b c", a=shape[0], b=shape[1])
                return v
            return cut

        x_all, agg_all = arena_n[:, 0:NA], arena_n[:, NA:2 * NA]
        mask8 = arena_n[0:EP, 0:MASKW].bitcast(U8)
        before = arena_n[:, MASKW:MASKW + P]
        cmp = arena_n[:, MASKW + P:MASKW + P + 4 * NB].rearrange("p (a b) -> p a b", a=4)
        msg_pad = agg_all[:, 0:G * MSG]
        c = cutter(arena_r)
        bk_i, bk_f = c(ET)[0:EP].bitcast(I32), c(ET)[0:EP]
        scan, prod = [c(ET)[0:EP] for _ in range(2)], [c(ET)[0:EP] for _ in range(2)]
        c = cutter(arena_r)
        rec_all, oh_t, ohl, wex = c(NX * 16), c(2, GE), c(GE), c(GE)
        dsb = c(2, G * (K + 1)).rearrange("p q (j k) -> p q j k", j=G)
        c = cutter(arena_r)
        raw_w, wih_t, wc = c(12, D), c(2 * 3 * D), c(4, D)
        whh_t = c(2 * 3 * D)
        c = cutter(arena_e)
        dst_i, src_i = c(ET)[0:EP].bitcast(I32), c(ET)[0:EP].bitcast(I32)
        w_f, dloc = c(ET)[0:EP], c(ET)[0:EP]
        slot = [c(ET)[0:EP].bitcast(I32) for _ in range(2)]
        msgs = cutter(arena_e)(4, G, MSG)
        c = cutter(arena_e)
        feat, kron, kron_t = c(4, G, ROW), c(G, 4 * KC), c(2, 4 * P)
        normed, clipped = c(2, D), c(2, MSG)
        node = c(NT * (K + 1))
        c = cutter(arena_e)
        gln_b, bln_b, gc_b, bc_b, xf, cx, wa, wb, outb = [c(D) for _ in range(9)]
        cat, tr4, cat_t, rz, bih_r, bhh_r, bcr_r = c(2 * D), c(4 * P), c(4 * P), c(2 * D), c(3 * D), c(3 * D), c(D)

        ident = sb("ident", [P, P])
        ones = sb("ones", [P, P])
        iota = sb("iota", [P, P])
        gidx = sb("gidx", [P, 4])
        minus_half = sb("minus_half", [P, 1])
        eps_c = sb("eps_c", [P, 1])
        eps_root = sb("eps_root", [1, 1])
        gate = sb("gate", [P, 4])
        cnt, gsz, gend, base = (sb(n, [P, NB]) for n in ("cnt", "gsz", "gend", "base"))
        gsz_i = sb("gsz_i", [P, 2, NB], I32)
        tmap_f = sb("tmap_f", [P, 4])
        tmap_i = sb("tmap_i", [P, 2, 4], I32)
        tile_of = sb("tile_of", [1, 2, NX], I32)
        stage = sb("stage", [P, 2, SC, 4])
        sidx = sb("sidx", [P, 2, SC], I32)
        recq = sb("recq", [P, 4, 16])
        oh = sb("oh", [P, 4, GE])
        idxq = sb("idxq", [P, 4, G], I32)
        sloc_i = sb("sloc_i", [P, G], I32)
        wk = sb("wk", [P, 4, HC])
        w0_t = sb("w0_t", [P, 2 * D])
        wt = sb("wt", [P, 2, ROW])
        wt_b = sb("wt_b", [1, ROW])
        gk_b, betak_b, nbetak_b = (sb(n, [P, D]) for n in ("gk_b", "betak_b", "nbetak_b"))
        gp_b, betap_b = sb("gp_b", [P, K]), sb("betap_b", [P, K])
        row = sb("row", [P, ROW])
        st = sb("st", [P, 16])
        tr2 = sb("tr2", [P, 2, D])
        junk = sb("junk", [P, 2, HC])
        y_sb, x1_sb = junk[:, 0, 0:D], junk[:, 1, 0:D]
        pad_rec = junk[:, :, :].rearrange("p a b -> p (a b)")[:, 0:GP * 4].rearrange(
            "p (r f) -> p r f", f=4)
        lg = sb("lg", [P, 2, G])
        valid = sb("valid", [P, G])
        mg = sb("mg", [P, 2])
        mnew = sb("mnew", [P, 1])
        mrun = sb("mrun", [P, NT])
        edd = sb("edd", [P, 2, 8])
        ee = sb("ee", [P, 2, 8])
        var = sb("var", [P, G])
        rstd = sb("rstd", [P, G])

        s_in, s_wt, s_w0, s_x = sem("edges_loaded"), sem("weights_loaded"), sem("w0_loaded"), sem("x_loaded")
        pool_steps, dve_steps, act_steps = sem("pool_steps"), sem("dve_steps"), sem("act_steps")
        s_const, s_wzero, s_cen = sem("constants_ready"), sem("weights_cleared"), sem("kron_weights_centered")
        s_counted, s_totals = sem("buckets_counted"), sem("bucket_totals_ready")
        s_prod, s_psum = sem("slot_product_ready"), sem("slot_product_added")
        s_map, s_mapst, s_mapld = sem("tile_map_ready"), sem("tile_map_stored"), sem("tile_map_loaded")
        s_slots, s_xclr = sem("slots_ready"), sem("x_tail_cleared")
        s_stage, s_gate = sem("records_staged"), sem("scatter_gate")
        s_scat = [sem(f"records_scattered{q}") for q in range(2)]
        s_pads, s_fill, s_mfill = sem("pads_ready"), sem("record_pads_stored"), sem("message_pads_stored")
        s_recs, s_mpad = sem("records_loaded"), sem("message_pad_ready")
        s_w0t = sem("w0_turned")
        m_oh, m_oht, m_ohts, m_x, m_msg, m_loc = (sem("m_" + n) for n in (
            "onehot", "onehot_t", "onehot_t_sbuf", "rows", "messages", "slots_and_locals"))
        m_gate = sem("m_scatter_gate")
        m_out = [sem(f"m_scattered{q}") for q in range(4)]
        a_in = [sem(f"a_messages_loaded{q}") for q in range(4)]
        a_oh, a_sum, a_add = sem("a_onehot"), sem("a_summed"), sem("a_added")
        n_agg = sem("n_aggregate")
        n_t, n_ts, n_lin, n_var, n_std, n_x1, n_tab, n_hv, n_row, n_st = (sem("n_" + n) for n in (
            "turned", "turned_sbuf", "linear", "variance", "deviation", "x1", "table", "values", "row", "stored"))
        l_rec, l_oh, l_oht, l_ohts, l_d = (sem("l_" + n) for n in (
            "records", "onehot", "onehot_t", "onehot_t_sbuf", "dst_rows"))
        l_feat = [sem(f"l_rows_gathered{q}") for q in range(4)]
        l_ohl, l_ohlt, l_mg, l_me, l_dd, l_ex, l_wex, l_ctx, l_comb, l_ksum = (sem("l_" + n) for n in (
            "logits", "logits_t", "group_max", "edge_max", "differences", "exponentials",
            "weighted_onehot", "context", "context_added", "kron_added"))
        k_kron, k_t, k_ts, k_h, k_sq, k_rs, k_n, k_seg = (sem("k_" + n) for n in (
            "products", "turned", "turned_sbuf", "linear", "variance", "rstd", "normed", "summed"))
        f_w, f_wp, f_ws, f_x, f_pre, f_t, f_ts, f_gate, f_sig, f_n0, f_tanh = (sem("f_" + n) for n in (
            "weights_loaded", "weights_turned", "weights_turned_sbuf", "x1_loaded", "context", "turned",
            "turned_sbuf", "gates", "sigmoid", "candidate", "tanh"))
        f_var, f_std, f_cat, f_ct, f_cts, f_lin, f_out, f_st = (sem("f_" + n) for n in (
            "variance", "deviation", "features", "features_t", "features_t_sbuf", "linear", "result", "stored"))

        def nth(i, head=0):
            return i + 1 + head

        HEAD = 4

        def tiles_of(engine, order, g, n):
            _, v = nc.values_load_multi_w_load_instructions(
                tile_of[0:1, order, bass.ds(g, n)], engines=[engine], min_val=0, max_val=NT - 1,
                skip_runtime_bounds_check_because="the map is clamped to the last tile")
            return v

        def rec(u):
            return recq[:, u, :].rearrange("p (j f) -> p j f", f=4)

        def over_nodes(a):
            return a.unsqueeze(2).broadcast_to([P, G, P])

        iota_g = iota[:, :].unsqueeze(1).broadcast_to([P, G, P])

        def grouped(a):
            return a.rearrange("p (j n) -> p j n", j=G)

        def node_of(t, n=K + 1):
            return at(node, t, n, K + 1)

        block = ctx.enter_context(nc.Block())

        @block.sync
        def _(sp):
            sp.dma_start(dst_i, io["dst"].rearrange("(p t) -> p t", p=EP)).then_inc(s_in, 16)
            sp.dma_start(src_i, io["src"].rearrange("(p t) -> p t", p=EP)).then_inc(s_in, 16)
            sp.dma_start(w_f, io["edge_weight"].rearrange("(p t) -> p t", p=EP)).then_inc(s_in, 16)
            sp.wait_ge(s_pads, 1)
            with sp.Fori(0, 16) as i:
                sp.dma_start(rec_dram[bass.ds(i * (P * GP), P * GP), :].rearrange("(p r) f -> p (r f)", p=P),
                             pad_rec.rearrange("p r f -> p (r f)")).then_inc(s_fill, 16)
            for k in range(2):
                sp.wait_ge(s_map, k + 1)
                sp.dma_start(map_dram[k].rearrange("(c p) -> p c", c=4), tmap_i[0:GP, k, :],
                             allow_slow_non_contiguous=True).then_inc(s_mapst, 16)
                sp.wait_ge(s_mapst, 16 * (k + 1))
                sp.dma_start(tile_of[0:1, k, :], map_dram[k:k + 1, :]).then_inc(s_mapld, 16)
            sp.wait_ge(s_slots, 2)
            xv = x_all.rearrange("p (t c) -> p t c", c=MSG)
            sp.dma_start(xv[:, 0:NT - 1, 0:D],
                         io["x"][0:(NT - 1) * P, :].rearrange("(t p) d -> p t d", p=P)).then_inc(s_x, 16)
            sp.wait_ge(s_xclr, 1)
            sp.dma_start(xv[0:VL, NT - 1, 0:D], io["x"][(NT - 1) * P:V, :]).then_inc(s_x, 16)
            sp.wait_ge(s_mpad, 2)
            with sp.Fori(0, NX) as i:
                sp.dma_start(msg_dram[bass.ds(i * GE, GE), :].rearrange("(p j) c -> p (j c)", p=P),
                             msg_pad).then_inc(s_mfill, 16)
            for q in range(2):
                sp.wait_ge(s_scat[q], 16 * SC * SL)
            sp.dma_start(rec_all.rearrange("p (g f) -> p g f", f=4 * G),
                         rec_dram.rearrange("(g p j) f -> p g (j f)", p=P, j=G)).then_inc(s_recs, 16)
            for u in range(4):
                sp.wait_ge(m_out[u], 16 * G * (NG // 4))
            def load_messages(g, u):
                sp.wait_ge(a_sum, nth(g - 4, HEAD))
                lo = g * GE
                src = msg_dram[lo:lo + GE, :] if isinstance(lo, int) else msg_dram[bass.ds(lo, GE), :]
                sp.dma_start(msgs[:, u].rearrange("p j c -> p (j c)"),
                             src.rearrange("(p j) c -> p (j c)", p=P)).then_inc(a_in[u], 16)

            with sp.Fori(0, NG // 4) as it:
                for u in range(4):
                    load_messages(it * 4 + u, u)
            load_messages(NG, 0)
            with sp.Fori(0, NT) as t:
                sp.wait_ge(n_x1, t + 1)
                sp.dma_start(rows(x1_dram, t), x1_sb[:, :]).then_inc(n_st, 16)
                sp.wait_ge(n_row, nth(t, HEAD))
                sp.wait_ge(n_hv, nth(t, HEAD))
                sp.dma_start(rows(tab_dram, t), row[:, :]).then_inc(n_st, 16)
            sp.wait_ge(l_ksum, nth(NG - 1, HEAD))
            sp.wait_ge(k_kron, nth(4 * NG + 1))
            sp.wait_ge(k_ts, nth(4 * NG, HEAD))
            sp.wait_ge(k_seg, nth(4 * NG - 1, HEAD))
            for u in range(4):
                sp.wait_ge(l_feat[u], 16 * G * (NG // 4 + (u < 3)))
            sp.dma_start(raw_w[:, 0:6, :], io["L1_gnn_W_ih"].rearrange("(a p) d -> p a d", p=P)).then_inc(f_w, 16)
            sp.dma_start(raw_w[:, 6:12, :], io["L1_gnn_W_hh"].rearrange("(a p) d -> p a d", p=P)).then_inc(f_w, 16)
            sp.dma_start(wc, io["L1_gnn_Wc"].rearrange("(a p) d -> p a d", p=P)).then_inc(f_w, 16)
            for dst, name in ((gln_b, "g_ln"), (bln_b, "beta_ln"), (gc_b, "gc"), (bc_b, "betac")):
                sp.dma_start(dst, io["L1_gnn_" + name].partition_broadcast(P)).then_inc(f_w, 16)
            for dst, name in ((bih_r, "b_ih"), (bhh_r, "b_hh"), (bcr_r, "bc")):
                sp.dma_start(dst[0:1, :], io["L1_gnn_" + name].unsqueeze(0)).then_inc(f_w, 16)

            def results(t, n):
                sp.wait_ge(f_out, nth(t - 1, HEAD))
                sp.dma_start(xf, rows(x1_dram, t)).then_inc(f_x, 16)
                sp.wait_ge(f_out, nth(t, HEAD))
                sp.dma_start(rows(io["out"], t, n), outb[0:n, :]).then_inc(f_st, 16)

            with sp.Fori(0, NT - 1) as t:
                results(t, P)
            results(NT - 1, VL)
            sp.wait_ge(f_st, 16 * NT)

        @block.gpsimd
        def _(pool):
            step = Chain(pool, pool_steps)
            step(nc.gpsimd.memset(ident[:, :], 0.0))
            step(nc.gpsimd.affine_select(out=ident[:, :], in_=ident[:, :], compare_op=ALU.not_equal, fill=1.0,
                                         base=0, pattern=[[-1, P]], channel_multiplier=1))
            step(nc.gpsimd.memset(before, 1.0))
            step(nc.gpsimd.affine_select(out=before, in_=before, compare_op=ALU.is_gt, fill=0.0,
                                         base=0, pattern=[[1, P]], channel_multiplier=-1))
            step(nc.gpsimd.iota(iota[:, :], [[1, P]], base=0, channel_multiplier=0,
                                allow_small_or_imprecise_dtypes=True))
            step(nc.gpsimd.iota(gidx[0:GP, :], [[GP, 4]], base=0, channel_multiplier=1,
                                allow_small_or_imprecise_dtypes=True))
            step(nc.gpsimd.memset(minus_half[:, :], -0.5))
            step(nc.gpsimd.memset(eps_c[:, :], EPS))
            step(nc.gpsimd.memset(eps_root[:, :], 16.0 * EPS ** 0.5))
            step(nc.gpsimd.memset(ones[:, :], 1.0))
            nc.gpsimd.memset(gate[:, :], 0.0).then_inc(s_const, 1)
            pool.sem_inc(s_gate, HEAD)
            pool.sem_inc(m_gate, HEAD)
            step(nc.gpsimd.memset(pad_rec[:, :, 0:1], 0.0))
            step(nc.gpsimd.memset(pad_rec[:, :, 1:2], -1.0))
            step(nc.gpsimd.memset(pad_rec[:, :, 2:3], 0.0))
            nc.gpsimd.memset(pad_rec[:, :, 3:4], float(FAR)).then_inc(s_pads, 1)
            pool.wait_ge(s_fill, 16 * 16)
            with pool.Fori(0, SL) as it:
                for q in range(2):
                    pool.wait_ge(s_stage, nth(it * 2 + q))
                    nc.gpsimd.tensor_tensor(gate[:, q:q + 1], ones[:, 0:1], ones[:, 1:2], ALU.mult).then_inc(s_gate, 1)
                    for i in range(SC):
                        nc.gpsimd.indirect_dma_start(
                            out=rec_dram, in_=stage[0:EP, q, i, :], in_offset=None,
                            out_offset=bass.IndirectOffsetOnAxis(ap=sidx[0:EP, q, i:i + 1].bitcast(U32), axis=0),
                        ).then_inc(s_scat[q], 16)
            pool.wait_ge(s_mfill, 16 * NX)
            pool.wait_ge(s_gate, nth(2 * SL - 1, HEAD))
            with pool.Fori(0, NG // 4) as it:
                for u in range(4):
                    pool.wait_ge(m_loc, nth(it * 4 + u))
                    pool.wait_ge(m_msg, nth((it * 4 + u) * 4 + 3, HEAD))
                    nc.gpsimd.tensor_tensor(gate[:, u:u + 1], ones[:, 0:1], ones[:, 1:2], ALU.mult).then_inc(m_gate, 1)
                    for j in range(G):
                        nc.gpsimd.indirect_dma_start(
                            out=msg_dram, in_=msgs[:, u, j, :], in_offset=None,
                            out_offset=bass.IndirectOffsetOnAxis(ap=idxq[:, u, j:j + 1].bitcast(U32), axis=0),
                            bounds_check=NG * GE - 1, oob_is_err=False,
                        ).then_inc(m_out[u], 16)

            def gather(u, j):
                nc.gpsimd.indirect_dma_start(
                    out=feat[:, u, j, :], out_offset=None, in_=tab_dram,
                    in_offset=bass.IndirectOffsetOnAxis(ap=idxq[:, u, j:j + 1].bitcast(U32), axis=0),
                ).then_inc(l_feat[u], 16)

            pool.wait_ge(n_st, 32 * NT)
            pool.wait_ge(l_rec, 3)
            for u in range(3):
                for j in range(G):
                    gather(u, j)
            with pool.Fori(0, NG // 4) as it:
                for u in range(4):
                    g = it * 4 + u
                    pool.wait_ge(l_rec, nth(g + 3))
                    for j in range(G):
                        pool.wait_ge(k_sq, nth(g * 4 + j, HEAD))
                        nc.gpsimd.tensor_tensor(rstd[:, j:j + 1], var[:, j:j + 1], minus_half[:, :],
                                                ALU.pow).then_inc(k_rs, 1)
                        gather((u + 3) % 4, j)

        @block.scalar
        def _(act):
            step = Chain(act, act_steps)
            act.wait_ge(s_wzero, 1)
            L1 = "L1_gnn_"
            for c in range(3):
                act.dma_start(wk[0:KC, c, 0:D], io[L1 + "Wk"][c * KC:(c + 1) * KC, :]).then_inc(s_wt, 16)
            last = K * K - 3 * KC
            act.dma_start(wk[0:last, 3, 0:D], io[L1 + "Wk"][3 * KC:K * K, :]).then_inc(s_wt, 16)
            act.dma_start(wk[last:last + 1, 3, 0:D], io[L1 + "bk"].unsqueeze(0)).then_inc(s_wt, 16)
            act.wait_ge(s_const, 1)
            act.dma_start(wk[last:last + 1, 3, D:D + 1], eps_root[:, :]).then_inc(s_wt, 16)
            with nc.allow_non_contiguous_dma("columns of weights"):
                act.dma_start(wt[:, :, 0:D], io[L1 + "Wn"].rearrange("(c p) d -> p c d", p=P)).then_inc(s_wt, 16)
                act.dma_start(wt[:, :, D:D + 1], io[L1 + "We"][0:D, :].rearrange("(c p) d -> p c d", p=P)).then_inc(s_wt, 16)
                act.dma_start(wt[:, :, D + 1:D + 1 + K], io[L1 + "Wp"].rearrange("(c p) d -> p c d", p=P)).then_inc(s_wt, 16)
                act.dma_start(wt[:, :, ROW - 1:ROW], io[L1 + "We"][D:2 * D, :].rearrange("(c p) d -> p c d", p=P)).then_inc(s_wt, 16)
            act.dma_start(wt_b[:, 0:D], io[L1 + "bn"].unsqueeze(0)).then_inc(s_wt, 16)
            act.dma_start(wt_b[:, D:D + 1], io[L1 + "be"].unsqueeze(0)).then_inc(s_wt, 16)
            act.dma_start(wt_b[:, D + 1:D + 1 + K], io[L1 + "bp"].unsqueeze(0)).then_inc(s_wt, 16)
            for dst, name in ((gk_b, "gk"), (betak_b, "betak"), (gp_b, "gp"), (betap_b, "betap")):
                act.dma_start(dst[:, :], io[L1 + name].partition_broadcast(P)).then_inc(s_wt, 16)
            act.dma_start(tr2[:, :, :], io["L0_gnn_W"].rearrange("(c p) d -> p c d", p=P)).then_inc(s_w0, 16)
            act.wait_ge(s_w0t, 1)
            step(nc.scalar.activation(w0_t[:, :], ps[:, 7, :], ACT.Copy))

            act.sem_inc(m_msg, HEAD)

            def weigh(it):
                for u in range(4):
                    g, q = it * 4 + u, u % 2
                    act.wait_ge(m_oht, nth(g, HEAD))
                    nc.scalar.activation(oh_t[:, q, :], ps[:, q, :], ACT.Copy).then_inc(m_ohts, 1)
                    if not is_zero(it):
                        act.wait_ge(m_out[u], 16 * G * it)
                    for j in range(G):
                        act.wait_ge(m_x, nth(g * 4 + j))
                        nc.scalar.activation(msgs[:, u, j, 0:D], ps[:, 2 + j, 0:D], ACT.Copy,
                                             scale=recq[:, u, 4 * j + 2:4 * j + 3]).then_inc(m_msg, 1)

            weigh(0)
            with act.Fori(1, NG // 4) as it:
                weigh(it)

            def node_functions(t):
                for h in range(2):
                    act.wait_ge(n_t, nth(t * 2 + h))
                    nc.scalar.activation(tr2[:, h, :], ps[:, h, 0:D], ACT.Copy).then_inc(n_ts, 1)
                    if h == 0:
                        act.wait_ge(n_var, nth(t * 2))
                        nc.scalar.activation(st[:, 8:9], st[:, 7:8], ACT.Sqrt, bias=eps_c[:, :]).then_inc(n_std, 1)
                act.wait_ge(n_tab, nth(t))
                if not is_zero(t):
                    act.wait_ge(n_st, 32 * t)
                nc.scalar.activation(row[:, :], ps[:, 3, 0:ROW], ACT.Copy).then_inc(n_hv, 1)
                act.wait_ge(n_var, nth(t * 2 + 1))
                nc.scalar.activation(st[:, 8:9], st[:, 7:8], ACT.Sqrt, bias=eps_c[:, :]).then_inc(n_std, 1)

            act.sem_inc(n_hv, HEAD)
            node_functions(0)
            with act.Fori(1, NT) as t:
                node_functions(t)

            act.sem_inc(k_ts, HEAD)
            act.sem_inc(k_sq, HEAD)

            def evacuate(tau, b):
                act.wait_ge(k_t, nth(tau, HEAD))
                act.wait_ge(k_h, nth(tau - 2, HEAD))
                nc.scalar.activation(kron_t[0:KC, b, :], ps[0:KC, b, :], ACT.Copy).then_inc(k_ts, 1)

            def square(tau, j):
                act.wait_ge(k_h, nth(tau, HEAD))
                act.wait_ge(k_sq, nth(tau - 2, HEAD))
                nc.scalar.activation(junk[:, j % 2, :], ps[:, 2 + j % 2, 0:HC], ACT.Square, scale=1.0 / 16,
                                     accum_out=var[:, j:j + 1]).then_inc(k_sq, 1)

            def evacuate_onehot(g, q):
                act.wait_ge(l_oht, nth(g))
                nc.scalar.activation(oh_t[:, q, :], ps[:, 6, :], ACT.Copy).then_inc(l_ohts, 1)

            def exponentials(g, q):
                act.wait_ge(l_dd, nth(g, HEAD))
                nc.scalar.activation(ee[:, q, 0:6], edd[:, q, 0:6], ACT.Exp).then_inc(l_ex, 1)

            evacuate_onehot(0, 0)
            exponentials(0, 0)
            evacuate(0, 0)
            with act.Fori(0, NG // 4) as it:
                for u in range(4):
                    g, q = it * 4 + u, u % 2
                    for j in range(G):
                        if j == 1:
                            evacuate_onehot(g + 1, 1 - q)
                        evacuate(g * 4 + j + 1, (j + 1) % 2)
                        square(g * 4 + j, j)
                    exponentials(g + 1, 1 - q)

            for b in range(6):
                act.wait_ge(f_wp, b + 1)
                dst = (wih_t if b < 3 else whh_t)[:, (b % 3) * 512:(b % 3 + 1) * 512]
                nc.scalar.activation(dst, ps[:, b, :], ACT.Copy).then_inc(f_ws, 1)

            def functions(t):
                act.wait_ge(f_t, nth(t))
                nc.scalar.activation(tr4, ps[:, 0, :], ACT.Copy).then_inc(f_ts, 1)
                act.wait_ge(f_gate, nth(t))
                nc.scalar.activation(rz, ps[:, 1, :], ACT.Sigmoid).then_inc(f_sig, 1)
                act.wait_ge(f_n0, nth(t))
                nc.scalar.activation(wb, wa, ACT.Tanh).then_inc(f_tanh, 1)
                for i in range(3):
                    act.wait_ge(f_var, nth(t * 3 + i))
                    nc.scalar.activation(st[:, 8:9], st[:, 7:8], ACT.Sqrt, bias=eps_c[:, :]).then_inc(f_std, 1)
                    if i == 0:
                        act.wait_ge(f_ct, nth(t))
                        nc.scalar.activation(cat_t, ps[:, 3, :], ACT.Copy).then_inc(f_cts, 1)

            with act.Fori(0, NT - 1) as t:
                functions(t)
            functions(NT - 1)

        @block.vector
        def _(dve):
            step = Chain(dve, dve_steps)
            def move(out, src):
                return nc.vector.tensor_scalar(out, src, 1.0, None, ALU.mult)

            tt, ts, stt = nc.vector.tensor_tensor, nc.vector.tensor_scalar, nc.vector.scalar_tensor_tensor
            step(nc.vector.memset(wk[:, :, :], 0.0))
            nc.vector.memset(wt_b[:, ROW - 1:ROW], 0.0).then_inc(s_wzero, 1)
            dve.wait_ge(s_in, 48)
            step(ts(bk_i, dst_i, P - 1, None, ALU.bitwise_and))
            step(nc.vector.tensor_copy(dloc, bk_i))
            dve.wait_ge(s_const, 1)
            dve.wait_ge(pool_steps, 10)
            one_row = ones[0:EP, 0:1].broadcast_to([EP, ET])
            for k, ids in enumerate((dst_i, src_i)):
                step(ts(bk_i, ids, 7, None, ALU.arith_shift_right))
                step(nc.vector.tensor_copy(bk_f, bk_i))
                with dve.Fori(0, NB) as b:
                    ts(at(mask8, b, ET, ET), bk_f, at(iota[0:EP, :], b), 0.0, ALU.is_equal, ALU.add,
                       accum_out=at(cnt[0:EP, :], b)).then_inc(s_counted, 1)
                dve.wait_ge(s_totals, k + 1)
                step(ts(gsz_i[:, 0, :], ps[:, 4, 0:NB], float(GE - 1), None, ALU.add))
                step(ts(gsz_i[:, 1, :], gsz_i[:, 0, :], GE.bit_length() - 1, None, ALU.arith_shift_right))
                step(nc.vector.tensor_copy(gsz[:, :], gsz_i[:, 1, :]))
                step(nc.vector.tensor_tensor_scan(gend[:, :], ones[:, 0:NB], gsz[:, :], 0.0, ALU.mult, ALU.add))
                step(tt(base[:, :], gend[:, :], gsz[:, :], ALU.subtract))
                step(stt(out=base[0:EP, :], in0=base[0:EP, :], scalar=float(GE), in1=ps[0:EP, 5, 0:NB],
                         op0=ALU.mult, op1=ALU.add))
                step(ts(base[0:EP, :], base[0:EP, :], -1.0, None, ALU.add))
                step(tt(cmp[0:GP], gend[0:GP, :].unsqueeze(1).broadcast_to([GP, 4, NB]),
                        gidx[0:GP, :].unsqueeze(2).broadcast_to([GP, 4, NB]), ALU.is_le))
                step(nc.vector.tensor_reduce(tmap_f[0:GP, :], cmp[0:GP], AX_X, ALU.add))
                ts(tmap_i[0:GP, k, :], tmap_f[0:GP, :], float(NT - 1), None, ALU.min).then_inc(s_map, 1)
                held = step.done
                with dve.Fori(0, NB // 2) as it:
                    step.loop(held, it, 2)
                    for q in range(2):
                        m = at(mask8, it * 2 + q, ET, ET)
                        step(nc.vector.tensor_tensor_scan(scan[q], one_row, m, at(base[0:EP, :], it * 2 + q),
                                                          ALU.mult, ALU.add))
                        dve.wait_ge(s_psum, nth(it * 2 + (k * NB + q - 2), HEAD))
                        tt(prod[q], scan[q], m, ALU.mult).then_inc(s_prod, 1)
                step.loop_ended(held, NB // 2, 2)
                dve.wait_ge(s_prod, NB * (k + 1))
                dve.wait_ge(s_psum, nth((k + 1) * NB - 1, HEAD))
                nc.vector.tensor_copy(slot[k], ps[0:EP, 0:4, :].rearrange("p b c -> p (b c)")[:, 0:ET]
                                      ).then_inc(s_slots, 1)
            dve.wait_ge(s_slots, 2)
            nc.vector.memset(x_all[:, (NT - 1) * MSG:NT * MSG], 0.0).then_inc(s_xclr, 1)
            nc.vector.memset(msg_pad, 0.0).then_inc(s_mpad, 1)
            dve.wait_ge(s_mpad, 1)
            nc.vector.memset(msg_pad.rearrange("p (j c) -> p j c", c=MSG)[:, :, D:MSG], -1.0).then_inc(s_mpad, 1)

            held = step.done

            def stage_records(it):
                step.loop(held, it, 8)
                for q in range(2):
                    i = it * 2 + q
                    if not is_zero(it):
                        dve.wait_ge(s_scat[q], 16 * SC * it)
                    dve.wait_ge(s_gate, nth(i - 2, HEAD))
                    step(move(stage[0:EP, q, :, 0], at(src_i, i, SC, SC)))
                    step(move(stage[0:EP, q, :, 1], at(dloc, i, SC, SC)))
                    step(move(stage[0:EP, q, :, 2], at(w_f, i, SC, SC)))
                    step(move(stage[0:EP, q, :, 3], at(slot[1], i, SC, SC)))
                    move(sidx[0:EP, q, :], at(slot[0], i, SC, SC)).then_inc(s_stage, 1)

            stage_records(0)
            with dve.Fori(1, SL) as it:
                stage_records(it)
            step.loop_ended(held, SL, 8)

            dve.wait_ge(s_wt, 16 * 17)
            for c in range(4):
                step(nc.vector.tensor_reduce(var[:, c:c + 1], wk[:, c, 0:D], AX_X, ALU.add))
            step(ts(var[:, :], var[:, :], 1.0 / D, None, ALU.mult))
            for c in range(4):
                step(ts(wk[:, c, 0:D], wk[:, c, 0:D], var[:, c:c + 1], None, ALU.subtract))
            step(ts(nbetak_b[:, :], betak_b[:, :], -1.0, None, ALU.mult))

            def onehot(out, local):
                return tt(grouped(out), iota_g, over_nodes(local), ALU.is_equal)

            dve.wait_ge(s_recs, 16)
            held = step.done

            def prepare_messages(it):
                step.loop(held, it, 16)
                for u in range(4):
                    g, q = it * 4 + u, u % 2
                    if not is_zero(it):
                        dve.wait_ge(m_out[u], 16 * G * it)
                    dve.wait_ge(m_gate, nth(g - 4, HEAD))
                    dve.wait_ge(m_oht, nth(g - 2, HEAD))
                    step(move(recq[:, u, :], at(rec_all, g, 16, 16)))
                    onehot(oh[:, q, :], rec(u)[:, :, 1]).then_inc(m_oh, 1)
                    step(nc.vector.tensor_copy(idxq[:, u, :], rec(u)[:, :, 3]))
                    step(nc.vector.tensor_copy(sloc_i[:, :], rec(u)[:, :, 0]))
                    step(ts(sloc_i[:, :], sloc_i[:, :], P - 1, None, ALU.bitwise_and))
                    nc.vector.tensor_copy(msgs[:, u, :, D], sloc_i[:, :]).then_inc(m_loc, 1)

            prepare_messages(0)
            with dve.Fori(1, NG // 4) as it:
                prepare_messages(it)
            step.loop_ended(held, NG // 4, 16)

            dve.wait_ge(s_mfill, 16 * NX)
            step(nc.vector.memset(agg_all, 0.0))
            dve.wait_ge(a_in[0], 16)
            onehot(oh[:, 0, :], msgs[:, 0, :, D]).then_inc(a_oh, 1)
            dve.wait_ge(s_mapld, 32)
            dve.sem_inc(a_add, HEAD)
            with dve.Fori(0, NG // 4) as it:
                nt = tiles_of(ENG.DVE, 1, it * 4, 4)
                for u in range(4):
                    g, q = it * 4 + u, u % 2
                    dve.wait_ge(a_in[(u + 1) % 4], 16 * (it + 1 + (u == 3)))
                    dve.wait_ge(a_sum, nth(g - 1, HEAD))
                    onehot(oh[:, 1 - q, :], msgs[:, (u + 1) % 4, :, D]).then_inc(a_oh, 1)
                    dve.wait_ge(a_sum, nth(g, HEAD))
                    dve.wait_ge(a_add, nth(g - 1, HEAD))
                    tt(at(agg_all, nt[u], D, MSG), at(agg_all, nt[u], D, MSG), ps[:, q, 0:D], ALU.add).then_inc(a_add, 1)

            def norm_stats(src, out):
                nc.vector.bn_stats(st[:, 0:6], src)
                dve.drain()
                nc.vector.bn_aggr(st[:, 6:8], st[:, 0:6]).then_inc(out, 1)

            def normalize(out, src, deviation, i):
                dve.wait_ge(deviation, i)
                step(nc.vector.reciprocal(st[:, 9:10], st[:, 8:9]))
                return ts(out, src, st[:, 6:7], st[:, 9:10], ALU.subtract, ALU.mult)

            dve.wait_ge(a_add, nth(NG - 1, HEAD))
            dve.wait_ge(s_x, 32)
            held = step.done

            def node_stage(t):
                step.loop(held, t, 9)
                move(y_sb[:, :], at(agg_all, t, D, MSG)).then_inc(n_agg, 1)
                dve.wait_ge(n_lin, nth(t))
                step(stt(out=y_sb[:, :], in0=ps[:, 2, 0:D], scalar=0.0, in1=at(x_all, t, D, MSG),
                         op0=ALU.max, op1=ALU.add))
                norm_stats(y_sb[:, :], n_var)
                if not is_zero(t):
                    dve.wait_ge(n_st, 32 * t)
                normalize(x1_sb[:, :], y_sb[:, :], n_std, nth(t * 2)).then_inc(n_x1, 1)
                dve.wait_ge(n_hv, nth(t, HEAD))
                pj = row[:, D + 1:D + 1 + K]
                norm_stats(pj, n_var)
                step(normalize(pj, pj, n_std, nth(t * 2 + 1)))
                step(tt(pj, pj, gp_b[:, :], ALU.mult))
                step(tt(pj, pj, betap_b[:, :], ALU.add))
                step(ts(pj, pj, 0.0, None, ALU.max))
                step(move(node_of(t, K), pj))
                step(move(at(node[:, K:], t, 1, K + 1), row[:, D:D + 1]))
                nc.vector.memset(row[:, D:D + 1], 1.0).then_inc(n_row, 1)

            dve.sem_inc(n_row, HEAD)
            node_stage(0)
            with dve.Fori(1, NT) as t:
                node_stage(t)
            step.loop_ended(held, NT, 9)
            dve.wait_ge(n_row, nth(NT - 1, HEAD))

            step(nc.vector.memset(arena_n[:, 0:2 * NA], 0.0))
            step(nc.vector.memset(mrun[:, :], 0.0))
            step(nc.vector.memset(kron[:, :, K * K:K * K + 1], 1.0))
            step(nc.vector.memset(kron[:, :, K * K + 1:4 * KC], 0.0))
            step(nc.vector.memset(clipped[:, :, D:MSG], 1.0))
            dve.sem_inc(k_n, HEAD)

            def take_records(g, u):
                step(move(recq[:, u, :], at(rec_all, g, 16, 16)))
                nc.vector.tensor_copy(idxq[:, u, :], rec(u)[:, :, 0]).then_inc(l_rec, 1)

            def products(tau, u, q, j):
                dve.wait_ge(k_t, nth(tau - 4, HEAD))
                tt(kron[:, j, 0:K * K].rearrange("p (a b) -> p a b", a=K),
                   feat[:, u, j, D + 1:D + 1 + K].unsqueeze(2).broadcast_to([P, K, K]),
                   dsb[:, q, j, 0:K].unsqueeze(1).broadcast_to([P, K, K]), ALU.mult).then_inc(k_kron, 1)

            def local_onehot(g, u):
                onehot(oh[:, u, :], rec(u)[:, :, 1]).then_inc(l_oh, 1)

            def logits(g, u, q, it):
                dve.wait_ge(l_d, nth(g))
                step(nc.vector.tensor_copy(dsb[:, q].rearrange("p j k -> p (j k)"), ps[:, 7, 0:G * (K + 1)]))
                step(ts(valid[:, :], rec(u)[:, :, 1], 0.0, None, ALU.is_ge))
                dve.wait_ge(l_feat[u], 16 * G * (it + 1))
                step(tt(lg[:, q, :], feat[:, u, :, ROW - 1], dsb[:, q, :, K], ALU.add))
                step(stt(out=lg[:, q, :], in0=lg[:, q, :], scalar=0.0, in1=valid[:, :], op0=ALU.max, op1=ALU.mult))
                tt(grouped(ohl[:, :]), grouped(oh[:, u, :]), over_nodes(lg[:, q, :]), ALU.mult).then_inc(l_ohl, 1)

            def group_max(g, q):
                dve.wait_ge(l_ohlt, nth(g))
                nc.vector.tensor_reduce(mg[:, q:q + 1], ps[:, 6, :], AX_X, ALU.max).then_inc(l_mg, 1)

            def differences(g, q, nt):
                dve.wait_ge(l_mg, nth(g, HEAD))
                mr, m = at(mrun, nt), mg[:, q:q + 1]
                step(tt(mnew[:, :], mr, m, ALU.max))
                step(tt(edd[:, q, 4:5], mr, mnew[:, :], ALU.subtract))
                step(tt(edd[:, q, 5:6], m, mnew[:, :], ALU.subtract))
                step(move(mr, mnew[:, :]))
                dve.wait_ge(l_me, nth(g))
                tt(edd[:, q, 0:4], lg[:, q, :], ps[:, 7, P:P + G], ALU.subtract).then_inc(l_dd, 1)

            def normalized(tau, j):
                dve.wait_ge(k_rs, nth(tau))
                step(stt(out=normed[:, j % 2, :], in0=ps[:, 2 + j % 2, 0:D], scalar=rstd[:, j:j + 1],
                         in1=gk_b[:, :], op0=ALU.mult, op1=ALU.mult))
                dve.wait_ge(k_seg, nth(tau - 2, HEAD))
                tt(clipped[:, j % 2, 0:D], normed[:, j % 2, :], nbetak_b[:, :], ALU.max).then_inc(k_n, 1)

            def add_kron(g, nt):
                dve.wait_ge(k_seg, nth(g * 4 + 3, HEAD))
                ksum = at(x_all, nt, MSG, MSG)
                tt(ksum, ksum, ps[:, 4, 0:MSG], ALU.add).then_inc(l_ksum, 1)

            for s in (l_mg, l_dd, l_ksum, l_comb):
                dve.sem_inc(s, HEAD)
            for u in range(3):
                take_records(u, u)
            dve.wait_ge(l_rec, 3)
            first = tiles_of(ENG.DVE, 0, 0, 1)
            local_onehot(0, 0)
            logits(0, 0, 0, 0)
            group_max(0, 0)
            differences(0, 0, first[0])
            products(0, 0, 0, 0)
            products(1, 0, 0, 1)
            local_onehot(1, 1)
            held = step.done
            PER = 1 + G + 4 + 4 + 1

            def edge_groups(it, nt, before_nt):
                for u in range(4):
                    g, q, u1, q1 = it * 4 + u, u % 2, (u + 1) % 4, 1 - u % 2
                    started = u > 0 or not is_zero(it)
                    products(g * 4 + 2, u, q, 2)
                    if started:
                        normalized(g * 4 - 1, 3)
                    take_records(g + 3, (u + 3) % 4)
                    dve.wait_ge(l_ex, nth(g))
                    tt(grouped(wex[:, :]), grouped(oh[:, u, :]), over_nodes(ee[:, q, 0:4]), ALU.mult).then_inc(l_wex, 1)
                    products(g * 4 + 3, u, q, 3)
                    normalized(g * 4, 0)
                    logits(g + 1, u1, q1, it + 1 if u == 3 else it)
                    products(g * 4 + 4, u1, q1, 0)
                    normalized(g * 4 + 1, 1)
                    if started:
                        add_kron(g - 1, nt[u - 1] if u > 0 else before_nt)
                    group_max(g + 1, q1)
                    dve.wait_ge(l_ctx, nth(g))
                    att = at(agg_all, nt[u], MSG, MSG)
                    step(ts(att, att, ee[:, q, 4:5], None, ALU.mult))
                    stt(out=att, in0=ps[:, 5, 0:MSG], scalar=ee[:, q, 5:6], in1=att,
                        op0=ALU.mult, op1=ALU.add).then_inc(l_comb, 1)
                    products(g * 4 + 5, u1, q1, 1)
                    normalized(g * 4 + 2, 2)
                    local_onehot(g + 2, (u + 2) % 4)
                    differences(g + 1, q1, nt[u + 1])

            step.loop(held, 0, 4 * PER)
            edge_groups(0, tiles_of(ENG.DVE, 0, 0, 5), None)
            held2 = step.done
            assert held2 == held + 4 * PER - 1
            with dve.Fori(1, NG // 4) as it:
                step.loop(held2 - 4 * PER, it, 4 * PER)
                loaded = tiles_of(ENG.DVE, 0, it * 4 - 1, 6)
                edge_groups(it, loaded[1:], loaded[0])
            step.loop_ended(held2 - 4 * PER, NG // 4, 4 * PER)
            normalized(NG * 4 - 1, 3)
            add_kron(NG - 1, tiles_of(ENG.DVE, 0, NG - 1, 1)[0])

            dve.wait_ge(f_w, 16 * 10)
            dve.wait_ge(l_ksum, nth(NG - 1, HEAD))
            dve.wait_ge(l_comb, nth(NG - 1, HEAD))
            held = step.done
            PER2 = 17

            def last_norm(out, src, t, i):
                norm_stats(src, f_var)
                return normalize(out, src, f_std, nth(t * 3 + i))

            def last_stage(t):
                att, ksum = at(agg_all, t, MSG, MSG), at(x_all, t, MSG, MSG)
                step(ts(st[:, 10:11], att[:, D:MSG], 1e-30, None, ALU.max))
                step(nc.vector.reciprocal(st[:, 11:12], st[:, 10:11]))
                step(ts(cx, att[:, 0:D], st[:, 11:12], 0.0, ALU.mult, ALU.max))
                stt(out=cat[:, D:2 * D], in0=betak_b[:, :], scalar=ksum[:, D:MSG], in1=ksum[:, 0:D],
                    op0=ALU.mult, op1=ALU.add).then_inc(f_pre, 1)
                dve.wait_ge(f_sig, nth(t))
                step(tt(wa, rz[:, 0:D], ps[:, 2, D:2 * D], ALU.mult))
                tt(wa, wa, ps[:, 2, 0:D], ALU.add).then_inc(f_n0, 1)
                dve.wait_ge(f_tanh, nth(t))
                step(tt(wa, xf, wb, ALU.subtract))
                step(tt(wa, wa, rz[:, D:2 * D], ALU.mult))
                step(tt(wa, wa, wb, ALU.add))
                step(ts(wa, wa, 0.0, None, ALU.max))
                step(last_norm(wb, wa, t, 0))
                step(tt(wb, wb, gln_b, ALU.mult))
                tt(cat[:, 0:D], wb, bln_b, ALU.add).then_inc(f_cat, 1)
                dve.wait_ge(f_lin, nth(t))
                step(last_norm(wa, ps[:, 4, 0:D], t, 1))
                step(tt(wa, wa, gc_b, ALU.mult))
                step(tt(wa, wa, bc_b, ALU.add))
                step(stt(out=wb, in0=wa, scalar=0.0, in1=xf, op0=ALU.max, op1=ALU.add))
                if not is_zero(t):
                    dve.wait_ge(f_st, 16 * t)
                last_norm(outb, wb, t, 2).then_inc(f_out, 1)

            dve.sem_inc(f_out, HEAD)
            step.loop(held, 0, PER2)
            last_stage(0)
            step.loop_ended(held, 1, PER2)
            with dve.Fori(1, NT - 1) as t:
                step.loop(held, t, PER2)
                last_stage(t)
            step.loop_ended(held, NT - 1, PER2)
            last_stage(NT - 1)

        @block.tensor
        def _(pe):
            mm = nc.tensor.matmul

            def turn(out, src):
                return nc.tensor.transpose(out, src, ident[:, :])

            pe.wait_ge(s_const, 1)
            pe.wait_ge(pool_steps, 10)
            pe.wait_ge(s_w0, 16)
            for ic in range(2):
                for oc in range(2):
                    i = 2 * ic + oc
                    ins = turn(ps[:, 7, i * P:(i + 1) * P], tr2[:, oc, ic * P:(ic + 1) * P])
            ins.then_inc(s_w0t, 1)

            pe.sem_inc(s_psum, HEAD)
            for k in range(2):
                pe.wait_ge(s_counted, NB * (k + 1))
                pe.wait_ge(s_map, k)
                mm(ps[:, 4, 0:NB], ones[0:EP, :], cnt[0:EP, :], start=True, stop=True)
                mm(ps[0:EP, 5, 0:NB], before[0:EP, 0:EP], cnt[0:EP, :], start=True, stop=True).then_inc(s_totals, 1)
                pe.wait_ge(s_slots, k)

                def add_product(b, q, first=False, last=False):
                    pe.wait_ge(s_prod, nth(b))
                    for i in range(-(-ET // 512)):
                        n = min(512, ET - 512 * i)
                        ins = mm(ps[0:EP, i, 0:n], ident[0:EP, 0:EP], prod[q][:, i * 512:i * 512 + n],
                                 start=first, stop=last)
                    ins.then_inc(s_psum, 1)

                add_product(k * NB, 0, first=True)
                add_product(k * NB + 1, 1)
                with pe.Fori(1, NB // 2 - 1) as it:
                    for q in range(2):
                        add_product(it * 2 + (k * NB + q), q)
                add_product((k + 1) * NB - 2, 0)
                add_product((k + 1) * NB - 1, 1, last=True)

            pe.wait_ge(s_mapld, 32)
            pe.wait_ge(s_x, 32)
            pe.sem_inc(m_oht, HEAD)
            with pe.Fori(0, NG // 4) as it:
                nt = tiles_of(ENG.PE, 0, it * 4, 4)
                for u in range(4):
                    g, q = it * 4 + u, u % 2
                    pe.wait_ge(m_oh, nth(g))
                    for j in range(G):
                        ins = turn(ps[:, q, j * P:(j + 1) * P], oh[:, q, j * P:(j + 1) * P])
                    ins.then_inc(m_oht, 1)
                    pe.wait_ge(m_ohts, nth(g))
                    for j in range(G):
                        pe.wait_ge(m_msg, nth((g - 1) * 4 + j, HEAD))
                        mm(ps[:, 2 + j, 0:D], oh_t[:, q, j * P:(j + 1) * P], at(x_all, nt[u], D, MSG),
                           start=True, stop=True).then_inc(m_x, 1)

            pe.sem_inc(a_sum, HEAD)
            with pe.Fori(0, NG // 4) as it:
                for u in range(4):
                    g, q = it * 4 + u, u % 2
                    pe.wait_ge(a_oh, nth(g))
                    pe.wait_ge(a_add, nth(g - 2, HEAD))
                    for j in range(G):
                        ins = mm(ps[:, q, 0:D], oh[:, q, j * P:(j + 1) * P], msgs[:, u, j, 0:D],
                                 start=(j == 0), stop=(j == G - 1))
                    ins.then_inc(a_sum, 1)

            pe.wait_ge(s_wt, 16 * 17)
            pe.wait_ge(s_wzero, 1)
            pe.wait_ge(act_steps, 1)
            with pe.Fori(0, NT) as t:
                pe.wait_ge(n_agg, nth(t))
                for c in range(2):
                    ins = turn(ps[:, 0, c * P:(c + 1) * P], y_sb[:, c * P:(c + 1) * P])
                ins.then_inc(n_t, 1)
                pe.wait_ge(n_ts, nth(t * 2))
                for c in range(2):
                    ins = mm(ps[:, 2, 0:D], tr2[:, 0, c * P:(c + 1) * P], w0_t[:, c * D:(c + 1) * D],
                             start=(c == 0), stop=(c == 1))
                ins.then_inc(n_lin, 1)
                pe.wait_ge(n_x1, nth(t))
                for c in range(2):
                    ins = turn(ps[:, 1, c * P:(c + 1) * P], x1_sb[:, c * P:(c + 1) * P])
                ins.then_inc(n_t, 1)
                pe.wait_ge(n_ts, nth(t * 2 + 1))
                pe.wait_ge(n_hv, nth(t - 1, HEAD))
                mm(ps[:, 3, 0:ROW], ones[0:1, :], wt_b[:, :], start=True, stop=False)
                for c in range(2):
                    ins = mm(ps[:, 3, 0:ROW], tr2[:, 1, c * P:(c + 1) * P], wt[:, c, :],
                             start=False, stop=(c == 1))
                ins.then_inc(n_tab, 1)

            for s in (k_t, k_h, k_seg):
                pe.sem_inc(s, HEAD)

            def turn_products(tau, j):
                pe.wait_ge(k_kron, nth(tau))
                pe.wait_ge(k_ts, nth(tau - 2, HEAD))
                for c in range(4):
                    ins = turn(ps[0:KC, j % 2, c * P:(c + 1) * P], kron[:, j, c * KC:(c + 1) * KC])
                ins.then_inc(k_t, 1)

            def linear(tau, j):
                pe.wait_ge(k_ts, nth(tau, HEAD))
                pe.wait_ge(k_n, nth(tau - 2, HEAD))
                for c in range(4):
                    ins = mm(ps[:, 2 + j % 2, 0:HC], kron_t[0:KC, j % 2, c * P:(c + 1) * P], wk[0:KC, c, :],
                             start=(c == 0), stop=(c == 3))
                ins.then_inc(k_h, 1)

            def sum_kron(g, u, j):
                pe.wait_ge(k_n, nth(g * 4 + j, HEAD))
                if j == 0:
                    pe.wait_ge(l_ksum, nth(g - 1, HEAD))
                mm(ps[:, 4, 0:MSG], oh[:, u, j * P:(j + 1) * P], clipped[:, j % 2, :],
                   start=(j == 0), stop=(j == G - 1)).then_inc(k_seg, 1)

            def turn_onehot(g, u):
                pe.wait_ge(l_oh, nth(g))
                pe.wait_ge(l_mg, nth(g - 1, HEAD))
                for j in range(G):
                    ins = turn(ps[:, 6, j * P:(j + 1) * P], oh[:, u, j * P:(j + 1) * P])
                ins.then_inc(l_oht, 1)

            def dst_rows(g, q, nt):
                pe.wait_ge(l_ohts, nth(g))
                pe.wait_ge(l_dd, nth(g - 1, HEAD))
                for j in range(G):
                    ins = mm(ps[:, 7, j * (K + 1):(j + 1) * (K + 1)], oh_t[:, q, j * P:(j + 1) * P], node_of(nt),
                             start=True, stop=True)
                ins.then_inc(l_d, 1)

            def turn_logits(g):
                pe.wait_ge(l_ohl, nth(g))
                for j in range(G):
                    ins = turn(ps[:, 6, j * P:(j + 1) * P], ohl[:, j * P:(j + 1) * P])
                ins.then_inc(l_ohlt, 1)

            def edge_max(g, q):
                pe.wait_ge(l_mg, nth(g, HEAD))
                for j in range(G):
                    ins = mm(ps[:, 7, P + j:P + j + 1], oh_t[:, q, j * P:(j + 1) * P], mg[:, q:q + 1],
                             start=True, stop=True)
                ins.then_inc(l_me, 1)

            def context(g, u):
                pe.wait_ge(l_wex, nth(g))
                pe.wait_ge(l_comb, nth(g - 1, HEAD))
                for j in range(G):
                    ins = mm(ps[:, 5, 0:MSG], wex[:, j * P:(j + 1) * P], feat[:, u, j, 0:MSG],
                             start=(j == 0), stop=(j == G - 1))
                ins.then_inc(l_ctx, 1)

            first = tiles_of(ENG.PE, 0, 0, 1)
            pe.wait_ge(n_row, nth(NT - 1, HEAD))
            turn_onehot(0, 0)
            dst_rows(0, 0, first[0])
            turn_logits(0)
            edge_max(0, 0)
            turn_products(0, 0)

            def edge_groups(it):
                nt = tiles_of(ENG.PE, 0, it * 4, 5)
                for u in range(4):
                    g, q, q1 = it * 4 + u, u % 2, 1 - u % 2
                    started = u > 0 or not is_zero(it)
                    turn_products(g * 4 + 1, 1)
                    linear(g * 4, 0)
                    turn_onehot(g + 1, (u + 1) % 4)
                    if started:
                        sum_kron(g - 1, (u + 3) % 4, 2)

                    turn_products(g * 4 + 2, 2)
                    context(g, u)
                    dst_rows(g + 1, q1, nt[u + 1])
                    linear(g * 4 + 1, 1)
                    if started:
                        sum_kron(g - 1, (u + 3) % 4, 3)

                    turn_products(g * 4 + 3, 3)
                    turn_logits(g + 1)
                    linear(g * 4 + 2, 2)
                    sum_kron(g, u, 0)

                    turn_products(g * 4 + 4, 0)
                    edge_max(g + 1, q1)
                    linear(g * 4 + 3, 3)
                    sum_kron(g, u, 1)

            edge_groups(0)
            with pe.Fori(1, NG // 4) as it:
                edge_groups(it)
            sum_kron(NG - 1, 3, 2)
            sum_kron(NG - 1, 3, 3)

            pe.wait_ge(f_w, 16 * 10)
            pe.wait_ge(l_comb, nth(NG - 1, HEAD))
            for b in range(6):
                for r in range(4):
                    c, o = divmod((b % 3) * 4 + r, 6)
                    ins = turn(ps[:, b, r * P:(r + 1) * P], raw_w[:, 6 * (b // 3) + o, c * P:(c + 1) * P])
                ins.then_inc(f_wp, 1)
            pe.wait_ge(f_ws, 6)

            def gates(out, lo, n, parts):
                both = ((bih_r, wih_t, 0), (bhh_r, whh_t, 2))
                both = [both[i] for i in parts]
                first = True
                for b, _, _ in both:
                    mm(out, ones[0:1, :], b[0:1, lo:lo + n], start=first, stop=False)
                    first = False
                for i, (_, w, x) in enumerate(both):
                    for c in range(2):
                        ins = mm(out, tr4[:, (x + c) * P:(x + c + 1) * P], w[:, c * 3 * D + lo:c * 3 * D + lo + n],
                                 start=False, stop=(i == len(both) - 1 and c == 1))
                return ins

            def last_products(t):
                pe.wait_ge(f_pre, nth(t))
                pe.wait_ge(f_x, 16 * (t + 1))
                for c in range(2):
                    turn(ps[:, 0, c * P:(c + 1) * P], cx[:, c * P:(c + 1) * P])
                for c in range(2):
                    ins = turn(ps[:, 0, (2 + c) * P:(3 + c) * P], xf[:, c * P:(c + 1) * P])
                ins.then_inc(f_t, 1)
                pe.wait_ge(f_ts, nth(t))
                gates(ps[:, 1, :], 0, 2 * D, (0, 1))
                gates(ps[:, 2, 0:D], 2 * D, D, (0,))
                gates(ps[:, 2, D:2 * D], 2 * D, D, (1,)).then_inc(f_gate, 1)
                pe.wait_ge(f_cat, nth(t))
                for c in range(4):
                    ins = turn(ps[:, 3, c * P:(c + 1) * P], cat[:, c * P:(c + 1) * P])
                ins.then_inc(f_ct, 1)
                pe.wait_ge(f_cts, nth(t))
                mm(ps[:, 4, 0:D], ones[0:1, :], bcr_r[0:1, :], start=True, stop=False)
                for c in range(4):
                    ins = mm(ps[:, 4, 0:D], cat_t[:, c * P:(c + 1) * P], wc[:, c, :], start=False, stop=(c == 3))
                ins.then_inc(f_lin, 1)

            with pe.Fori(0, NT - 1) as t:
                last_products(t)
            last_products(NT - 1)


INPUTS = ["x", "src", "dst", "edge_weight", "L0_gnn_W"] + ["L1_gnn_" + n for n in (
    "Wp", "bp", "gp", "betap", "Wk", "bk", "gk", "betak", "We", "be", "Wn", "bn", "W_ih", "W_hh", "b_ih", "b_hh",
    "g_ln", "beta_ln", "Wc", "bc", "gc", "betac")]


def kernel(**inputs):
    import numpy as _np
    import concourse.bacc as _bacc
    from concourse import mybir as _mybir
    from concourse.bass_utils import run_bass_kernel_spmd as _run

    nc = _bacc.Bacc("TRN2", target_bir_lowering=False, num_devices=1)
    arrays, io = {}, {}
    for name in INPUTS:
        a = _np.ascontiguousarray(inputs[name])
        arrays["in_" + name] = a
        io[name] = nc.dram_tensor("in_" + name, a.shape, _mybir.dt.from_np(a.dtype), kind="ExternalInput").ap()
    V, E = inputs["x"].shape[0], inputs["src"].shape[0]
    io["out"] = nc.dram_tensor("out", (V, D), F32, kind="ExternalOutput").ap()
    gnn_program(nc, io, V, E, 125)
    r = _run(nc, [arrays], core_ids=[0])
    return r.results[0]["out"]
```

```python
from contextlib import ExitStack

import concourse.bass as bass
from concourse import mybir

P = 128
D = 256
K = 20
G = 4
GE = G * P
EPS = 1e-5
FAR = 1 << 24

ROW = D + 1 + K + 1
MSG = D + 1
KC = 101
HC = D + 1

ALU = mybir.AluOpType
ACT = mybir.ActivationFunctionType
AX_X = mybir.AxisListType.X
F32 = mybir.dt.float32
I32 = mybir.dt.int32
U32 = mybir.dt.uint32
U8 = mybir.dt.uint8
ENG = mybir.EngineType


class Chain:

    def __init__(self, eng, sem):
        self.eng, self.sem, self.done, self.taken = eng, sem, 0, 0

    def __call__(self, ins):
        ins.then_inc(self.sem, 1)
        self.done = self.done + 1
        self.taken += 1
        self.eng.wait_ge(self.sem, self.done)

    def loop(self, start, i, per):
        self.done, self.taken = start + i * per, 0

    def loop_ended(self, start, n, per):
        assert self.taken == per, (self.taken, per)
        self.done = start + n * per


def at(a, i, n=1, step=1):
    if isinstance(i, int):
        return a[:, i * step:i * step + n]
    return a[:, bass.ds(i * step, n)]


def is_zero(i):
    return isinstance(i, int) and i == 0


def rows(a, i, n=P):
    return a[i * P:i * P + n, :] if isinstance(i, int) else a[bass.ds(i * P, n), :]


def gnn_program(nc, io, V, E, EP):
    NT = -(-V // P)
    VL = V - (NT - 1) * P
    NB = NT + NT % 2
    ET = E // EP
    NG = -(-((E + (GE - 1) * NT) // GE) // 4) * 4
    NX = NG + 4
    GP = NX // 4
    SC = 16
    SL = ET // SC
    NA = NT * MSG
    MASKW = -(-NB * ET // 4)
    assert E == EP * ET and ET == SL * SC and GP <= P and EP <= P and NB <= P

    with ExitStack() as ctx:
        def sb(name, shape, dt=F32):
            return ctx.enter_context(nc.sbuf_tensor(name, shape, dt))

        def sem(name):
            return ctx.enter_context(nc.semaphore(name))

        rec_dram = nc.dram_tensor("rec_dram", [E + GE, 4], F32).ap()
        msg_dram = nc.dram_tensor("msg_dram", [E + GE, MSG], F32).ap()
        tab_dram = nc.dram_tensor("tab_dram", [NT * P, ROW], F32).ap()
        x1_dram = nc.dram_tensor("x1_dram", [NT * P, D], F32).ap()
        map_dram = nc.dram_tensor("map_dram", [4, NX], I32).ap()
        left_dram = nc.dram_tensor("left_dram", [2, NX], F32).ap()

        ps = ctx.enter_context(nc.psum_tensor("ps", [P, 8, 512], F32))

        arena_n = sb("arena_n", [P, max(2 * NA, MASKW + P + 8 * NB)])
        arena_r = sb("arena_r", [P, max(6 * ET, NX * 16 + 4 * GE + 2 * G * (K + 1), 7200)])
        arena_e = sb("arena_e", [P, max(6 * ET, 8200 + NT * (K + 1))])

        def cutter(arena):
            used = [0]

            def cut(*shape):
                n = 1
                for s in shape:
                    n *= s
                v = arena[:, used[0]:used[0] + n]
                used[0] += n
                if len(shape) == 2:
                    v = v.rearrange("p (a b) -> p a b", a=shape[0])
                if len(shape) == 3:
                    v = v.rearrange("p (a b c) -> p a b c", a=shape[0], b=shape[1])
                return v
            return cut

        x_all, agg_all = arena_n[:, 0:NA], arena_n[:, NA:2 * NA]
        mask8 = arena_n[0:EP, 0:MASKW].bitcast(U8)
        before = arena_n[:, MASKW:MASKW + P]
        cmp = arena_n[:, MASKW + P:MASKW + P + 4 * NB].rearrange("p (a b) -> p a b", a=4)
        weighed = arena_n[:, MASKW + P + 4 * NB:MASKW + P + 8 * NB].rearrange("p (a b) -> p a b", a=4)
        tail = agg_all[:, 0:G * MSG]
        c = cutter(arena_r)
        bk_i, bk_f = c(ET)[0:EP].bitcast(I32), c(ET)[0:EP]
        scan, prod = [c(ET)[0:EP] for _ in range(2)], [c(ET)[0:EP] for _ in range(2)]
        recs = arena_r[0:EP, 0:4 * ET]
        place, slot_f = prod
        c = cutter(arena_r)
        rec_all, oh_t, ohl, wex = c(NX * 16), c(2, GE), c(GE), c(GE)
        dsb = c(2, G * (K + 1)).rearrange("p q (j k) -> p q j k", j=G)
        c = cutter(arena_r)
        raw_w, wih_t, wc = c(12, D), c(2 * 3 * D), c(4, D)
        whh_t = c(2 * 3 * D)
        c = cutter(arena_e)
        dst_i, src_i = c(ET)[0:EP].bitcast(I32), c(ET)[0:EP].bitcast(I32)
        w_f, dloc = c(ET)[0:EP], c(ET)[0:EP]
        slot = [c(ET)[0:EP].bitcast(I32), c(ET)[0:EP]]
        c = cutter(arena_e)
        msgs = c(4, G, MSG)
        row_of = c(2, NX)[0:1].bitcast(I32)
        left = c(2, NX)
        c = cutter(arena_e)
        feat, kron, kron_t = c(4, G, ROW), c(G, 4 * KC), c(2, 4 * P)
        normed, clipped = c(2, D), c(2, MSG)
        node = c(NT * (K + 1))
        c = cutter(arena_e)
        gln_b, bln_b, gc_b, bc_b, xf, cx, wa, wb, outb = [c(D) for _ in range(9)]
        cat, tr4, cat_t, rz, bih_r, bhh_r, bcr_r = c(2 * D), c(4 * P), c(4 * P), c(2 * D), c(3 * D), c(3 * D), c(D)

        ident = sb("ident", [P, P])
        ones = sb("ones", [P, P])
        iota = sb("iota", [P, P])
        gidx = sb("gidx", [P, 4])
        minus_half = sb("minus_half", [P, 1])
        eps_c = sb("eps_c", [P, 1])
        eps_root = sb("eps_root", [1, 1])
        gate = sb("gate", [P, 6])
        cnt, gsz, gend, base = (sb(n, [P, NB]) for n in ("cnt", "gsz", "gend", "base"))
        gsz_i = sb("gsz_i", [P, 2, NB], I32)
        tmap_f = sb("tmap_f", [P, 4])
        tmap_i = sb("tmap_i", [P, 4, 4], I32)
        left_f = sb("left_f", [P, 2, 4])
        total = sb("total", [P, NB + 1])
        short = sb("short", [P, NB])
        slot128 = sb("slot128", [P, G])
        moved = sb("moved", [P, 1])
        moved_i = sb("moved_i", [1, 1], I32)
        far = sb("far", [P, G])
        tile_of = sb("tile_of", [1, 2, NX], I32)
        stage = sb("stage", [P, SC * 5])
        sidx_f = stage[0:EP, SC * 4:SC * 5]
        sidx = sb("sidx", [P, SC], I32)
        recq = sb("recq", [P, 4, 16])
        oh = sb("oh", [P, 4, GE])
        idxq = sb("idxq", [P, 4, G], I32)
        sloc_i = sb("sloc_i", [P, G], I32)
        wk = sb("wk", [P, 4, HC])
        w0_t = sb("w0_t", [P, 2 * D])
        wt = sb("wt", [P, 2, ROW])
        wt_b = sb("wt_b", [1, ROW])
        gk_b, betak_b, nbetak_b = (sb(n, [P, D]) for n in ("gk_b", "betak_b", "nbetak_b"))
        gp_b, betap_b = sb("gp_b", [P, K]), sb("betap_b", [P, K])
        row = sb("row", [P, ROW])
        st = sb("st", [P, 16])
        tr2 = sb("tr2", [P, 2, D])
        junk = sb("junk", [P, 2, HC])
        y_sb, x1_sb = junk[:, 0, 0:D], junk[:, 1, 0:D]
        lg = sb("lg", [P, 2, G])
        valid = sb("valid", [P, G])
        mg = sb("mg", [P, 2])
        mnew = sb("mnew", [P, 1])
        mrun = sb("mrun", [P, NT])
        edd = sb("edd", [P, 2, 8])
        ee = sb("ee", [P, 2, 8])
        var = sb("var", [P, G])
        rstd = sb("rstd", [P, G])

        s_in, s_wt, s_w0, s_x = sem("edges_loaded"), sem("weights_loaded"), sem("w0_loaded"), sem("x_loaded")
        pool_steps, dve_steps, act_steps = sem("pool_steps"), sem("dve_steps"), sem("act_steps")
        s_const, s_wzero, s_cen = sem("constants_ready"), sem("weights_cleared"), sem("kron_weights_centered")
        s_counted, s_totals = sem("buckets_counted"), sem("bucket_totals_ready")
        s_prod, s_psum = sem("slot_product_ready"), sem("slot_product_added")
        s_map, s_mapst, s_mapld = sem("tile_map_ready"), sem("tile_map_stored"), sem("tile_map_loaded")
        s_slots, s_xclr = sem("slots_ready"), sem("x_tail_cleared")
        s_place, s_packed, s_moved, s_flag = (sem(n) for n in (
            "places_ready", "records_packed", "moved_edges_counted", "moved_edges_known"))
        s_recst, s_stage, s_scat, s_order = (sem(n) for n in (
            "records_stored", "records_staged", "records_scattered", "records_in_order"))
        s_tail, s_tailst = sem("tail_ready"), sem("tail_stored")
        s_rowld, s_recs = sem("rows_and_left_loaded"), sem("records_loaded")
        s_w0t = sem("w0_turned")
        m_oh, m_oht, m_ohts, m_x, m_msg, m_loc = (sem("m_" + n) for n in (
            "onehot", "onehot_t", "onehot_t_sbuf", "rows", "messages", "slots_and_locals"))
        m_gate = sem("m_scatter_gate")
        m_out = [sem(f"m_scattered{q}") for q in range(4)]
        a_in = [sem(f"a_messages_loaded{q}") for q in range(4)]
        a_oh, a_sum, a_add = sem("a_onehot"), sem("a_summed"), sem("a_added")
        n_agg = sem("n_aggregate")
        n_t, n_ts, n_lin, n_var, n_std, n_x1, n_tab, n_hv, n_row, n_st = (sem("n_" + n) for n in (
            "turned", "turned_sbuf", "linear", "variance", "deviation", "x1", "table", "values", "row", "stored"))
        l_rec, l_oh, l_oht, l_ohts, l_d = (sem("l_" + n) for n in (
            "records", "onehot", "onehot_t", "onehot_t_sbuf", "dst_rows"))
        l_feat = [sem(f"l_rows_gathered{q}") for q in range(4)]
        l_ohl, l_ohlt, l_mg, l_me, l_dd, l_ex, l_wex, l_ctx, l_comb, l_ksum = (sem("l_" + n) for n in (
            "logits", "logits_t", "group_max", "edge_max", "differences", "exponentials",
            "weighted_onehot", "context", "context_added", "kron_added"))
        k_kron, k_t, k_ts, k_h, k_sq, k_rs, k_n, k_seg = (sem("k_" + n) for n in (
            "products", "turned", "turned_sbuf", "linear", "variance", "rstd", "normed", "summed"))
        f_w, f_wp, f_ws, f_x, f_pre, f_t, f_ts, f_gate, f_sig, f_n0, f_tanh = (sem("f_" + n) for n in (
            "weights_loaded", "weights_turned", "weights_turned_sbuf", "x1_loaded", "context", "turned",
            "turned_sbuf", "gates", "sigmoid", "candidate", "tanh"))
        f_var, f_std, f_cat, f_ct, f_cts, f_lin, f_out, f_st = (sem("f_" + n) for n in (
            "variance", "deviation", "features", "features_t", "features_t_sbuf", "linear", "result", "stored"))

        def nth(i, head=0):
            return i + 1 + head

        HEAD = 4

        def tiles_of(engine, order, g, n):
            _, v = nc.values_load_multi_w_load_instructions(
                tile_of[0:1, order, bass.ds(g, n)], engines=[engine], min_val=0, max_val=NT - 1,
                skip_runtime_bounds_check_because="the map is clamped to the last tile")
            return v

        def first_rows(order, g, n):
            _, v = nc.values_load_multi_w_load_instructions(
                row_of[0:1, order, bass.ds(g, n)], engines=[ENG.SP], min_val=0, max_val=E,
                skip_runtime_bounds_check_because="the rows are clamped to the edges' number")
            return v

        def rec(u):
            return recq[:, u, :].rearrange("p (j f) -> p j f", f=4)

        def over_nodes(a):
            return a.unsqueeze(2).broadcast_to([P, G, P])

        iota_g = iota[:, :].unsqueeze(1).broadcast_to([P, G, P])

        def grouped(a):
            return a.rearrange("p (j n) -> p j n", j=G)

        def node_of(t, n=K + 1):
            return at(node, t, n, K + 1)

        block = ctx.enter_context(nc.Block())

        @block.sync
        def _(sp):
            sp.dma_start(dst_i, io["dst"].rearrange("(p t) -> p t", p=EP)).then_inc(s_in, 16)
            sp.dma_start(src_i, io["src"].rearrange("(p t) -> p t", p=EP)).then_inc(s_in, 16)
            sp.dma_start(w_f, io["edge_weight"].rearrange("(p t) -> p t", p=EP)).then_inc(s_in, 16)
            for k in range(2):
                sp.wait_ge(s_map, k + 1)
                for i in range(2):
                    sp.dma_start(map_dram[2 * k + i].rearrange("(c p) -> p c", c=4), tmap_i[0:GP, 2 * k + i, :],
                                 allow_slow_non_contiguous=True).then_inc(s_mapst, 16)
                sp.dma_start(left_dram[k].rearrange("(c p) -> p c", c=4), left_f[0:GP, k, :],
                             allow_slow_non_contiguous=True).then_inc(s_mapst, 16)
                sp.wait_ge(s_mapst, 48 * (k + 1))
                sp.dma_start(tile_of[0:1, k, :], map_dram[2 * k:2 * k + 1, :]).then_inc(s_mapld, 16)
            sp.wait_ge(s_tail, 1)
            sp.dma_start(rec_dram[E:E + GE, :].rearrange("(p j) c -> p (j c)", p=P), tail[:, 0:G * 4]).then_inc(s_tailst, 16)
            sp.dma_start(msg_dram[E:E + GE, :].rearrange("(p j) c -> p (j c)", p=P), tail).then_inc(s_tailst, 16)
            sp.wait_ge(s_packed, 4)
            sp.dma_start(rec_dram[0:E, :].rearrange("(p t) f -> p (t f)", p=EP), recs).then_inc(s_recst, 16)
            xv = x_all.rearrange("p (t c) -> p t c", c=MSG)
            sp.dma_start(xv[:, 0:NT - 1, 0:D],
                         io["x"][0:(NT - 1) * P, :].rearrange("(t p) d -> p t d", p=P)).then_inc(s_x, 16)
            sp.wait_ge(s_xclr, 1)
            sp.dma_start(xv[0:VL, NT - 1, 0:D], io["x"][(NT - 1) * P:V, :]).then_inc(s_x, 16)
            sp.wait_ge(s_order, 1)
            sp.wait_ge(s_tailst, 32)
            for k in range(2):
                sp.dma_start(row_of[:, k, :], map_dram[2 * k + 1:2 * k + 2, :]).then_inc(s_rowld, 16)
                sp.dma_start(left[:, k, :], left_dram[k].partition_broadcast(P)).then_inc(s_rowld, 16)
            sp.wait_ge(s_rowld, 64)
            sp.sem_inc(s_recs, HEAD)
            with sp.Fori(0, GP) as it:
                start = first_rows(0, it * 4, 4)
                sp.wait_ge(s_recs, 64 * it + HEAD)
                for u in range(4):
                    sp.dma_start(at(rec_all, it * 4 + u, 16, 16),
                                 rec_dram[bass.ds(start[u], GE), :].rearrange("(p j) f -> p (j f)", p=P)
                                 ).then_inc(s_recs, 16)
            for u in range(4):
                sp.wait_ge(m_out[u], 16 * G * (NG // 4))

            def load_messages(g, start, u):
                sp.wait_ge(a_sum, nth(g - 4, HEAD))
                sp.dma_start(msgs[:, u].rearrange("p j c -> p (j c)"),
                             msg_dram[bass.ds(start, GE), :].rearrange("(p j) c -> p (j c)", p=P)).then_inc(a_in[u], 16)

            with sp.Fori(0, NG // 4) as it:
                start = first_rows(1, it * 4, 4)
                for u in range(4):
                    load_messages(it * 4 + u, start[u], u)
            load_messages(NG, first_rows(1, NG, 1)[0], 0)
            with sp.Fori(0, NT) as t:
                sp.wait_ge(n_x1, t + 1)
                sp.dma_start(rows(x1_dram, t), x1_sb[:, :]).then_inc(n_st, 16)
                sp.wait_ge(n_row, nth(t, HEAD))
                sp.wait_ge(n_hv, nth(t, HEAD))
                sp.dma_start(rows(tab_dram, t), row[:, :]).then_inc(n_st, 16)
            sp.wait_ge(l_ksum, nth(NG - 1, HEAD))
            sp.wait_ge(k_kron, nth(4 * NG + 1))
            sp.wait_ge(k_ts, nth(4 * NG, HEAD))
            sp.wait_ge(k_seg, nth(4 * NG - 1, HEAD))
            for u in range(4):
                sp.wait_ge(l_feat[u], 16 * G * (NG // 4 + (u < 3)))
            sp.dma_start(raw_w[:, 0:6, :], io["L1_gnn_W_ih"].rearrange("(a p) d -> p a d", p=P)).then_inc(f_w, 16)
            sp.dma_start(raw_w[:, 6:12, :], io["L1_gnn_W_hh"].rearrange("(a p) d -> p a d", p=P)).then_inc(f_w, 16)
            sp.dma_start(wc, io["L1_gnn_Wc"].rearrange("(a p) d -> p a d", p=P)).then_inc(f_w, 16)
            for dst, name in ((gln_b, "g_ln"), (bln_b, "beta_ln"), (gc_b, "gc"), (bc_b, "betac")):
                sp.dma_start(dst, io["L1_gnn_" + name].partition_broadcast(P)).then_inc(f_w, 16)
            for dst, name in ((bih_r, "b_ih"), (bhh_r, "b_hh"), (bcr_r, "bc")):
                sp.dma_start(dst[0:1, :], io["L1_gnn_" + name].unsqueeze(0)).then_inc(f_w, 16)

            def results(t, n):
                sp.wait_ge(f_out, nth(t - 1, HEAD))
                sp.dma_start(xf, rows(x1_dram, t)).then_inc(f_x, 16)
                sp.wait_ge(f_out, nth(t, HEAD))
                sp.dma_start(rows(io["out"], t, n), outb[0:n, :]).then_inc(f_st, 16)

            with sp.Fori(0, NT - 1) as t:
                results(t, P)
            results(NT - 1, VL)
            sp.wait_ge(f_st, 16 * NT)

        @block.gpsimd
        def _(pool):
            step = Chain(pool, pool_steps)
            step(nc.gpsimd.memset(ident[:, :], 0.0))
            step(nc.gpsimd.affine_select(out=ident[:, :], in_=ident[:, :], compare_op=ALU.not_equal, fill=1.0,
                                         base=0, pattern=[[-1, P]], channel_multiplier=1))
            step(nc.gpsimd.memset(before, 1.0))
            step(nc.gpsimd.affine_select(out=before, in_=before, compare_op=ALU.is_gt, fill=0.0,
                                         base=0, pattern=[[1, P]], channel_multiplier=-1))
            step(nc.gpsimd.iota(iota[:, :], [[1, P]], base=0, channel_multiplier=0,
                                allow_small_or_imprecise_dtypes=True))
            step(nc.gpsimd.iota(gidx[0:GP, :], [[GP, 4]], base=0, channel_multiplier=1,
                                allow_small_or_imprecise_dtypes=True))
            step(nc.gpsimd.iota(slot128[:, :], [[P, G]], base=P, channel_multiplier=G * P,
                                allow_small_or_imprecise_dtypes=True))
            step(nc.gpsimd.memset(minus_half[:, :], -0.5))
            step(nc.gpsimd.memset(eps_c[:, :], EPS))
            step(nc.gpsimd.memset(eps_root[:, :], 16.0 * EPS ** 0.5))
            step(nc.gpsimd.memset(ones[:, :], 1.0))
            nc.gpsimd.memset(gate[:, :], 0.0).then_inc(s_const, 1)
            pool.sem_inc(m_gate, HEAD)
            pool.wait_ge(s_slots, 2)
            nc.gpsimd.iota(place, [[1, ET]], base=0, channel_multiplier=ET,
                           allow_small_or_imprecise_dtypes=True).then_inc(s_place, 1)
            pool.wait_ge(s_flag, 1)
            pool.wait_ge(s_recst, 16)
            pool.wait_ge(s_packed, 4)
            with pool.If(nc.values_load(moved_i[0:1, 0:1], engines=[ENG.Pool], min_val=0, max_val=E,
                                        skip_runtime_bounds_check_because="a count of edges") > 0):
                with pool.Fori(0, SL) as it:
                    nc.gpsimd.tensor_tensor(stage[0:EP, 0:4 * SC], at(recs, it, 4 * SC, 4 * SC), ones[0:EP, 0:4 * SC],
                                            ALU.mult).then_inc(s_stage, 1)
                    nc.gpsimd.tensor_tensor(sidx_f, at(slot_f, it, SC, SC), ones[0:EP, 0:SC],
                                            ALU.mult).then_inc(s_stage, 1)
                    pool.wait_ge(s_stage, 5 * it + 2)
                    nc.gpsimd.tensor_tensor(gate[:, 4:5], ones[:, 0:1], ones[:, 1:2], ALU.mult).then_inc(s_stage, 1)
                    nc.gpsimd.tensor_copy(sidx[0:EP, :], sidx_f).then_inc(s_stage, 1)
                    pool.wait_ge(s_stage, 5 * it + 4)
                    nc.gpsimd.tensor_tensor(gate[:, 5:6], ones[:, 0:1], ones[:, 1:2], ALU.mult).then_inc(s_stage, 1)
                    for i in range(SC):
                        nc.gpsimd.indirect_dma_start(
                            out=rec_dram, in_=stage[0:EP, 4 * i:4 * i + 4], in_offset=None,
                            out_offset=bass.IndirectOffsetOnAxis(ap=sidx[0:EP, i:i + 1].bitcast(U32), axis=0),
                        ).then_inc(s_scat, 16)
                    pool.wait_ge(s_scat, 16 * SC * (it + 1))
            pool.sem_inc(s_order, 1)
            with pool.Fori(0, NG // 4) as it:
                for u in range(4):
                    pool.wait_ge(m_loc, nth(it * 4 + u))
                    pool.wait_ge(m_msg, nth((it * 4 + u) * 4 + 3, HEAD))
                    nc.gpsimd.tensor_tensor(gate[:, u:u + 1], ones[:, 0:1], ones[:, 1:2], ALU.mult).then_inc(m_gate, 1)
                    for j in range(G):
                        nc.gpsimd.indirect_dma_start(
                            out=msg_dram, in_=msgs[:, u, j, :], in_offset=None,
                            out_offset=bass.IndirectOffsetOnAxis(ap=idxq[:, u, j:j + 1].bitcast(U32), axis=0),
                            bounds_check=E - 1, oob_is_err=False,
                        ).then_inc(m_out[u], 16)

            def gather(u, j):
                nc.gpsimd.indirect_dma_start(
                    out=feat[:, u, j, :], out_offset=None, in_=tab_dram,
                    in_offset=bass.IndirectOffsetOnAxis(ap=idxq[:, u, j:j + 1].bitcast(U32), axis=0),
                ).then_inc(l_feat[u], 16)

            pool.wait_ge(n_st, 32 * NT)
            pool.wait_ge(l_rec, 3)
            for u in range(3):
                for j in range(G):
                    gather(u, j)
            with pool.Fori(0, NG // 4) as it:
                for u in range(4):
                    g = it * 4 + u
                    pool.wait_ge(l_rec, nth(g + 3))
                    for j in range(G):
                        pool.wait_ge(k_sq, nth(g * 4 + j, HEAD))
                        nc.gpsimd.tensor_tensor(rstd[:, j:j + 1], var[:, j:j + 1], minus_half[:, :],
                                                ALU.pow).then_inc(k_rs, 1)
                        gather((u + 3) % 4, j)

        @block.scalar
        def _(act):
            step = Chain(act, act_steps)
            act.wait_ge(s_wzero, 1)
            L1 = "L1_gnn_"
            for c in range(3):
                act.dma_start(wk[0:KC, c, 0:D], io[L1 + "Wk"][c * KC:(c + 1) * KC, :]).then_inc(s_wt, 16)
            last = K * K - 3 * KC
            act.dma_start(wk[0:last, 3, 0:D], io[L1 + "Wk"][3 * KC:K * K, :]).then_inc(s_wt, 16)
            act.dma_start(wk[last:last + 1, 3, 0:D], io[L1 + "bk"].unsqueeze(0)).then_inc(s_wt, 16)
            act.wait_ge(s_const, 1)
            act.dma_start(wk[last:last + 1, 3, D:D + 1], eps_root[:, :]).then_inc(s_wt, 16)
            with nc.allow_non_contiguous_dma("columns of weights"):
                act.dma_start(wt[:, :, 0:D], io[L1 + "Wn"].rearrange("(c p) d -> p c d", p=P)).then_inc(s_wt, 16)
                act.dma_start(wt[:, :, D:D + 1], io[L1 + "We"][0:D, :].rearrange("(c p) d -> p c d", p=P)).then_inc(s_wt, 16)
                act.dma_start(wt[:, :, D + 1:D + 1 + K], io[L1 + "Wp"].rearrange("(c p) d -> p c d", p=P)).then_inc(s_wt, 16)
                act.dma_start(wt[:, :, ROW - 1:ROW], io[L1 + "We"][D:2 * D, :].rearrange("(c p) d -> p c d", p=P)).then_inc(s_wt, 16)
            act.dma_start(wt_b[:, 0:D], io[L1 + "bn"].unsqueeze(0)).then_inc(s_wt, 16)
            act.dma_start(wt_b[:, D:D + 1], io[L1 + "be"].unsqueeze(0)).then_inc(s_wt, 16)
            act.dma_start(wt_b[:, D + 1:D + 1 + K], io[L1 + "bp"].unsqueeze(0)).then_inc(s_wt, 16)
            for dst, name in ((gk_b, "gk"), (betak_b, "betak"), (gp_b, "gp"), (betap_b, "betap")):
                act.dma_start(dst[:, :], io[L1 + name].partition_broadcast(P)).then_inc(s_wt, 16)
            act.dma_start(tr2[:, :, :], io["L0_gnn_W"].rearrange("(c p) d -> p c d", p=P)).then_inc(s_w0, 16)
            act.wait_ge(s_w0t, 1)
            step(nc.scalar.activation(w0_t[:, :], ps[:, 7, :], ACT.Copy))

            act.sem_inc(m_msg, HEAD)

            def weigh(it):
                for u in range(4):
                    g, q = it * 4 + u, u % 2
                    act.wait_ge(m_oht, nth(g, HEAD))
                    nc.scalar.activation(oh_t[:, q, :], ps[:, q, :], ACT.Copy).then_inc(m_ohts, 1)
                    if not is_zero(it):
                        act.wait_ge(m_out[u], 16 * G * it)
                    for j in range(G):
                        act.wait_ge(m_x, nth(g * 4 + j))
                        nc.scalar.activation(msgs[:, u, j, 0:D], ps[:, 2 + j, 0:D], ACT.Copy,
                                             scale=recq[:, u, 4 * j + 2:4 * j + 3]).then_inc(m_msg, 1)

            weigh(0)
            with act.Fori(1, NG // 4) as it:
                weigh(it)

            def node_functions(t):
                for h in range(2):
                    act.wait_ge(n_t, nth(t * 2 + h))
                    nc.scalar.activation(tr2[:, h, :], ps[:, h, 0:D], ACT.Copy).then_inc(n_ts, 1)
                    if h == 0:
                        act.wait_ge(n_var, nth(t * 2))
                        nc.scalar.activation(st[:, 8:9], st[:, 7:8], ACT.Sqrt, bias=eps_c[:, :]).then_inc(n_std, 1)
                act.wait_ge(n_tab, nth(t))
                if not is_zero(t):
                    act.wait_ge(n_st, 32 * t)
                nc.scalar.activation(row[:, :], ps[:, 3, 0:ROW], ACT.Copy).then_inc(n_hv, 1)
                act.wait_ge(n_var, nth(t * 2 + 1))
                nc.scalar.activation(st[:, 8:9], st[:, 7:8], ACT.Sqrt, bias=eps_c[:, :]).then_inc(n_std, 1)

            act.sem_inc(n_hv, HEAD)
            node_functions(0)
            with act.Fori(1, NT) as t:
                node_functions(t)

            act.sem_inc(k_ts, HEAD)
            act.sem_inc(k_sq, HEAD)

            def evacuate(tau, b):
                act.wait_ge(k_t, nth(tau, HEAD))
                act.wait_ge(k_h, nth(tau - 2, HEAD))
                nc.scalar.activation(kron_t[0:KC, b, :], ps[0:KC, b, :], ACT.Copy).then_inc(k_ts, 1)

            def square(tau, j):
                act.wait_ge(k_h, nth(tau, HEAD))
                act.wait_ge(k_sq, nth(tau - 2, HEAD))
                nc.scalar.activation(junk[:, j % 2, :], ps[:, 2 + j % 2, 0:HC], ACT.Square, scale=1.0 / 16,
                                     accum_out=var[:, j:j + 1]).then_inc(k_sq, 1)

            def evacuate_onehot(g, q):
                act.wait_ge(l_oht, nth(g))
                nc.scalar.activation(oh_t[:, q, :], ps[:, 6, :], ACT.Copy).then_inc(l_ohts, 1)

            def exponentials(g, q):
                act.wait_ge(l_dd, nth(g, HEAD))
                nc.scalar.activation(ee[:, q, 0:6], edd[:, q, 0:6], ACT.Exp).then_inc(l_ex, 1)

            evacuate_onehot(0, 0)
            exponentials(0, 0)
            evacuate(0, 0)
            with act.Fori(0, NG // 4) as it:
                for u in range(4):
                    g, q = it * 4 + u, u % 2
                    for j in range(G):
                        if j == 1:
                            evacuate_onehot(g + 1, 1 - q)
                        evacuate(g * 4 + j + 1, (j + 1) % 2)
                        square(g * 4 + j, j)
                    exponentials(g + 1, 1 - q)

            for b in range(6):
                act.wait_ge(f_wp, b + 1)
                dst = (wih_t if b < 3 else whh_t)[:, (b % 3) * 512:(b % 3 + 1) * 512]
                nc.scalar.activation(dst, ps[:, b, :], ACT.Copy).then_inc(f_ws, 1)

            def functions(t):
                act.wait_ge(f_t, nth(t))
                nc.scalar.activation(tr4, ps[:, 0, :], ACT.Copy).then_inc(f_ts, 1)
                act.wait_ge(f_gate, nth(t))
                nc.scalar.activation(rz, ps[:, 1, :], ACT.Sigmoid).then_inc(f_sig, 1)
                act.wait_ge(f_n0, nth(t))
                nc.scalar.activation(wb, wa, ACT.Tanh).then_inc(f_tanh, 1)
                for i in range(3):
                    act.wait_ge(f_var, nth(t * 3 + i))
                    nc.scalar.activation(st[:, 8:9], st[:, 7:8], ACT.Sqrt, bias=eps_c[:, :]).then_inc(f_std, 1)
                    if i == 0:
                        act.wait_ge(f_ct, nth(t))
                        nc.scalar.activation(cat_t, ps[:, 3, :], ACT.Copy).then_inc(f_cts, 1)

            with act.Fori(0, NT - 1) as t:
                functions(t)
            functions(NT - 1)

        @block.vector
        def _(dve):
            step = Chain(dve, dve_steps)
            def move(out, src):
                return nc.vector.tensor_scalar(out, src, 1.0, None, ALU.mult)

            tt, ts, stt = nc.vector.tensor_tensor, nc.vector.tensor_scalar, nc.vector.scalar_tensor_tensor
            step(nc.vector.memset(wk[:, :, :], 0.0))
            nc.vector.memset(wt_b[:, ROW - 1:ROW], 0.0).then_inc(s_wzero, 1)
            dve.wait_ge(s_in, 48)
            step(ts(bk_i, dst_i, P - 1, None, ALU.bitwise_and))
            step(nc.vector.tensor_copy(dloc, bk_i))
            dve.wait_ge(s_const, 1)
            dve.wait_ge(pool_steps, 11)
            one_row = ones[0:EP, 0:1].broadcast_to([EP, ET])
            for k, ids in enumerate((dst_i, src_i)):
                step(ts(bk_i, ids, 7, None, ALU.arith_shift_right))
                step(nc.vector.tensor_copy(bk_f, bk_i))
                with dve.Fori(0, NB) as b:
                    ts(at(mask8, b, ET, ET), bk_f, at(iota[0:EP, :], b), 0.0, ALU.is_equal, ALU.add,
                       accum_out=at(cnt[0:EP, :], b)).then_inc(s_counted, 1)
                dve.wait_ge(s_totals, k + 1)
                step(nc.vector.tensor_copy(total[:, 0:NB], ps[:, 4, 0:NB]))
                step(nc.vector.memset(total[:, NB:NB + 1], 0.0))
                step(nc.vector.tensor_tensor_scan(base[:, :], ones[:, 0:NB], total[:, 0:NB], 0.0, ALU.mult, ALU.add))
                step(tt(base[:, :], base[:, :], total[:, 0:NB], ALU.subtract))
                step(stt(out=base[0:EP, :], in0=base[0:EP, :], scalar=-1.0, in1=ps[0:EP, 5, 0:NB],
                         op0=ALU.add, op1=ALU.add))
                step(ts(gsz_i[:, 0, :], total[:, 0:NB], float(GE - 1), None, ALU.add))
                step(ts(gsz_i[:, 1, :], gsz_i[:, 0, :], GE.bit_length() - 1, None, ALU.arith_shift_right))
                step(nc.vector.tensor_copy(gsz[:, :], gsz_i[:, 1, :]))
                step(nc.vector.tensor_tensor_scan(gend[:, :], ones[:, 0:NB], gsz[:, :], 0.0, ALU.mult, ALU.add))
                step(tt(cmp[0:GP], gend[0:GP, :].unsqueeze(1).broadcast_to([GP, 4, NB]),
                        gidx[0:GP, :].unsqueeze(2).broadcast_to([GP, 4, NB]), ALU.is_le))
                step(nc.vector.tensor_reduce(tmap_f[0:GP, :], cmp[0:GP], AX_X, ALU.add))
                step(ts(tmap_i[0:GP, 2 * k, :], tmap_f[0:GP, :], float(NT - 1), None, ALU.min))

                def over_buckets(a):
                    return a.unsqueeze(1).broadcast_to([GP, 4, NB])

                step(stt(out=short[:, :], in0=gsz[:, :], scalar=-float(GE), in1=total[:, 0:NB],
                         op0=ALU.mult, op1=ALU.add))
                step(tt(weighed[0:GP], cmp[0:GP], over_buckets(short[0:GP, :]), ALU.mult))
                step(nc.vector.tensor_reduce(tmap_f[0:GP, :], weighed[0:GP], AX_X, ALU.add))
                step(stt(out=tmap_f[0:GP, :], in0=gidx[0:GP, :], scalar=float(GE), in1=tmap_f[0:GP, :],
                         op0=ALU.mult, op1=ALU.add))
                step(ts(tmap_f[0:GP, :], tmap_f[0:GP, :], float(E), None, ALU.min))
                step(nc.vector.tensor_copy(tmap_i[0:GP, 2 * k + 1, :], tmap_f[0:GP, :]))
                step(tt(weighed[0:GP], cmp[0:GP], over_buckets(total[0:GP, 1:NB + 1]), ALU.mult))
                step(nc.vector.tensor_reduce(left_f[0:GP, k, :], weighed[0:GP], AX_X, ALU.add))
                step(ts(left_f[0:GP, k, :], left_f[0:GP, k, :], total[0:GP, 0:1], None, ALU.add))
                step(tt(left_f[0:GP, k, :], left_f[0:GP, k, :], tmap_f[0:GP, :], ALU.subtract))
                ts(left_f[0:GP, k, :], left_f[0:GP, k, :], float(P), None, ALU.mult).then_inc(s_map, 1)
                held = step.done
                with dve.Fori(0, NB // 2) as it:
                    step.loop(held, it, 2)
                    for q in range(2):
                        m = at(mask8, it * 2 + q, ET, ET)
                        step(nc.vector.tensor_tensor_scan(scan[q], one_row, m, at(base[0:EP, :], it * 2 + q),
                                                          ALU.mult, ALU.add))
                        dve.wait_ge(s_psum, nth(it * 2 + (k * NB + q - 2), HEAD))
                        tt(prod[q], scan[q], m, ALU.mult).then_inc(s_prod, 1)
                step.loop_ended(held, NB // 2, 2)
                dve.wait_ge(s_prod, NB * (k + 1))
                dve.wait_ge(s_psum, nth((k + 1) * NB - 1, HEAD))
                nc.vector.tensor_copy(slot[k], ps[0:EP, 0:4, :].rearrange("p b c -> p (b c)")[:, 0:ET]
                                      ).then_inc(s_slots, 1)
            dve.wait_ge(s_slots, 2)
            nc.vector.memset(x_all[:, (NT - 1) * MSG:NT * MSG], 0.0).then_inc(s_xclr, 1)
            nc.vector.memset(tail, 0.0).then_inc(s_tail, 1)

            for f, field in enumerate((src_i, dloc, w_f, slot[1])):
                nc.vector.tensor_copy(recs.rearrange("p (t f) -> p t f", f=4)[:, :, f], field).then_inc(s_packed, 1)
            step(nc.vector.tensor_copy(slot_f, slot[0]))
            dve.wait_ge(s_place, 1)
            step(tt(place, place, slot_f, ALU.not_equal))
            nc.vector.tensor_reduce(moved[0:EP, :], place, AX_X, ALU.add).then_inc(s_moved, 1)
            dve.wait_ge(s_moved, 2)
            nc.vector.tensor_copy(moved_i[:, :], ps[0:1, 4, 0:1]).then_inc(s_flag, 1)

            dve.wait_ge(s_wt, 16 * 17)
            for c in range(4):
                step(nc.vector.tensor_reduce(var[:, c:c + 1], wk[:, c, 0:D], AX_X, ALU.add))
            step(ts(var[:, :], var[:, :], 1.0 / D, None, ALU.mult))
            for c in range(4):
                step(ts(wk[:, c, 0:D], wk[:, c, 0:D], var[:, c:c + 1], None, ALU.subtract))
            step(ts(nbetak_b[:, :], betak_b[:, :], -1.0, None, ALU.mult))

            def onehot(out, local):
                return tt(grouped(out), iota_g, over_nodes(local), ALU.is_equal)

            dve.wait_ge(s_rowld, 64)
            held = step.done

            def prepare_messages(it):
                step.loop(held, it, 32)
                for u in range(4):
                    g, q = it * 4 + u, u % 2
                    if not is_zero(it):
                        dve.wait_ge(m_out[u], 16 * G * it)
                    dve.wait_ge(m_gate, nth(g - 4, HEAD))
                    dve.wait_ge(m_oht, nth(g - 2, HEAD))
                    dve.wait_ge(s_recs, 64 * (it + 1) + HEAD)
                    step(move(recq[:, u, :], at(rec_all, g, 16, 16)))
                    local, there = rec(u)[:, :, 1], rec(u)[:, :, 3]
                    step(stt(out=local, in0=slot128[:, :], scalar=at(left[:, 0, :], g), in1=local,
                             op0=ALU.subtract, op1=ALU.max))
                    step(ts(far[:, :], local, float(P), float(FAR), ALU.is_ge, ALU.mult))
                    step(tt(there, there, far[:, :], ALU.max))
                    step(move(at(rec_all, g, 16, 16), recq[:, u, :]))
                    onehot(oh[:, q, :], rec(u)[:, :, 1]).then_inc(m_oh, 1)
                    step(nc.vector.tensor_copy(idxq[:, u, :], rec(u)[:, :, 3]))
                    step(nc.vector.tensor_copy(sloc_i[:, :], rec(u)[:, :, 0]))
                    step(ts(sloc_i[:, :], sloc_i[:, :], P - 1, None, ALU.bitwise_and))
                    nc.vector.tensor_copy(msgs[:, u, :, D], sloc_i[:, :]).then_inc(m_loc, 1)

            prepare_messages(0)
            with dve.Fori(1, NG // 4) as it:
                prepare_messages(it)
            step.loop_ended(held, NG // 4, 32)
            dve.wait_ge(s_recs, 64 * GP + HEAD)
            read_ahead = rec_all[:, NG * 16:NX * 16].rearrange("p (n f) -> p n f", f=4)
            step(ts(read_ahead[:, :, 1], read_ahead[:, :, 1], float(P), None, ALU.add))

            step(nc.vector.memset(agg_all, 0.0))
            dve.wait_ge(a_in[0], 16)

            def mask_pads(g, u):
                local = msgs[:, u, :, D]
                step(stt(out=local, in0=slot128[:, :], scalar=at(left[:, 1, :], g), in1=local,
                         op0=ALU.subtract, op1=ALU.max))

            mask_pads(0, 0)
            onehot(oh[:, 0, :], msgs[:, 0, :, D]).then_inc(a_oh, 1)
            held = step.done
            dve.wait_ge(s_mapld, 32)
            dve.sem_inc(a_add, HEAD)
            with dve.Fori(0, NG // 4) as it:
                step.loop(held, it, 4)
                nt = tiles_of(ENG.DVE, 1, it * 4, 4)
                for u in range(4):
                    g, q = it * 4 + u, u % 2
                    dve.wait_ge(a_in[(u + 1) % 4], 16 * (it + 1 + (u == 3)))
                    mask_pads(g + 1, (u + 1) % 4)
                    dve.wait_ge(a_sum, nth(g - 1, HEAD))
                    onehot(oh[:, 1 - q, :], msgs[:, (u + 1) % 4, :, D]).then_inc(a_oh, 1)
                    dve.wait_ge(a_sum, nth(g, HEAD))
                    dve.wait_ge(a_add, nth(g - 1, HEAD))
                    tt(at(agg_all, nt[u], D, MSG), at(agg_all, nt[u], D, MSG), ps[:, q, 0:D], ALU.add).then_inc(a_add, 1)
            step.loop_ended(held, NG // 4, 4)

            def norm_stats(src, out):
                nc.vector.bn_stats(st[:, 0:6], src)
                dve.drain()
                nc.vector.bn_aggr(st[:, 6:8], st[:, 0:6]).then_inc(out, 1)

            def normalize(out, src, deviation, i):
                dve.wait_ge(deviation, i)
                step(nc.vector.reciprocal(st[:, 9:10], st[:, 8:9]))
                return ts(out, src, st[:, 6:7], st[:, 9:10], ALU.subtract, ALU.mult)

            dve.wait_ge(a_add, nth(NG - 1, HEAD))
            dve.wait_ge(s_x, 32)
            held = step.done

            def node_stage(t):
                step.loop(held, t, 9)
                move(y_sb[:, :], at(agg_all, t, D, MSG)).then_inc(n_agg, 1)
                dve.wait_ge(n_lin, nth(t))
                step(stt(out=y_sb[:, :], in0=ps[:, 2, 0:D], scalar=0.0, in1=at(x_all, t, D, MSG),
                         op0=ALU.max, op1=ALU.add))
                norm_stats(y_sb[:, :], n_var)
                if not is_zero(t):
                    dve.wait_ge(n_st, 32 * t)
                normalize(x1_sb[:, :], y_sb[:, :], n_std, nth(t * 2)).then_inc(n_x1, 1)
                dve.wait_ge(n_hv, nth(t, HEAD))
                pj = row[:, D + 1:D + 1 + K]
                norm_stats(pj, n_var)
                step(normalize(pj, pj, n_std, nth(t * 2 + 1)))
                step(tt(pj, pj, gp_b[:, :], ALU.mult))
                step(tt(pj, pj, betap_b[:, :], ALU.add))
                step(ts(pj, pj, 0.0, None, ALU.max))
                step(move(node_of(t, K), pj))
                step(move(at(node[:, K:], t, 1, K + 1), row[:, D:D + 1]))
                nc.vector.memset(row[:, D:D + 1], 1.0).then_inc(n_row, 1)

            dve.sem_inc(n_row, HEAD)
            node_stage(0)
            with dve.Fori(1, NT) as t:
                node_stage(t)
            step.loop_ended(held, NT, 9)
            dve.wait_ge(n_row, nth(NT - 1, HEAD))

            step(nc.vector.memset(arena_n[:, 0:2 * NA], 0.0))
            step(nc.vector.memset(mrun[:, :], 0.0))
            step(nc.vector.memset(kron[:, :, K * K:K * K + 1], 1.0))
            step(nc.vector.memset(kron[:, :, K * K + 1:4 * KC], 0.0))
            step(nc.vector.memset(clipped[:, :, D:MSG], 1.0))
            dve.sem_inc(k_n, HEAD)

            def take_records(g, u):
                step(move(recq[:, u, :], at(rec_all, g, 16, 16)))
                nc.vector.tensor_copy(idxq[:, u, :], rec(u)[:, :, 0]).then_inc(l_rec, 1)

            def products(tau, u, q, j):
                dve.wait_ge(k_t, nth(tau - 4, HEAD))
                tt(kron[:, j, 0:K * K].rearrange("p (a b) -> p a b", a=K),
                   feat[:, u, j, D + 1:D + 1 + K].unsqueeze(2).broadcast_to([P, K, K]),
                   dsb[:, q, j, 0:K].unsqueeze(1).broadcast_to([P, K, K]), ALU.mult).then_inc(k_kron, 1)

            def local_onehot(g, u):
                onehot(oh[:, u, :], rec(u)[:, :, 1]).then_inc(l_oh, 1)

            def logits(g, u, q, it):
                dve.wait_ge(l_d, nth(g))
                step(nc.vector.tensor_copy(dsb[:, q].rearrange("p j k -> p (j k)"), ps[:, 7, 0:G * (K + 1)]))
                step(ts(valid[:, :], rec(u)[:, :, 1], float(P), None, ALU.is_lt))
                dve.wait_ge(l_feat[u], 16 * G * (it + 1))
                step(tt(lg[:, q, :], feat[:, u, :, ROW - 1], dsb[:, q, :, K], ALU.add))
                step(stt(out=lg[:, q, :], in0=lg[:, q, :], scalar=0.0, in1=valid[:, :], op0=ALU.max, op1=ALU.mult))
                tt(grouped(ohl[:, :]), grouped(oh[:, u, :]), over_nodes(lg[:, q, :]), ALU.mult).then_inc(l_ohl, 1)

            def group_max(g, q):
                dve.wait_ge(l_ohlt, nth(g))
                nc.vector.tensor_reduce(mg[:, q:q + 1], ps[:, 6, :], AX_X, ALU.max).then_inc(l_mg, 1)

            def differences(g, q, nt):
                dve.wait_ge(l_mg, nth(g, HEAD))
                mr, m = at(mrun, nt), mg[:, q:q + 1]
                step(tt(mnew[:, :], mr, m, ALU.max))
                step(tt(edd[:, q, 4:5], mr, mnew[:, :], ALU.subtract))
                step(tt(edd[:, q, 5:6], m, mnew[:, :], ALU.subtract))
                step(move(mr, mnew[:, :]))
                dve.wait_ge(l_me, nth(g))
                tt(edd[:, q, 0:4], lg[:, q, :], ps[:, 7, P:P + G], ALU.subtract).then_inc(l_dd, 1)

            def normalized(tau, j):
                dve.wait_ge(k_rs, nth(tau))
                step(stt(out=normed[:, j % 2, :], in0=ps[:, 2 + j % 2, 0:D], scalar=rstd[:, j:j + 1],
                         in1=gk_b[:, :], op0=ALU.mult, op1=ALU.mult))
                dve.wait_ge(k_seg, nth(tau - 2, HEAD))
                tt(clipped[:, j % 2, 0:D], normed[:, j % 2, :], nbetak_b[:, :], ALU.max).then_inc(k_n, 1)

            def add_kron(g, nt):
                dve.wait_ge(k_seg, nth(g * 4 + 3, HEAD))
                ksum = at(x_all, nt, MSG, MSG)
                tt(ksum, ksum, ps[:, 4, 0:MSG], ALU.add).then_inc(l_ksum, 1)

            for s in (l_mg, l_dd, l_ksum, l_comb):
                dve.sem_inc(s, HEAD)
            for u in range(3):
                take_records(u, u)
            dve.wait_ge(l_rec, 3)
            first = tiles_of(ENG.DVE, 0, 0, 1)
            local_onehot(0, 0)
            logits(0, 0, 0, 0)
            group_max(0, 0)
            differences(0, 0, first[0])
            products(0, 0, 0, 0)
            products(1, 0, 0, 1)
            local_onehot(1, 1)
            held = step.done
            PER = 1 + G + 4 + 4 + 1

            def edge_groups(it, nt, before_nt):
                for u in range(4):
                    g, q, u1, q1 = it * 4 + u, u % 2, (u + 1) % 4, 1 - u % 2
                    started = u > 0 or not is_zero(it)
                    products(g * 4 + 2, u, q, 2)
                    if started:
                        normalized(g * 4 - 1, 3)
                    take_records(g + 3, (u + 3) % 4)
                    dve.wait_ge(l_ex, nth(g))
                    tt(grouped(wex[:, :]), grouped(oh[:, u, :]), over_nodes(ee[:, q, 0:4]), ALU.mult).then_inc(l_wex, 1)
                    products(g * 4 + 3, u, q, 3)
                    normalized(g * 4, 0)
                    logits(g + 1, u1, q1, it + 1 if u == 3 else it)
                    products(g * 4 + 4, u1, q1, 0)
                    normalized(g * 4 + 1, 1)
                    if started:
                        add_kron(g - 1, nt[u - 1] if u > 0 else before_nt)
                    group_max(g + 1, q1)
                    dve.wait_ge(l_ctx, nth(g))
                    att = at(agg_all, nt[u], MSG, MSG)
                    step(ts(att, att, ee[:, q, 4:5], None, ALU.mult))
                    stt(out=att, in0=ps[:, 5, 0:MSG], scalar=ee[:, q, 5:6], in1=att,
                        op0=ALU.mult, op1=ALU.add).then_inc(l_comb, 1)
                    products(g * 4 + 5, u1, q1, 1)
                    normalized(g * 4 + 2, 2)
                    local_onehot(g + 2, (u + 2) % 4)
                    differences(g + 1, q1, nt[u + 1])

            step.loop(held, 0, 4 * PER)
            edge_groups(0, tiles_of(ENG.DVE, 0, 0, 5), None)
            held2 = step.done
            assert held2 == held + 4 * PER - 1
            with dve.Fori(1, NG // 4) as it:
                step.loop(held2 - 4 * PER, it, 4 * PER)
                loaded = tiles_of(ENG.DVE, 0, it * 4 - 1, 6)
                edge_groups(it, loaded[1:], loaded[0])
            step.loop_ended(held2 - 4 * PER, NG // 4, 4 * PER)
            normalized(NG * 4 - 1, 3)
            add_kron(NG - 1, tiles_of(ENG.DVE, 0, NG - 1, 1)[0])

            dve.wait_ge(f_w, 16 * 10)
            dve.wait_ge(l_ksum, nth(NG - 1, HEAD))
            dve.wait_ge(l_comb, nth(NG - 1, HEAD))
            held = step.done
            PER2 = 17

            def last_norm(out, src, t, i):
                norm_stats(src, f_var)
                return normalize(out, src, f_std, nth(t * 3 + i))

            def last_stage(t):
                att, ksum = at(agg_all, t, MSG, MSG), at(x_all, t, MSG, MSG)
                step(ts(st[:, 10:11], att[:, D:MSG], 1e-30, None, ALU.max))
                step(nc.vector.reciprocal(st[:, 11:12], st[:, 10:11]))
                step(ts(cx, att[:, 0:D], st[:, 11:12], 0.0, ALU.mult, ALU.max))
                stt(out=cat[:, D:2 * D], in0=betak_b[:, :], scalar=ksum[:, D:MSG], in1=ksum[:, 0:D],
                    op0=ALU.mult, op1=ALU.add).then_inc(f_pre, 1)
                dve.wait_ge(f_sig, nth(t))
                step(tt(wa, rz[:, 0:D], ps[:, 2, D:2 * D], ALU.mult))
                tt(wa, wa, ps[:, 2, 0:D], ALU.add).then_inc(f_n0, 1)
                dve.wait_ge(f_tanh, nth(t))
                step(tt(wa, xf, wb, ALU.subtract))
                step(tt(wa, wa, rz[:, D:2 * D], ALU.mult))
                step(tt(wa, wa, wb, ALU.add))
                step(ts(wa, wa, 0.0, None, ALU.max))
                step(last_norm(wb, wa, t, 0))
                step(tt(wb, wb, gln_b, ALU.mult))
                tt(cat[:, 0:D], wb, bln_b, ALU.add).then_inc(f_cat, 1)
                dve.wait_ge(f_lin, nth(t))
                step(last_norm(wa, ps[:, 4, 0:D], t, 1))
                step(tt(wa, wa, gc_b, ALU.mult))
                step(tt(wa, wa, bc_b, ALU.add))
                step(stt(out=wb, in0=wa, scalar=0.0, in1=xf, op0=ALU.max, op1=ALU.add))
                if not is_zero(t):
                    dve.wait_ge(f_st, 16 * t)
                last_norm(outb, wb, t, 2).then_inc(f_out, 1)

            dve.sem_inc(f_out, HEAD)
            step.loop(held, 0, PER2)
            last_stage(0)
            step.loop_ended(held, 1, PER2)
            with dve.Fori(1, NT - 1) as t:
                step.loop(held, t, PER2)
                last_stage(t)
            step.loop_ended(held, NT - 1, PER2)
            last_stage(NT - 1)

        @block.tensor
        def _(pe):
            mm = nc.tensor.matmul

            def turn(out, src):
                return nc.tensor.transpose(out, src, ident[:, :])

            pe.wait_ge(s_const, 1)
            pe.wait_ge(pool_steps, 11)
            pe.wait_ge(s_w0, 16)
            for ic in range(2):
                for oc in range(2):
                    i = 2 * ic + oc
                    ins = turn(ps[:, 7, i * P:(i + 1) * P], tr2[:, oc, ic * P:(ic + 1) * P])
            ins.then_inc(s_w0t, 1)

            pe.sem_inc(s_psum, HEAD)
            for k in range(2):
                pe.wait_ge(s_counted, NB * (k + 1))
                pe.wait_ge(s_map, k)
                mm(ps[:, 4, 0:NB], ones[0:EP, :], cnt[0:EP, :], start=True, stop=True)
                mm(ps[0:EP, 5, 0:NB], before[0:EP, 0:EP], cnt[0:EP, :], start=True, stop=True).then_inc(s_totals, 1)
                pe.wait_ge(s_slots, k)

                def add_product(b, q, first=False, last=False):
                    pe.wait_ge(s_prod, nth(b))
                    for i in range(-(-ET // 512)):
                        n = min(512, ET - 512 * i)
                        ins = mm(ps[0:EP, i, 0:n], ident[0:EP, 0:EP], prod[q][:, i * 512:i * 512 + n],
                                 start=first, stop=last)
                    ins.then_inc(s_psum, 1)

                add_product(k * NB, 0, first=True)
                add_product(k * NB + 1, 1)
                with pe.Fori(1, NB // 2 - 1) as it:
                    for q in range(2):
                        add_product(it * 2 + (k * NB + q), q)
                add_product((k + 1) * NB - 2, 0)
                add_product((k + 1) * NB - 1, 1, last=True)

            pe.wait_ge(s_moved, 1)
            mm(ps[:, 4, 0:1], ones[0:EP, :], moved[0:EP, :], start=True, stop=True).then_inc(s_moved, 1)

            pe.wait_ge(s_flag, 1)
            pe.wait_ge(s_mapld, 32)
            pe.wait_ge(s_x, 32)
            pe.sem_inc(m_oht, HEAD)
            with pe.Fori(0, NG // 4) as it:
                nt = tiles_of(ENG.PE, 0, it * 4, 4)
                for u in range(4):
                    g, q = it * 4 + u, u % 2
                    pe.wait_ge(m_oh, nth(g))
                    for j in range(G):
                        ins = turn(ps[:, q, j * P:(j + 1) * P], oh[:, q, j * P:(j + 1) * P])
                    ins.then_inc(m_oht, 1)
                    pe.wait_ge(m_ohts, nth(g))
                    for j in range(G):
                        pe.wait_ge(m_msg, nth((g - 1) * 4 + j, HEAD))
                        mm(ps[:, 2 + j, 0:D], oh_t[:, q, j * P:(j + 1) * P], at(x_all, nt[u], D, MSG),
                           start=True, stop=True).then_inc(m_x, 1)

            pe.sem_inc(a_sum, HEAD)
            with pe.Fori(0, NG // 4) as it:
                for u in range(4):
                    g, q = it * 4 + u, u % 2
                    pe.wait_ge(a_oh, nth(g))
                    pe.wait_ge(a_add, nth(g - 2, HEAD))
                    for j in range(G):
                        ins = mm(ps[:, q, 0:D], oh[:, q, j * P:(j + 1) * P], msgs[:, u, j, 0:D],
                                 start=(j == 0), stop=(j == G - 1))
                    ins.then_inc(a_sum, 1)

            pe.wait_ge(s_wt, 16 * 17)
            pe.wait_ge(s_wzero, 1)
            pe.wait_ge(act_steps, 1)
            with pe.Fori(0, NT) as t:
                pe.wait_ge(n_agg, nth(t))
                for c in range(2):
                    ins = turn(ps[:, 0, c * P:(c + 1) * P], y_sb[:, c * P:(c + 1) * P])
                ins.then_inc(n_t, 1)
                pe.wait_ge(n_ts, nth(t * 2))
                for c in range(2):
                    ins = mm(ps[:, 2, 0:D], tr2[:, 0, c * P:(c + 1) * P], w0_t[:, c * D:(c + 1) * D],
                             start=(c == 0), stop=(c == 1))
                ins.then_inc(n_lin, 1)
                pe.wait_ge(n_x1, nth(t))
                for c in range(2):
                    ins = turn(ps[:, 1, c * P:(c + 1) * P], x1_sb[:, c * P:(c + 1) * P])
                ins.then_inc(n_t, 1)
                pe.wait_ge(n_ts, nth(t * 2 + 1))
                pe.wait_ge(n_hv, nth(t - 1, HEAD))
                mm(ps[:, 3, 0:ROW], ones[0:1, :], wt_b[:, :], start=True, stop=False)
                for c in range(2):
                    ins = mm(ps[:, 3, 0:ROW], tr2[:, 1, c * P:(c + 1) * P], wt[:, c, :],
                             start=False, stop=(c == 1))
                ins.then_inc(n_tab, 1)

            for s in (k_t, k_h, k_seg):
                pe.sem_inc(s, HEAD)

            def turn_products(tau, j):
                pe.wait_ge(k_kron, nth(tau))
                pe.wait_ge(k_ts, nth(tau - 2, HEAD))
                for c in range(4):
                    ins = turn(ps[0:KC, j % 2, c * P:(c + 1) * P], kron[:, j, c * KC:(c + 1) * KC])
                ins.then_inc(k_t, 1)

            def linear(tau, j):
                pe.wait_ge(k_ts, nth(tau, HEAD))
                pe.wait_ge(k_n, nth(tau - 2, HEAD))
                for c in range(4):
                    ins = mm(ps[:, 2 + j % 2, 0:HC], kron_t[0:KC, j % 2, c * P:(c + 1) * P], wk[0:KC, c, :],
                             start=(c == 0), stop=(c == 3))
                ins.then_inc(k_h, 1)

            def sum_kron(g, u, j):
                pe.wait_ge(k_n, nth(g * 4 + j, HEAD))
                if j == 0:
                    pe.wait_ge(l_ksum, nth(g - 1, HEAD))
                mm(ps[:, 4, 0:MSG], oh[:, u, j * P:(j + 1) * P], clipped[:, j % 2, :],
                   start=(j == 0), stop=(j == G - 1)).then_inc(k_seg, 1)

            def turn_onehot(g, u):
                pe.wait_ge(l_oh, nth(g))
                pe.wait_ge(l_mg, nth(g - 1, HEAD))
                for j in range(G):
                    ins = turn(ps[:, 6, j * P:(j + 1) * P], oh[:, u, j * P:(j + 1) * P])
                ins.then_inc(l_oht, 1)

            def dst_rows(g, q, nt):
                pe.wait_ge(l_ohts, nth(g))
                pe.wait_ge(l_dd, nth(g - 1, HEAD))
                for j in range(G):
                    ins = mm(ps[:, 7, j * (K + 1):(j + 1) * (K + 1)], oh_t[:, q, j * P:(j + 1) * P], node_of(nt),
                             start=True, stop=True)
                ins.then_inc(l_d, 1)

            def turn_logits(g):
                pe.wait_ge(l_ohl, nth(g))
                for j in range(G):
                    ins = turn(ps[:, 6, j * P:(j + 1) * P], ohl[:, j * P:(j + 1) * P])
                ins.then_inc(l_ohlt, 1)

            def edge_max(g, q):
                pe.wait_ge(l_mg, nth(g, HEAD))
                for j in range(G):
                    ins = mm(ps[:, 7, P + j:P + j + 1], oh_t[:, q, j * P:(j + 1) * P], mg[:, q:q + 1],
                             start=True, stop=True)
                ins.then_inc(l_me, 1)

            def context(g, u):
                pe.wait_ge(l_wex, nth(g))
                pe.wait_ge(l_comb, nth(g - 1, HEAD))
                for j in range(G):
                    ins = mm(ps[:, 5, 0:MSG], wex[:, j * P:(j + 1) * P], feat[:, u, j, 0:MSG],
                             start=(j == 0), stop=(j == G - 1))
                ins.then_inc(l_ctx, 1)

            first = tiles_of(ENG.PE, 0, 0, 1)
            pe.wait_ge(n_row, nth(NT - 1, HEAD))
            turn_onehot(0, 0)
            dst_rows(0, 0, first[0])
            turn_logits(0)
            edge_max(0, 0)
            turn_products(0, 0)

            def edge_groups(it):
                nt = tiles_of(ENG.PE, 0, it * 4, 5)
                for u in range(4):
                    g, q, q1 = it * 4 + u, u % 2, 1 - u % 2
                    started = u > 0 or not is_zero(it)
                    turn_products(g * 4 + 1, 1)
                    linear(g * 4, 0)
                    turn_onehot(g + 1, (u + 1) % 4)
                    if started:
                        sum_kron(g - 1, (u + 3) % 4, 2)

                    turn_products(g * 4 + 2, 2)
                    context(g, u)
                    dst_rows(g + 1, q1, nt[u + 1])
                    linear(g * 4 + 1, 1)
                    if started:
                        sum_kron(g - 1, (u + 3) % 4, 3)

                    turn_products(g * 4 + 3, 3)
                    turn_logits(g + 1)
                    linear(g * 4 + 2, 2)
                    sum_kron(g, u, 0)

                    turn_products(g * 4 + 4, 0)
                    edge_max(g + 1, q1)
                    linear(g * 4 + 3, 3)
                    sum_kron(g, u, 1)

            edge_groups(0)
            with pe.Fori(1, NG // 4) as it:
                edge_groups(it)
            sum_kron(NG - 1, 3, 2)
            sum_kron(NG - 1, 3, 3)

            pe.wait_ge(f_w, 16 * 10)
            pe.wait_ge(l_comb, nth(NG - 1, HEAD))
            for b in range(6):
                for r in range(4):
                    c, o = divmod((b % 3) * 4 + r, 6)
                    ins = turn(ps[:, b, r * P:(r + 1) * P], raw_w[:, 6 * (b // 3) + o, c * P:(c + 1) * P])
                ins.then_inc(f_wp, 1)
            pe.wait_ge(f_ws, 6)

            def gates(out, lo, n, parts):
                both = ((bih_r, wih_t, 0), (bhh_r, whh_t, 2))
                both = [both[i] for i in parts]
                first = True
                for b, _, _ in both:
                    mm(out, ones[0:1, :], b[0:1, lo:lo + n], start=first, stop=False)
                    first = False
                for i, (_, w, x) in enumerate(both):
                    for c in range(2):
                        ins = mm(out, tr4[:, (x + c) * P:(x + c + 1) * P], w[:, c * 3 * D + lo:c * 3 * D + lo + n],
                                 start=False, stop=(i == len(both) - 1 and c == 1))
                return ins

            def last_products(t):
                pe.wait_ge(f_pre, nth(t))
                pe.wait_ge(f_x, 16 * (t + 1))
                for c in range(2):
                    turn(ps[:, 0, c * P:(c + 1) * P], cx[:, c * P:(c + 1) * P])
                for c in range(2):
                    ins = turn(ps[:, 0, (2 + c) * P:(3 + c) * P], xf[:, c * P:(c + 1) * P])
                ins.then_inc(f_t, 1)
                pe.wait_ge(f_ts, nth(t))
                gates(ps[:, 1, :], 0, 2 * D, (0, 1))
                gates(ps[:, 2, 0:D], 2 * D, D, (0,))
                gates(ps[:, 2, D:2 * D], 2 * D, D, (1,)).then_inc(f_gate, 1)
                pe.wait_ge(f_cat, nth(t))
                for c in range(4):
                    ins = turn(ps[:, 3, c * P:(c + 1) * P], cat[:, c * P:(c + 1) * P])
                ins.then_inc(f_ct, 1)
                pe.wait_ge(f_cts, nth(t))
                mm(ps[:, 4, 0:D], ones[0:1, :], bcr_r[0:1, :], start=True, stop=False)
                for c in range(4):
                    ins = mm(ps[:, 4, 0:D], cat_t[:, c * P:(c + 1) * P], wc[:, c, :], start=False, stop=(c == 3))
                ins.then_inc(f_lin, 1)

            with pe.Fori(0, NT - 1) as t:
                last_products(t)
            last_products(NT - 1)


INPUTS = ["x", "src", "dst", "edge_weight", "L0_gnn_W"] + ["L1_gnn_" + n for n in (
    "Wp", "bp", "gp", "betap", "Wk", "bk", "gk", "betak", "We", "be", "Wn", "bn", "W_ih", "W_hh", "b_ih", "b_hh",
    "g_ln", "beta_ln", "Wc", "bc", "gc", "betac")]


def kernel(**inputs):
    import numpy as _np
    import concourse.bacc as _bacc
    from concourse import mybir as _mybir
    from concourse.bass_utils import run_bass_kernel_spmd as _run

    nc = _bacc.Bacc("TRN2", target_bir_lowering=False, num_devices=1)
    arrays, io = {}, {}
    for name in INPUTS:
        a = _np.ascontiguousarray(inputs[name])
        arrays["in_" + name] = a
        io[name] = nc.dram_tensor("in_" + name, a.shape, _mybir.dt.from_np(a.dtype), kind="ExternalInput").ap()
    V, E = inputs["x"].shape[0], inputs["src"].shape[0]
    io["out"] = nc.dram_tensor("out", (V, D), F32, kind="ExternalOutput").ap()
    gnn_program(nc, io, V, E, 125)
    r = _run(nc, [arrays], core_ids=[0])
    return r.results[0]["out"]
```

```python
from contextlib import ExitStack

import concourse.bass as bass
from concourse import mybir

P = 128
D = 256
K = 20
G = 4
GE = G * P
EPS = 1e-5
FAR = 1 << 24

ROW = D + 1 + K + 1
MSG = D + 1
KC = 101
RC = D + 2
HC = D + 1

ALU = mybir.AluOpType
ACT = mybir.ActivationFunctionType
AX_X = mybir.AxisListType.X
F32 = mybir.dt.float32
F32R = mybir.dt.float32r
I32 = mybir.dt.int32
U32 = mybir.dt.uint32
U8 = mybir.dt.uint8
ENG = mybir.EngineType


class Chain:

    def __init__(self, eng, sem):
        self.eng, self.sem, self.done, self.taken = eng, sem, 0, 0

    def __call__(self, ins):
        ins.then_inc(self.sem, 1)
        self.done = self.done + 1
        self.taken += 1
        self.eng.wait_ge(self.sem, self.done)

    def loop(self, start, i, per):
        self.done, self.taken = start + i * per, 0

    def loop_ended(self, start, n, per):
        assert self.taken == per, (self.taken, per)
        self.done = start + n * per


def at(a, i, n=1, step=1):
    if isinstance(i, int):
        return a[:, i * step:i * step + n]
    return a[:, bass.ds(i * step, n)]


def is_zero(i):
    return isinstance(i, int) and i == 0


def rows(a, i, n=P):
    return a[i * P:i * P + n, :] if isinstance(i, int) else a[bass.ds(i * P, n), :]


def gnn_program(nc, io, V, E, EP):
    NT = -(-V // P)
    VL = V - (NT - 1) * P
    NB = NT + NT % 2
    ET = E // EP
    NG = -(-((E + (GE - 1) * NT) // GE) // 4) * 4
    NX = NG + 4
    GP = NX // 4
    SC = 16
    SL = ET // SC
    NA = NT * MSG
    MASKW = -(-NB * ET // 4)
    SPARE = max(MASKW, NA + G * MSG)
    assert E == EP * ET and ET == SL * SC and GP <= P and EP <= P and NB <= P

    with ExitStack() as ctx:
        def sb(name, shape, dt=F32):
            return ctx.enter_context(nc.sbuf_tensor(name, shape, dt))

        def sem(name):
            return ctx.enter_context(nc.semaphore(name))

        rec_dram = nc.dram_tensor("rec_dram", [E + GE, 4], F32).ap()
        msg_dram = nc.dram_tensor("msg_dram", [E + GE, MSG], F32).ap()
        tab_dram = nc.dram_tensor("tab_dram", [NT * P, ROW], F32).ap()
        x1_dram = nc.dram_tensor("x1_dram", [NT * P, D], F32).ap()
        map_dram = nc.dram_tensor("map_dram", [4, NX], I32).ap()
        left_dram = nc.dram_tensor("left_dram", [2, NX], F32).ap()

        ps = ctx.enter_context(nc.psum_tensor("ps", [P, 8, 512], F32))

        arena_n = sb("arena_n", [P, max(2 * NA, SPARE + P + 14 * NB + 1 + 6 * SC)])
        arena_r = sb("arena_r", [P, max(6 * ET, NX * 16 + 3 * GE + 2 * G * (K + 1), 7200)])
        arena_e = sb("arena_e", [P, max(6 * ET, 8200 + NT * (K + 1))])

        def cutter(arena):
            used = [0]

            def cut(*shape):
                n = 1
                for s in shape:
                    n *= s
                v = arena[:, used[0]:used[0] + n]
                used[0] += n
                if len(shape) == 2:
                    v = v.rearrange("p (a b) -> p a b", a=shape[0])
                if len(shape) == 3:
                    v = v.rearrange("p (a b c) -> p a b c", a=shape[0], b=shape[1])
                return v
            return cut

        x_all, agg_all = arena_n[:, 0:NA], arena_n[:, NA:2 * NA]
        mask8 = arena_n[0:EP, 0:MASKW].bitcast(U8)
        before = arena_n[:, SPARE:SPARE + P]
        cmp = arena_n[:, SPARE + P:SPARE + P + 4 * NB].rearrange("p (a b) -> p a b", a=4)
        weighed = arena_n[:, SPARE + P + 4 * NB:SPARE + P + 8 * NB].rearrange("p (a b) -> p a b", a=4)
        tail = agg_all[:, 0:G * MSG]
        c = cutter(arena_n[:, SPARE + P + 8 * NB:])
        stage, sidx_f, sidx = c(4 * SC), c(SC)[0:EP], c(SC).bitcast(I32)
        gsz, gend, short, total, gsz_i = c(NB), c(NB), c(NB), c(NB + 1), c(2, NB).bitcast(I32)
        c = cutter(arena_r)
        bk_i, bk_f = c(ET)[0:EP].bitcast(I32), c(ET)[0:EP]
        scan, prod = [c(ET)[0:EP] for _ in range(2)], [c(ET)[0:EP] for _ in range(2)]
        recs = arena_r[0:EP, 0:4 * ET]
        place, slot_f = prod
        c = cutter(arena_r)
        rec_all, oh_t, ohl = c(NX * 16), c(2, GE), c(GE)
        dsb = c(2, G * (K + 1)).rearrange("p q (j k) -> p q j k", j=G)
        c = cutter(arena_r)
        raw_w, wih_t, wc = c(12, D), c(2 * 3 * D), c(4, D)
        whh_t = c(2 * 3 * D)
        c = cutter(arena_e)
        dst_i, src_i = c(ET)[0:EP].bitcast(I32), c(ET)[0:EP].bitcast(I32)
        w_f, dloc = c(ET)[0:EP], c(ET)[0:EP]
        slot = [c(ET)[0:EP].bitcast(I32), c(ET)[0:EP]]
        c = cutter(arena_e)
        msgs = c(4, G, MSG)
        row_of = c(2, NX)[0:1].bitcast(I32)
        left = c(2, NX)
        w0_t, wt, tr2, row = c(2 * D), c(2, ROW), c(2, D), c(ROW)
        c = cutter(arena_e)
        feat, kron, kron_t = c(4, G, ROW), c(G, 4 * KC), c(2, 4 * P)
        normed, clipped = c(2, D), c(2, MSG)
        node = c(NT * (K + 1))
        c = cutter(arena_e)
        gln_b, bln_b, gc_b, bc_b, cx, wa, wb, ya, yb, outb = [c(D) for _ in range(10)]
        xf, xr = [[c(D) for _ in range(2)] for _ in range(2)]
        cat, tr4, cat_t, rz, bih_r, bhh_r, bcr_r = c(2 * D), c(4 * P), c(4 * P), c(2 * D), c(3 * D), c(3 * D), c(D)

        ident = sb("ident", [P, P])
        ones = sb("ones", [P, P])
        iota = sb("iota", [P, P])
        gidx = sb("gidx", [P, 4])
        minus_half = sb("minus_half", [P, 1])
        eps_c = sb("eps_c", [P, 1])
        eps_root = sb("eps_root", [1, 1])
        gate = sb("gate", [P, 6])
        cnt, base = sb("cnt", [P, NB]), sb("base", [P, NB])
        tmap_f = sb("tmap_f", [P, 4])
        tmap_i = sb("tmap_i", [P, 4, 4], I32)
        left_f = sb("left_f", [P, 2, 4])
        slot128 = sb("slot128", [P, G])
        moved = sb("moved", [P, 1])
        moved_i = sb("moved_i", [1, 1], I32)
        far = sb("far", [P, G])
        tile_of = sb("tile_of", [1, 2, NX], I32)
        recq = sb("recq", [P, 4, 16])
        oh_r = sb("oh_r", [P, 4, GE], F32R)
        oh = oh_r[:, :, :].bitcast(F32)
        idxq = sb("idxq", [P, 4, G], I32)
        sloc_i = sb("sloc_i", [P, G], I32)
        wk = sb("wk", [P, 4, HC])
        wt_b = sb("wt_b", [1, ROW])
        chi, clo = sb("chi", [P, 2, RC], F32R), sb("clo", [P, 2, D], F32R)
        whi, wlo = sb("whi", [P, 2, RC], F32R), sb("wlo", [P, 2, RC], F32R)
        gk_b, betak_b, nbetak_b = (sb(n, [P, D]) for n in ("gk_b", "betak_b", "nbetak_b"))
        gp_b, betap_b = sb("gp_b", [P, K]), sb("betap_b", [P, K])
        st = sb("st", [P, 16])
        junk = sb("junk", [P, 2, HC])
        y_sb, x1_sb = junk[:, 0, 0:D], junk[:, 1, 0:D]
        lg = sb("lg", [P, 2, G])
        valid = sb("valid", [P, G])
        mg = sb("mg", [P, 2])
        mnew = sb("mnew", [P, 1])
        mrun = sb("mrun", [P, NT])
        edd = sb("edd", [P, 2, 8])
        ee = sb("ee", [P, 2, 8])
        var = sb("var", [P, G])
        rstd = sb("rstd", [P, G])

        s_in, s_wt, s_w0, s_x = sem("edges_loaded"), sem("weights_loaded"), sem("w0_loaded"), sem("x_loaded")
        pool_steps, dve_steps, act_steps = sem("pool_steps"), sem("dve_steps"), sem("act_steps")
        s_const, s_wzero = sem("constants_ready"), sem("weights_cleared")
        s_counted, s_totals = sem("buckets_counted"), sem("bucket_totals_ready")
        s_prod, s_psum = sem("slot_product_ready"), sem("slot_product_added")
        s_map, s_mapst, s_mapld = sem("tile_map_ready"), sem("tile_map_stored"), sem("tile_map_loaded")
        s_slots, s_xclr = sem("slots_ready"), sem("x_tail_cleared")
        s_place, s_packed, s_moved, s_flag = (sem(n) for n in (
            "places_ready", "records_packed", "moved_edges_counted", "moved_edges_known"))
        s_recst, s_stage, s_scat, s_order = (sem(n) for n in (
            "records_stored", "records_staged", "records_scattered", "records_in_order"))
        s_tail, s_tailst = sem("tail_ready"), sem("tail_stored")
        s_rowld, s_recs = sem("rows_and_left_loaded"), sem("records_loaded")
        s_w0t = sem("w0_turned")
        m_oh, m_oht, m_ohts, m_x, m_msg, m_loc = (sem("m_" + n) for n in (
            "onehot", "onehot_t", "onehot_t_sbuf", "rows", "messages", "slots_and_locals"))
        m_gate = sem("m_scatter_gate")
        m_out = [sem(f"m_scattered{q}") for q in range(4)]
        a_in = [sem(f"a_messages_loaded{q}") for q in range(4)]
        a_oh, a_sum, a_add = sem("a_onehot"), sem("a_summed"), sem("a_added")
        n_agg = sem("n_aggregate")
        n_t, n_ts, n_lin, n_var, n_std, n_x1, n_tab, n_hv, n_row, n_st = (sem("n_" + n) for n in (
            "turned", "turned_sbuf", "linear", "variance", "deviation", "x1", "table", "values", "row", "stored"))
        l_rec, l_oh, l_oht, l_ohts, l_d = (sem("l_" + n) for n in (
            "records", "onehot", "onehot_t", "onehot_t_sbuf", "dst_rows"))
        l_feat = [sem(f"l_rows_gathered{q}") for q in range(4)]
        l_hi, l_lo, k_hi, k_lo = (sem(n) for n in (
            "l_weighted_high", "l_weighted_low", "k_clipped_high", "k_clipped_low"))
        l_ohl, l_ohlt, l_mg, l_me, l_dd, l_ex, l_ctx, l_comb, l_ksum = (sem("l_" + n) for n in (
            "logits", "logits_t", "group_max", "edge_max", "differences", "exponentials",
            "context", "context_added", "kron_added"))
        k_kron, k_t, k_ts, k_h, k_sq, k_rs, k_n, k_seg = (sem("k_" + n) for n in (
            "products", "turned", "turned_sbuf", "linear", "variance", "rstd", "normed", "summed"))
        f_w, f_wp, f_ws, f_x, f_pre, f_t, f_ts, f_gate, f_sig, f_n0, f_tanh = (sem("f_" + n) for n in (
            "weights_loaded", "weights_turned", "weights_turned_sbuf", "x1_loaded", "context", "turned",
            "turned_sbuf", "gates", "sigmoid", "candidate", "tanh"))
        f_var2, f_std2 = sem("f_last_variances"), sem("f_last_deviations")
        f_var, f_std, f_cat, f_ct, f_cts, f_lin, f_out, f_st = (sem("f_" + n) for n in (
            "variance", "deviation", "features", "features_t", "features_t_sbuf", "linear", "result", "stored"))

        def nth(i, head=0):
            return i + 1 + head

        HEAD = 4

        def last_loop(engine, body, before=None, after=None):
            pairs = (NT - 3) // 2
            body(0, 0)
            if before:
                before()
            with engine.Fori(0, pairs) as it:
                if before:
                    before(it)
                for q in range(2):
                    body(it * 2 + (1 + q), 1 - q)
            if after:
                after(pairs)
            for t in range(1 + 2 * pairs, NT):
                body(t, t % 2)

        def is_tile(t):
            return not isinstance(t, int) or 0 <= t < NT

        def tiles_of(engine, order, g, n):
            _, v = nc.values_load_multi_w_load_instructions(
                tile_of[0:1, order, bass.ds(g, n)], engines=[engine], min_val=0, max_val=NT - 1,
                skip_runtime_bounds_check_because="the map is clamped to the last tile")
            return v

        def first_rows(order, g, n):
            _, v = nc.values_load_multi_w_load_instructions(
                row_of[0:1, order, bass.ds(g, n)], engines=[ENG.SP], min_val=0, max_val=E,
                skip_runtime_bounds_check_because="the rows are clamped to the edges' number")
            return v

        def rec(u):
            return recq[:, u, :].rearrange("p (j f) -> p j f", f=4)

        def over_nodes(a):
            return a.unsqueeze(2).broadcast_to([P, G, P])

        iota_g = iota[:, :].unsqueeze(1).broadcast_to([P, G, P])

        def grouped(a):
            return a.rearrange("p (j n) -> p j n", j=G)

        def node_of(t, n=K + 1):
            return at(node, t, n, K + 1)

        block = ctx.enter_context(nc.Block())

        @block.sync
        def _(sp):
            sp.dma_start(dst_i, io["dst"].rearrange("(p t) -> p t", p=EP)).then_inc(s_in, 16)
            sp.dma_start(src_i, io["src"].rearrange("(p t) -> p t", p=EP)).then_inc(s_in, 16)
            sp.dma_start(w_f, io["edge_weight"].rearrange("(p t) -> p t", p=EP)).then_inc(s_in, 16)
            for k in range(2):
                sp.wait_ge(s_map, k + 1)
                for i in range(2):
                    sp.dma_start(map_dram[2 * k + i].rearrange("(c p) -> p c", c=4), tmap_i[0:GP, 2 * k + i, :],
                                 allow_slow_non_contiguous=True).then_inc(s_mapst, 16)
                sp.dma_start(left_dram[k].rearrange("(c p) -> p c", c=4), left_f[0:GP, k, :],
                             allow_slow_non_contiguous=True).then_inc(s_mapst, 16)
                sp.wait_ge(s_mapst, 48 * (k + 1))
                sp.dma_start(tile_of[0:1, k, :], map_dram[2 * k:2 * k + 1, :]).then_inc(s_mapld, 16)
            sp.wait_ge(s_tail, 1)
            sp.dma_start(rec_dram[E:E + GE, :].rearrange("(p j) c -> p (j c)", p=P), tail[:, 0:G * 4]).then_inc(s_tailst, 16)
            sp.dma_start(msg_dram[E:E + GE, :].rearrange("(p j) c -> p (j c)", p=P), tail).then_inc(s_tailst, 16)
            sp.wait_ge(s_packed, 4)
            sp.dma_start(rec_dram[0:E, :].rearrange("(p t) f -> p (t f)", p=EP), recs).then_inc(s_recst, 16)
            xv = x_all.rearrange("p (t c) -> p t c", c=MSG)
            sp.dma_start(xv[:, 0:NT - 1, 0:D],
                         io["x"][0:(NT - 1) * P, :].rearrange("(t p) d -> p t d", p=P)).then_inc(s_x, 16)
            sp.wait_ge(s_xclr, 1)
            sp.dma_start(xv[0:VL, NT - 1, 0:D], io["x"][(NT - 1) * P:V, :]).then_inc(s_x, 16)
            sp.wait_ge(s_order, 1)
            sp.wait_ge(s_tailst, 32)
            for k in range(2):
                sp.dma_start(row_of[:, k, :], map_dram[2 * k + 1:2 * k + 2, :]).then_inc(s_rowld, 16)
                sp.dma_start(left[:, k, :], left_dram[k].partition_broadcast(P)).then_inc(s_rowld, 16)
            sp.wait_ge(s_rowld, 64)
            sp.sem_inc(s_recs, HEAD)
            with sp.Fori(0, GP) as it:
                start = first_rows(0, it * 4, 4)
                sp.wait_ge(s_recs, 64 * it + HEAD)
                for u in range(4):
                    sp.dma_start(at(rec_all, it * 4 + u, 16, 16),
                                 rec_dram[bass.ds(start[u], GE), :].rearrange("(p j) f -> p (j f)", p=P)
                                 ).then_inc(s_recs, 16)
            for u in range(4):
                sp.wait_ge(m_out[u], 16 * G * (NG // 4))

            def load_messages(g, start, u):
                sp.wait_ge(a_sum, nth(g - 4, HEAD))
                sp.dma_start(msgs[:, u].rearrange("p j c -> p (j c)"),
                             msg_dram[bass.ds(start, GE), :].rearrange("(p j) c -> p (j c)", p=P)).then_inc(a_in[u], 16)

            with sp.Fori(0, NG // 4) as it:
                start = first_rows(1, it * 4, 4)
                for u in range(4):
                    load_messages(it * 4 + u, start[u], u)
            load_messages(NG, first_rows(1, NG, 1)[0], 0)
            with sp.Fori(0, NT) as t:
                sp.wait_ge(n_x1, t + 1)
                sp.dma_start(rows(x1_dram, t), x1_sb[:, :]).then_inc(n_st, 16)
                sp.wait_ge(n_row, nth(t, HEAD))
                sp.wait_ge(n_hv, nth(t, HEAD))
                sp.dma_start(rows(tab_dram, t), row).then_inc(n_st, 16)
            sp.wait_ge(l_ksum, nth(NG - 1, HEAD))
            sp.wait_ge(l_comb, nth(NG - 1, HEAD))
            sp.wait_ge(k_kron, nth(4 * NG + 1))
            sp.wait_ge(k_ts, nth(4 * NG, HEAD))
            sp.wait_ge(k_seg, nth(4 * NG - 1, HEAD))
            for u in range(4):
                sp.wait_ge(l_feat[u], 16 * G * (NG // 4 + (u < 3)))
            sp.dma_start(raw_w[:, 0:6, :], io["L1_gnn_W_ih"].rearrange("(a p) d -> p a d", p=P)).then_inc(f_w, 16)
            sp.dma_start(raw_w[:, 6:12, :], io["L1_gnn_W_hh"].rearrange("(a p) d -> p a d", p=P)).then_inc(f_w, 16)
            sp.dma_start(wc, io["L1_gnn_Wc"].rearrange("(a p) d -> p a d", p=P)).then_inc(f_w, 16)
            for dst, name in ((gln_b, "g_ln"), (bln_b, "beta_ln"), (gc_b, "gc"), (bc_b, "betac")):
                sp.dma_start(dst, io["L1_gnn_" + name].partition_broadcast(P)).then_inc(f_w, 16)
            for dst, name in ((bih_r, "b_ih"), (bhh_r, "b_hh"), (bcr_r, "bc")):
                sp.dma_start(dst[0:1, :], io["L1_gnn_" + name].unsqueeze(0)).then_inc(f_w, 16)

            def load_x1(t, q):
                sp.dma_start(xf[q], rows(x1_dram, t)).then_inc(f_x, 16)

            def store(t, n=P):
                sp.wait_ge(f_out, nth(t))
                sp.dma_start(rows(io["out"], t, n), outb[0:n, :]).then_inc(f_st, 16)

            load_x1(0, 0)
            sp.wait_ge(f_x, 16)
            load_x1(1, 1)

            def transfers(t, q):
                if is_tile(t + 2):
                    sp.wait_ge(f_cat, nth(t))
                    sp.wait_ge(f_x, 16 * (t + 2))
                    load_x1(t + 2, q)
                if is_tile(t - 1):
                    store(t - 1)

            last_loop(sp, transfers)
            store(NT - 1, VL)
            sp.wait_ge(f_st, 16 * NT)

        @block.gpsimd
        def _(pool):
            step = Chain(pool, pool_steps)
            step(nc.gpsimd.memset(ident[:, :], 0.0))
            step(nc.gpsimd.affine_select(out=ident[:, :], in_=ident[:, :], compare_op=ALU.not_equal, fill=1.0,
                                         base=0, pattern=[[-1, P]], channel_multiplier=1))
            step(nc.gpsimd.memset(before, 1.0))
            step(nc.gpsimd.affine_select(out=before, in_=before, compare_op=ALU.is_gt, fill=0.0,
                                         base=0, pattern=[[1, P]], channel_multiplier=-1))
            step(nc.gpsimd.iota(iota[:, :], [[1, P]], base=0, channel_multiplier=0,
                                allow_small_or_imprecise_dtypes=True))
            step(nc.gpsimd.iota(gidx[0:GP, :], [[GP, 4]], base=0, channel_multiplier=1,
                                allow_small_or_imprecise_dtypes=True))
            step(nc.gpsimd.iota(slot128[:, :], [[P, G]], base=P, channel_multiplier=G * P,
                                allow_small_or_imprecise_dtypes=True))
            step(nc.gpsimd.memset(minus_half[:, :], -0.5))
            step(nc.gpsimd.memset(eps_c[:, :], EPS))
            step(nc.gpsimd.memset(eps_root[:, :], 16.0 * EPS ** 0.5))
            step(nc.gpsimd.memset(ones[:, :], 1.0))
            nc.gpsimd.memset(gate[:, :], 0.0).then_inc(s_const, 1)
            pool.sem_inc(m_gate, HEAD)
            pool.wait_ge(s_slots, 2)
            nc.gpsimd.iota(place, [[1, ET]], base=0, channel_multiplier=ET,
                           allow_small_or_imprecise_dtypes=True).then_inc(s_place, 1)
            pool.wait_ge(s_flag, 1)
            pool.wait_ge(s_recst, 16)
            pool.wait_ge(s_packed, 4)
            with pool.If(nc.values_load(moved_i[0:1, 0:1], engines=[ENG.Pool], min_val=0, max_val=E,
                                        skip_runtime_bounds_check_because="a count of edges") > 0):
                with pool.Fori(0, SL) as it:
                    nc.gpsimd.tensor_tensor(stage[0:EP, 0:4 * SC], at(recs, it, 4 * SC, 4 * SC), ones[0:EP, 0:4 * SC],
                                            ALU.mult).then_inc(s_stage, 1)
                    nc.gpsimd.tensor_tensor(sidx_f, at(slot_f, it, SC, SC), ones[0:EP, 0:SC],
                                            ALU.mult).then_inc(s_stage, 1)
                    pool.wait_ge(s_stage, 5 * it + 2)
                    nc.gpsimd.tensor_tensor(gate[:, 4:5], ones[:, 0:1], ones[:, 1:2], ALU.mult).then_inc(s_stage, 1)
                    nc.gpsimd.tensor_copy(sidx[0:EP, :], sidx_f).then_inc(s_stage, 1)
                    pool.wait_ge(s_stage, 5 * it + 4)
                    nc.gpsimd.tensor_tensor(gate[:, 5:6], ones[:, 0:1], ones[:, 1:2], ALU.mult).then_inc(s_stage, 1)
                    for i in range(SC):
                        nc.gpsimd.indirect_dma_start(
                            out=rec_dram, in_=stage[0:EP, 4 * i:4 * i + 4], in_offset=None,
                            out_offset=bass.IndirectOffsetOnAxis(ap=sidx[0:EP, i:i + 1].bitcast(U32), axis=0),
                        ).then_inc(s_scat, 16)
                    pool.wait_ge(s_scat, 16 * SC * (it + 1))
            pool.sem_inc(s_order, 1)
            with pool.Fori(0, NG // 4) as it:
                for u in range(4):
                    pool.wait_ge(m_loc, nth(it * 4 + u))
                    pool.wait_ge(m_msg, nth((it * 4 + u) * 4 + 3, HEAD))
                    nc.gpsimd.tensor_tensor(gate[:, u:u + 1], ones[:, 0:1], ones[:, 1:2], ALU.mult).then_inc(m_gate, 1)
                    for j in range(G):
                        nc.gpsimd.indirect_dma_start(
                            out=msg_dram, in_=msgs[:, u, j, :], in_offset=None,
                            out_offset=bass.IndirectOffsetOnAxis(ap=idxq[:, u, j:j + 1].bitcast(U32), axis=0),
                            bounds_check=E - 1, oob_is_err=False,
                        ).then_inc(m_out[u], 16)

            def gather(u, j):
                nc.gpsimd.indirect_dma_start(
                    out=feat[:, u, j, :], out_offset=None, in_=tab_dram,
                    in_offset=bass.IndirectOffsetOnAxis(ap=idxq[:, u, j:j + 1].bitcast(U32), axis=0),
                ).then_inc(l_feat[u], 16)

            pool.wait_ge(n_st, 32 * NT)
            pool.wait_ge(l_rec, 3)
            for u in range(3):
                for j in range(G):
                    gather(u, j)

            def edge_rows(it):
                for u in range(4):
                    g = it * 4 + u
                    pool.wait_ge(l_rec, nth(g + 3))
                    for j in range(G):
                        pool.wait_ge(k_sq, nth(g * 4 + j, HEAD))
                        nc.gpsimd.tensor_tensor(rstd[:, j:j + 1], var[:, j:j + 1], minus_half[:, :],
                                                ALU.pow).then_inc(k_rs, 1)
                        gather((u + 3) % 4, j)

            with pool.Fori(0, NG // 4) as it:
                edge_rows(it)

        @block.scalar
        def _(act):
            step = Chain(act, act_steps)
            act.wait_ge(s_wzero, 1)
            L1 = "L1_gnn_"
            for c in range(3):
                act.dma_start(wk[0:KC, c, 0:D], io[L1 + "Wk"][c * KC:(c + 1) * KC, :]).then_inc(s_wt, 16)
            last = K * K - 3 * KC
            act.dma_start(wk[0:last, 3, 0:D], io[L1 + "Wk"][3 * KC:K * K, :]).then_inc(s_wt, 16)
            act.dma_start(wk[last:last + 1, 3, 0:D], io[L1 + "bk"].unsqueeze(0)).then_inc(s_wt, 16)
            act.wait_ge(s_const, 1)
            act.dma_start(wk[last:last + 1, 3, D:D + 1], eps_root[:, :]).then_inc(s_wt, 16)
            act.dma_start(wt_b[:, 0:D], io[L1 + "bn"].unsqueeze(0)).then_inc(s_wt, 16)
            act.dma_start(wt_b[:, D:D + 1], io[L1 + "be"].unsqueeze(0)).then_inc(s_wt, 16)
            act.dma_start(wt_b[:, D + 1:D + 1 + K], io[L1 + "bp"].unsqueeze(0)).then_inc(s_wt, 16)
            for dst, name in ((gk_b, "gk"), (betak_b, "betak"), (gp_b, "gp"), (betap_b, "betap")):
                act.dma_start(dst[:, :], io[L1 + name].partition_broadcast(P)).then_inc(s_wt, 16)
            act.wait_ge(s_order, 1)
            with nc.allow_non_contiguous_dma("columns of weights"):
                act.dma_start(wt[:, :, 0:D], io[L1 + "Wn"].rearrange("(c p) d -> p c d", p=P)).then_inc(s_wt, 16)
                act.dma_start(wt[:, :, D:D + 1], io[L1 + "We"][0:D, :].rearrange("(c p) d -> p c d", p=P)).then_inc(s_wt, 16)
                act.dma_start(wt[:, :, D + 1:D + 1 + K], io[L1 + "Wp"].rearrange("(c p) d -> p c d", p=P)).then_inc(s_wt, 16)
                act.dma_start(wt[:, :, ROW - 1:ROW], io[L1 + "We"][D:2 * D, :].rearrange("(c p) d -> p c d", p=P)).then_inc(s_wt, 16)
            act.dma_start(tr2, io["L0_gnn_W"].rearrange("(c p) d -> p c d", p=P)).then_inc(s_w0, 16)
            act.wait_ge(s_w0t, 1)
            step(nc.scalar.activation(w0_t, ps[:, 7, :], ACT.Copy))

            act.sem_inc(m_msg, HEAD)

            def weigh(it):
                for u in range(4):
                    g, q = it * 4 + u, u % 2
                    act.wait_ge(m_oht, nth(g, HEAD))
                    nc.scalar.activation(oh_t[:, q, :], ps[:, q, :], ACT.Copy).then_inc(m_ohts, 1)
                    if not is_zero(it):
                        act.wait_ge(m_out[u], 16 * G * it)
                    for j in range(G):
                        act.wait_ge(m_x, nth(g * 4 + j))
                        nc.scalar.activation(msgs[:, u, j, 0:D], ps[:, 2 + j, 0:D], ACT.Copy,
                                             scale=recq[:, u, 4 * j + 2:4 * j + 3]).then_inc(m_msg, 1)

            weigh(0)
            with act.Fori(1, NG // 4) as it:
                weigh(it)

            def node_functions(t):
                for h in range(2):
                    act.wait_ge(n_t, nth(t * 2 + h))
                    nc.scalar.activation(tr2[:, h, :], ps[:, h, 0:D], ACT.Copy).then_inc(n_ts, 1)
                    if h == 0:
                        act.wait_ge(n_var, nth(t * 2))
                        nc.scalar.activation(st[:, 8:9], st[:, 7:8], ACT.Sqrt, bias=eps_c[:, :]).then_inc(n_std, 1)
                act.wait_ge(n_tab, nth(t))
                if not is_zero(t):
                    act.wait_ge(n_st, 32 * t)
                nc.scalar.activation(row, ps[:, 3, 0:ROW], ACT.Copy).then_inc(n_hv, 1)
                act.wait_ge(n_var, nth(t * 2 + 1))
                nc.scalar.activation(st[:, 8:9], st[:, 7:8], ACT.Sqrt, bias=eps_c[:, :]).then_inc(n_std, 1)

            act.sem_inc(n_hv, HEAD)
            node_functions(0)
            with act.Fori(1, NT) as t:
                node_functions(t)

            act.sem_inc(k_ts, HEAD)
            act.sem_inc(k_sq, HEAD)

            def evacuate(tau, b):
                act.wait_ge(k_t, nth(tau, HEAD))
                act.wait_ge(k_h, nth(tau - 2, HEAD))
                nc.scalar.activation(kron_t[0:KC, b, :], ps[0:KC, b, :], ACT.Copy).then_inc(k_ts, 1)

            def square(tau, j):
                act.wait_ge(k_h, nth(tau, HEAD))
                act.wait_ge(k_sq, nth(tau - 2, HEAD))
                nc.scalar.activation(junk[:, j % 2, :], ps[:, 2 + j % 2, 0:HC], ACT.Square, scale=1.0 / 16,
                                     accum_out=var[:, j:j + 1]).then_inc(k_sq, 1)

            def evacuate_onehot(g, q):
                act.wait_ge(l_oht, nth(g))
                nc.scalar.activation(oh_t[:, q, :], ps[:, 6, :], ACT.Copy).then_inc(l_ohts, 1)

            def exponentials(g, q):
                act.wait_ge(l_dd, nth(g, HEAD))
                nc.scalar.activation(ee[:, q, 0:6], edd[:, q, 0:6], ACT.Exp).then_inc(l_ex, 1)

            def clipped_high(tau, j):
                act.wait_ge(k_n, nth(tau, HEAD))
                act.wait_ge(k_seg, nth(tau - 2, HEAD))
                nc.scalar.activation(chi[:, j % 2, 0:D], clipped[:, j % 2, 0:D], ACT.Copy).then_inc(k_hi, 1)

            def weighted_high(g, u, q, j):
                act.wait_ge(l_ex, nth(g))
                act.wait_ge(l_ctx, nth(g * 4 + j - 2, HEAD))
                nc.scalar.activation(whi[:, j % 2, :], feat[:, u, j, 0:RC], ACT.Copy,
                                     scale=ee[:, q, j:j + 1]).then_inc(l_hi, 1)

            def edge_functions(it):
                for u in range(4):
                    g, q = it * 4 + u, u % 2
                    for j in range(G):
                        if j == 1:
                            evacuate_onehot(g + 1, 1 - q)
                        if not (is_zero(it) and u == 0 and j < 2):
                            clipped_high(g * 4 + (j - 2), j)
                        evacuate(g * 4 + j + 1, (j + 1) % 2)
                        square(g * 4 + j, j)
                        weighted_high(g, u, q, j)
                    exponentials(g + 1, 1 - q)

            evacuate_onehot(0, 0)
            exponentials(0, 0)
            evacuate(0, 0)
            edge_functions(0)
            with act.Fori(1, NG // 4) as it:
                edge_functions(it)
            clipped_high(NG * 4 - 2, 0)
            clipped_high(NG * 4 - 1, 1)

            for b in range(6):
                act.wait_ge(f_wp, b + 1)
                dst = (wih_t if b < 3 else whh_t)[:, (b % 3) * 512:(b % 3 + 1) * 512]
                nc.scalar.activation(dst, ps[:, b, :], ACT.Copy).then_inc(f_ws, 1)

            def turned(t):
                act.wait_ge(f_t, nth(t))
                nc.scalar.activation(tr4, ps[:, 0, :], ACT.Copy).then_inc(f_ts, 1)

            def sigmoids(t, q):
                act.wait_ge(f_gate, nth(t))
                if not is_zero(t):
                    act.wait_ge(f_cat, nth(t - 1))
                nc.scalar.activation(rz, ps[:, 1 + 4 * q, :], ACT.Sigmoid).then_inc(f_sig, 1)

            def deviation(var, std, i):
                act.wait_ge(var, nth(i))
                nc.scalar.activation(st[:, 8:9], st[:, 7:8], ACT.Sqrt, bias=eps_c[:, :]).then_inc(std, 1)

            def functions(t, q):
                if is_tile(t + 1):
                    turned(t + 1)
                act.wait_ge(f_n0, nth(t))
                nc.scalar.activation(wb, wa, ACT.Tanh).then_inc(f_tanh, 1)
                deviation(f_var, f_std, t)
                if is_tile(t - 1):
                    for i in range(2):
                        deviation(f_var2, f_std2, (t - 1) * 2 + i)
                if is_tile(t + 1):
                    sigmoids(t + 1, 1 - q)
                act.wait_ge(f_ct, nth(t))
                nc.scalar.activation(cat_t, ps[:, 3, :], ACT.Copy).then_inc(f_cts, 1)

            turned(0)
            sigmoids(0, 0)
            last_loop(act, functions)
            for i in range(2):
                deviation(f_var2, f_std2, (NT - 1) * 2 + i)

        @block.vector
        def _(dve):
            step = Chain(dve, dve_steps)
            def move(out, src):
                return nc.vector.tensor_scalar(out, src, 1.0, None, ALU.mult)

            tt, ts, stt = nc.vector.tensor_tensor, nc.vector.tensor_scalar, nc.vector.scalar_tensor_tensor
            step(nc.vector.memset(wk[:, :, :], 0.0))
            nc.vector.memset(wt_b[:, ROW - 1:ROW], 0.0).then_inc(s_wzero, 1)
            dve.wait_ge(s_in, 48)
            step(ts(bk_i, dst_i, P - 1, None, ALU.bitwise_and))
            step(nc.vector.tensor_copy(dloc, bk_i))
            dve.wait_ge(s_const, 1)
            dve.wait_ge(pool_steps, 11)
            one_row = ones[0:EP, 0:1].broadcast_to([EP, ET])
            for k, ids in enumerate((dst_i, src_i)):
                step(ts(bk_i, ids, 7, None, ALU.arith_shift_right))
                step(nc.vector.tensor_copy(bk_f, bk_i))
                with dve.Fori(0, NB) as b:
                    ts(at(mask8, b, ET, ET), bk_f, at(iota[0:EP, :], b), 0.0, ALU.is_equal, ALU.add,
                       accum_out=at(cnt[0:EP, :], b)).then_inc(s_counted, 1)
                dve.wait_ge(s_totals, k + 1)
                step(nc.vector.tensor_copy(total[:, 0:NB], ps[:, 4, 0:NB]))
                step(nc.vector.memset(total[:, NB:NB + 1], 0.0))
                step(nc.vector.tensor_tensor_scan(base[:, :], ones[:, 0:NB], total[:, 0:NB], 0.0, ALU.mult, ALU.add))
                step(tt(base[:, :], base[:, :], total[:, 0:NB], ALU.subtract))
                step(stt(out=base[0:EP, :], in0=base[0:EP, :], scalar=-1.0, in1=ps[0:EP, 5, 0:NB],
                         op0=ALU.add, op1=ALU.add))
                step(ts(gsz_i[:, 0, :], total[:, 0:NB], float(GE - 1), None, ALU.add))
                step(ts(gsz_i[:, 1, :], gsz_i[:, 0, :], GE.bit_length() - 1, None, ALU.arith_shift_right))
                step(nc.vector.tensor_copy(gsz, gsz_i[:, 1, :]))
                step(nc.vector.tensor_tensor_scan(gend, ones[:, 0:NB], gsz, 0.0, ALU.mult, ALU.add))
                step(tt(cmp[0:GP], gend[0:GP, :].unsqueeze(1).broadcast_to([GP, 4, NB]),
                        gidx[0:GP, :].unsqueeze(2).broadcast_to([GP, 4, NB]), ALU.is_le))
                step(nc.vector.tensor_reduce(tmap_f[0:GP, :], cmp[0:GP], AX_X, ALU.add))
                step(ts(tmap_i[0:GP, 2 * k, :], tmap_f[0:GP, :], float(NT - 1), None, ALU.min))

                def over_buckets(a):
                    return a.unsqueeze(1).broadcast_to([GP, 4, NB])

                step(stt(out=short, in0=gsz, scalar=-float(GE), in1=total[:, 0:NB],
                         op0=ALU.mult, op1=ALU.add))
                step(tt(weighed[0:GP], cmp[0:GP], over_buckets(short[0:GP, :]), ALU.mult))
                step(nc.vector.tensor_reduce(tmap_f[0:GP, :], weighed[0:GP], AX_X, ALU.add))
                step(stt(out=tmap_f[0:GP, :], in0=gidx[0:GP, :], scalar=float(GE), in1=tmap_f[0:GP, :],
                         op0=ALU.mult, op1=ALU.add))
                step(ts(tmap_f[0:GP, :], tmap_f[0:GP, :], float(E), None, ALU.min))
                step(nc.vector.tensor_copy(tmap_i[0:GP, 2 * k + 1, :], tmap_f[0:GP, :]))
                step(tt(weighed[0:GP], cmp[0:GP], over_buckets(total[0:GP, 1:NB + 1]), ALU.mult))
                step(nc.vector.tensor_reduce(left_f[0:GP, k, :], weighed[0:GP], AX_X, ALU.add))
                step(ts(left_f[0:GP, k, :], left_f[0:GP, k, :], total[0:GP, 0:1], None, ALU.add))
                step(tt(left_f[0:GP, k, :], left_f[0:GP, k, :], tmap_f[0:GP, :], ALU.subtract))
                ts(left_f[0:GP, k, :], left_f[0:GP, k, :], float(P), None, ALU.mult).then_inc(s_map, 1)
                held = step.done
                with dve.Fori(0, NB // 2) as it:
                    step.loop(held, it, 2)
                    for q in range(2):
                        m = at(mask8, it * 2 + q, ET, ET)
                        step(nc.vector.tensor_tensor_scan(scan[q], one_row, m, at(base[0:EP, :], it * 2 + q),
                                                          ALU.mult, ALU.add))
                        dve.wait_ge(s_psum, nth(it * 2 + (k * NB + q - 2), HEAD))
                        tt(prod[q], scan[q], m, ALU.mult).then_inc(s_prod, 1)
                step.loop_ended(held, NB // 2, 2)
                dve.wait_ge(s_prod, NB * (k + 1))
                dve.wait_ge(s_psum, nth((k + 1) * NB - 1, HEAD))
                nc.vector.tensor_copy(slot[k], ps[0:EP, 0:4, :].rearrange("p b c -> p (b c)")[:, 0:ET]
                                      ).then_inc(s_slots, 1)
            dve.wait_ge(s_slots, 2)
            nc.vector.memset(x_all[:, (NT - 1) * MSG:NT * MSG], 0.0).then_inc(s_xclr, 1)
            nc.vector.memset(tail, 0.0).then_inc(s_tail, 1)

            for f, field in enumerate((src_i, dloc, w_f, slot[1])):
                nc.vector.tensor_copy(recs.rearrange("p (t f) -> p t f", f=4)[:, :, f], field).then_inc(s_packed, 1)
            step(nc.vector.tensor_copy(slot_f, slot[0]))
            dve.wait_ge(s_place, 1)
            step(tt(place, place, slot_f, ALU.not_equal))
            nc.vector.tensor_reduce(moved[0:EP, :], place, AX_X, ALU.add).then_inc(s_moved, 1)
            dve.wait_ge(s_moved, 2)
            nc.vector.tensor_copy(moved_i[:, :], ps[0:1, 4, 0:1]).then_inc(s_flag, 1)

            dve.wait_ge(s_wt, 16 * 17)
            for c in range(4):
                step(nc.vector.tensor_reduce(var[:, c:c + 1], wk[:, c, 0:D], AX_X, ALU.add))
            step(ts(var[:, :], var[:, :], 1.0 / D, None, ALU.mult))
            for c in range(4):
                step(ts(wk[:, c, 0:D], wk[:, c, 0:D], var[:, c:c + 1], None, ALU.subtract))
            step(ts(nbetak_b[:, :], betak_b[:, :], -1.0, None, ALU.mult))

            def onehot(out, local):
                return tt(grouped(out), iota_g, over_nodes(local), ALU.is_equal)

            dve.wait_ge(s_rowld, 64)
            held = step.done

            def prepare_messages(it):
                step.loop(held, it, 32)
                for u in range(4):
                    g, q = it * 4 + u, u % 2
                    if not is_zero(it):
                        dve.wait_ge(m_out[u], 16 * G * it)
                    dve.wait_ge(m_gate, nth(g - 4, HEAD))
                    dve.wait_ge(m_oht, nth(g - 2, HEAD))
                    dve.wait_ge(s_recs, 64 * (it + 1) + HEAD)
                    step(move(recq[:, u, :], at(rec_all, g, 16, 16)))
                    local, there = rec(u)[:, :, 1], rec(u)[:, :, 3]
                    step(stt(out=local, in0=slot128[:, :], scalar=at(left[:, 0, :], g), in1=local,
                             op0=ALU.subtract, op1=ALU.max))
                    step(ts(far[:, :], local, float(P), float(FAR), ALU.is_ge, ALU.mult))
                    step(tt(there, there, far[:, :], ALU.max))
                    step(move(at(rec_all, g, 16, 16), recq[:, u, :]))
                    onehot(oh_r[:, q, :], rec(u)[:, :, 1]).then_inc(m_oh, 1)
                    step(nc.vector.tensor_copy(idxq[:, u, :], rec(u)[:, :, 3]))
                    step(nc.vector.tensor_copy(sloc_i[:, :], rec(u)[:, :, 0]))
                    step(ts(sloc_i[:, :], sloc_i[:, :], P - 1, None, ALU.bitwise_and))
                    nc.vector.tensor_copy(msgs[:, u, :, D], sloc_i[:, :]).then_inc(m_loc, 1)

            prepare_messages(0)
            with dve.Fori(1, NG // 4) as it:
                prepare_messages(it)
            step.loop_ended(held, NG // 4, 32)
            dve.wait_ge(s_recs, 64 * GP + HEAD)
            read_ahead = rec_all[:, NG * 16:NX * 16].rearrange("p (n f) -> p n f", f=4)
            step(ts(read_ahead[:, :, 1], read_ahead[:, :, 1], float(P), None, ALU.add))

            step(nc.vector.memset(agg_all, 0.0))
            dve.wait_ge(a_in[0], 16)

            def mask_pads(g, u):
                local = msgs[:, u, :, D]
                step(stt(out=local, in0=slot128[:, :], scalar=at(left[:, 1, :], g), in1=local,
                         op0=ALU.subtract, op1=ALU.max))

            mask_pads(0, 0)
            onehot(oh_r[:, 0, :], msgs[:, 0, :, D]).then_inc(a_oh, 1)
            held = step.done
            dve.wait_ge(s_mapld, 32)
            dve.sem_inc(a_add, HEAD)
            with dve.Fori(0, NG // 4) as it:
                step.loop(held, it, 4)
                nt = tiles_of(ENG.DVE, 1, it * 4, 4)
                for u in range(4):
                    g, q = it * 4 + u, u % 2
                    dve.wait_ge(a_in[(u + 1) % 4], 16 * (it + 1 + (u == 3)))
                    mask_pads(g + 1, (u + 1) % 4)
                    dve.wait_ge(a_sum, nth(g - 1, HEAD))
                    onehot(oh_r[:, 1 - q, :], msgs[:, (u + 1) % 4, :, D]).then_inc(a_oh, 1)
                    dve.wait_ge(a_sum, nth(g, HEAD))
                    dve.wait_ge(a_add, nth(g - 1, HEAD))
                    tt(at(agg_all, nt[u], D, MSG), at(agg_all, nt[u], D, MSG), ps[:, q, 0:D], ALU.add).then_inc(a_add, 1)
            step.loop_ended(held, NG // 4, 4)

            def norm_stats(src, out):
                nc.vector.bn_stats(st[:, 0:6], src)
                dve.drain()
                nc.vector.bn_aggr(st[:, 6:8], st[:, 0:6]).then_inc(out, 1)

            def normalize(out, src, deviation, i):
                dve.wait_ge(deviation, i)
                step(nc.vector.reciprocal(st[:, 9:10], st[:, 8:9]))
                return ts(out, src, st[:, 6:7], st[:, 9:10], ALU.subtract, ALU.mult)

            dve.wait_ge(a_add, nth(NG - 1, HEAD))
            dve.wait_ge(s_x, 32)
            held = step.done

            def node_stage(t):
                step.loop(held, t, 9)
                move(y_sb[:, :], at(agg_all, t, D, MSG)).then_inc(n_agg, 1)
                dve.wait_ge(n_lin, nth(t))
                step(stt(out=y_sb[:, :], in0=ps[:, 2, 0:D], scalar=0.0, in1=at(x_all, t, D, MSG),
                         op0=ALU.max, op1=ALU.add))
                norm_stats(y_sb[:, :], n_var)
                if not is_zero(t):
                    dve.wait_ge(n_st, 32 * t)
                normalize(x1_sb[:, :], y_sb[:, :], n_std, nth(t * 2)).then_inc(n_x1, 1)
                dve.wait_ge(n_hv, nth(t, HEAD))
                pj = row[:, D + 1:D + 1 + K]
                norm_stats(pj, n_var)
                step(normalize(pj, pj, n_std, nth(t * 2 + 1)))
                step(tt(pj, pj, gp_b[:, :], ALU.mult))
                step(tt(pj, pj, betap_b[:, :], ALU.add))
                step(ts(pj, pj, 0.0, None, ALU.max))
                step(move(node_of(t, K), pj))
                step(move(at(node[:, K:], t, 1, K + 1), row[:, D:D + 1]))
                nc.vector.memset(row[:, D:D + 1], 1.0).then_inc(n_row, 1)

            dve.sem_inc(n_row, HEAD)
            node_stage(0)
            with dve.Fori(1, NT) as t:
                node_stage(t)
            step.loop_ended(held, NT, 9)
            dve.wait_ge(n_row, nth(NT - 1, HEAD))

            dve.wait_ge(n_st, 32 * NT)
            step(nc.vector.memset(arena_n[:, 0:2 * NA], 0.0))
            step(nc.vector.memset(mrun[:, :], 0.0))
            step(nc.vector.memset(kron[:, :, K * K:K * K + 1], 1.0))
            step(nc.vector.memset(kron[:, :, K * K + 1:4 * KC], 0.0))
            step(nc.vector.tensor_copy(chi[:, :, D:RC], ones[:, 0:4].rearrange("p (a b) -> p a b", a=2)))
            dve.sem_inc(k_n, HEAD)

            def take_records(g, u):
                step(move(recq[:, u, :], at(rec_all, g, 16, 16)))
                nc.vector.tensor_copy(idxq[:, u, :], rec(u)[:, :, 0]).then_inc(l_rec, 1)

            def products(tau, u, q, j):
                dve.wait_ge(k_t, nth(tau - 4, HEAD))
                tt(kron[:, j, 0:K * K].rearrange("p (a b) -> p a b", a=K),
                   feat[:, u, j, D + 1:D + 1 + K].unsqueeze(2).broadcast_to([P, K, K]),
                   dsb[:, q, j, 0:K].unsqueeze(1).broadcast_to([P, K, K]), ALU.mult).then_inc(k_kron, 1)

            def local_onehot(g, u):
                onehot(oh_r[:, u, :], rec(u)[:, :, 1]).then_inc(l_oh, 1)

            def logits(g, u, q, it):
                dve.wait_ge(l_d, nth(g))
                step(nc.vector.tensor_copy(dsb[:, q].rearrange("p j k -> p (j k)"), ps[:, 7, 0:G * (K + 1)]))
                step(ts(valid[:, :], rec(u)[:, :, 1], float(P), None, ALU.is_lt))
                dve.wait_ge(l_feat[u], 16 * G * (it + 1))
                step(tt(lg[:, q, :], feat[:, u, :, ROW - 1], dsb[:, q, :, K], ALU.add))
                step(stt(out=lg[:, q, :], in0=lg[:, q, :], scalar=0.0, in1=valid[:, :], op0=ALU.max, op1=ALU.mult))
                tt(grouped(ohl[:, :]), grouped(oh[:, u, :]), over_nodes(lg[:, q, :]), ALU.mult).then_inc(l_ohl, 1)

            def group_max(g, q):
                dve.wait_ge(l_ohlt, nth(g))
                nc.vector.tensor_reduce(mg[:, q:q + 1], ps[:, 6, :], AX_X, ALU.max).then_inc(l_mg, 1)

            def differences(g, q, nt):
                dve.wait_ge(l_mg, nth(g, HEAD))
                mr, m = at(mrun, nt), mg[:, q:q + 1]
                step(tt(mnew[:, :], mr, m, ALU.max))
                step(tt(edd[:, q, 4:5], mr, mnew[:, :], ALU.subtract))
                step(tt(edd[:, q, 5:6], m, mnew[:, :], ALU.subtract))
                step(move(mr, mnew[:, :]))
                dve.wait_ge(l_me, nth(g))
                tt(edd[:, q, 0:4], lg[:, q, :], ps[:, 7, P:P + G], ALU.subtract).then_inc(l_dd, 1)

            def clipped_low(tau, j):
                dve.wait_ge(k_hi, nth(tau))
                tt(clo[:, j % 2, :], clipped[:, j % 2, 0:D], chi[:, j % 2, 0:D], ALU.subtract).then_inc(k_lo, 1)

            def normalized(tau, j):
                dve.wait_ge(k_rs, nth(tau))
                step(stt(out=normed[:, j % 2, :], in0=ps[:, 2 + j % 2, 0:D], scalar=rstd[:, j:j + 1],
                         in1=gk_b[:, :], op0=ALU.mult, op1=ALU.mult))
                dve.wait_ge(k_lo, nth(tau - 2, HEAD))
                tt(clipped[:, j % 2, 0:D], normed[:, j % 2, :], nbetak_b[:, :], ALU.max).then_inc(k_n, 1)

            def add_kron(g, nt):
                dve.wait_ge(k_seg, nth(g * 4 + 3, HEAD))
                ksum = at(x_all, nt, MSG, MSG)
                tt(ksum, ksum, ps[:, 4, 0:MSG], ALU.add).then_inc(l_ksum, 1)

            def weighted_low(g, u, q, j):
                dve.wait_ge(l_hi, nth(g * 4 + j))
                stt(out=wlo[:, j % 2, :], in0=feat[:, u, j, 0:RC], scalar=ee[:, q, j:j + 1], in1=whi[:, j % 2, :],
                    op0=ALU.mult, op1=ALU.subtract).then_inc(l_lo, 1)

            def add_context(g, q, nt):
                dve.wait_ge(l_ctx, nth(g * 4 + 3, HEAD))
                att = at(agg_all, nt, MSG, MSG)
                step(ts(att, att, ee[:, q, 4:5], None, ALU.mult))
                stt(out=att, in0=ps[:, 5, 0:MSG], scalar=ee[:, q, 5:6], in1=att,
                    op0=ALU.mult, op1=ALU.add).then_inc(l_comb, 1)

            for s in (l_mg, l_dd, l_ksum, l_comb, k_lo):
                dve.sem_inc(s, HEAD)
            for u in range(3):
                take_records(u, u)
            dve.wait_ge(l_rec, 3)
            first = tiles_of(ENG.DVE, 0, 0, 1)
            local_onehot(0, 0)
            logits(0, 0, 0, 0)
            group_max(0, 0)
            differences(0, 0, first[0])
            products(0, 0, 0, 0)
            products(1, 0, 0, 1)
            local_onehot(1, 1)
            held = step.done
            PER = 1 + G + 4 + 4 + 1

            def edge_groups(it, nt, before_nt):
                for u in range(4):
                    g, q, u1, q1 = it * 4 + u, u % 2, (u + 1) % 4, 1 - u % 2
                    started = u > 0 or not is_zero(it)
                    products(g * 4 + 2, u, q, 2)
                    if started:
                        clipped_low(g * 4 - 2, 2)
                        normalized(g * 4 - 1, 3)
                    if started:
                        weighted_low(g - 1, (u + 3) % 4, q1, 3)
                    take_records(g + 3, (u + 3) % 4)
                    products(g * 4 + 3, u, q, 3)
                    if started:
                        clipped_low(g * 4 - 1, 3)
                    normalized(g * 4, 0)
                    weighted_low(g, u, q, 0)
                    logits(g + 1, u1, q1, it + 1 if u == 3 else it)
                    if started:
                        add_context(g - 1, q1, nt[u - 1] if u > 0 else before_nt)
                    products(g * 4 + 4, u1, q1, 0)
                    clipped_low(g * 4, 0)
                    normalized(g * 4 + 1, 1)
                    weighted_low(g, u, q, 1)
                    group_max(g + 1, q1)
                    products(g * 4 + 5, u1, q1, 1)
                    clipped_low(g * 4 + 1, 1)
                    normalized(g * 4 + 2, 2)
                    if started:
                        add_kron(g - 1, nt[u - 1] if u > 0 else before_nt)
                    weighted_low(g, u, q, 2)
                    local_onehot(g + 2, (u + 2) % 4)
                    differences(g + 1, q1, nt[u + 1])

            step.loop(held, 0, 4 * PER)
            edge_groups(0, tiles_of(ENG.DVE, 0, 0, 5), None)
            held2 = step.done
            assert held2 == held + 4 * PER - 2
            with dve.Fori(1, NG // 4) as it:
                step.loop(held2 - 4 * PER, it, 4 * PER)
                loaded = tiles_of(ENG.DVE, 0, it * 4 - 1, 6)
                edge_groups(it, loaded[1:], loaded[0])
            step.loop_ended(held2 - 4 * PER, NG // 4, 4 * PER)
            clipped_low(NG * 4 - 2, 2)
            normalized(NG * 4 - 1, 3)
            last_nt = tiles_of(ENG.DVE, 0, NG - 1, 1)[0]
            weighted_low(NG - 1, 3, 1, 3)
            clipped_low(NG * 4 - 1, 3)
            add_kron(NG - 1, last_nt)
            add_context(NG - 1, 1, last_nt)

            dve.wait_ge(f_w, 16 * 10)
            dve.wait_ge(l_ksum, nth(NG - 1, HEAD))
            dve.wait_ge(l_comb, nth(NG - 1, HEAD))

            def last_norm(out, src, var, std, i):
                norm_stats(src, var)
                return normalize(out, src, std, nth(i))

            def context_of(t):
                att = at(agg_all, t, MSG, MSG)
                step(ts(st[:, 10:11], att[:, D:MSG], 1e-30, None, ALU.max))
                step(nc.vector.reciprocal(st[:, 11:12], st[:, 10:11]))
                if not is_zero(t):
                    dve.wait_ge(f_t, nth(t - 1))
                ts(cx, att[:, 0:D], st[:, 11:12], 0.0, ALU.mult, ALU.max).then_inc(f_pre, 1)

            def features(t, q):
                ksum, gates_n = at(x_all, t, MSG, MSG), ps[:, 2 + 4 * q, :]
                dve.wait_ge(f_sig, nth(t))
                step(tt(wa, rz[:, 0:D], gates_n[:, D:2 * D], ALU.mult))
                tt(wa, wa, gates_n[:, 0:D], ALU.add).then_inc(f_n0, 1)
                dve.wait_ge(f_x, 16 * (t + 1))
                step(nc.vector.tensor_copy(xr[q], xf[q]))
                if not is_zero(t):
                    dve.wait_ge(f_ct, nth(t - 1))
                step(stt(out=cat[:, D:2 * D], in0=betak_b[:, :], scalar=ksum[:, D:MSG], in1=ksum[:, 0:D],
                         op0=ALU.mult, op1=ALU.add))
                dve.wait_ge(f_tanh, nth(t))
                step(tt(wa, xf[q], wb, ALU.subtract))
                step(tt(wa, wa, rz[:, D:2 * D], ALU.mult))
                step(tt(wa, wa, wb, ALU.add))
                step(ts(wa, wa, 0.0, None, ALU.max))
                step(last_norm(wb, wa, f_var, f_std, t))
                step(tt(wb, wb, gln_b, ALU.mult))
                tt(cat[:, 0:D], wb, bln_b, ALU.add).then_inc(f_cat, 1)

            def result(t, q):
                dve.wait_ge(f_lin, nth(t))
                step(last_norm(ya, ps[:, 4 + 3 * q, 0:D], f_var2, f_std2, t * 2))
                step(tt(ya, ya, gc_b, ALU.mult))
                step(tt(ya, ya, bc_b, ALU.add))
                step(stt(out=yb, in0=ya, scalar=0.0, in1=xr[q], op0=ALU.max, op1=ALU.add))
                if not is_zero(t):
                    dve.wait_ge(f_st, 16 * t)
                last_norm(outb, yb, f_var2, f_std2, t * 2 + 1).then_inc(f_out, 1)

            def last_stage(t, q):
                features(t, q)
                if is_tile(t + 2):
                    context_of(t + 2)
                if is_tile(t - 1):
                    result(t - 1, 1 - q)

            PER2 = 18
            start = [0]

            def enter(it=None):
                if it is None:
                    start[0] = step.done
                else:
                    step.loop(start[0], it, 2 * PER2)

            context_of(0)
            context_of(1)
            last_loop(dve, last_stage, enter, lambda n: step.loop_ended(start[0], n, 2 * PER2))
            result(NT - 1, (NT - 1) % 2)

        @block.tensor
        def _(pe):
            mm = nc.tensor.matmul

            def turn(out, src):
                return nc.tensor.transpose(out, src, ident[:, :])

            pe.wait_ge(s_const, 1)
            pe.wait_ge(pool_steps, 11)

            pe.sem_inc(s_psum, HEAD)
            for k in range(2):
                pe.wait_ge(s_counted, NB * (k + 1))
                pe.wait_ge(s_map, k)
                mm(ps[:, 4, 0:NB], ones[0:EP, :], cnt[0:EP, :], start=True, stop=True)
                mm(ps[0:EP, 5, 0:NB], before[0:EP, 0:EP], cnt[0:EP, :], start=True, stop=True).then_inc(s_totals, 1)
                pe.wait_ge(s_slots, k)

                def add_product(b, q, first=False, last=False):
                    pe.wait_ge(s_prod, nth(b))
                    for i in range(-(-ET // 512)):
                        n = min(512, ET - 512 * i)
                        ins = mm(ps[0:EP, i, 0:n], ident[0:EP, 0:EP], prod[q][:, i * 512:i * 512 + n],
                                 start=first, stop=last)
                    ins.then_inc(s_psum, 1)

                add_product(k * NB, 0, first=True)
                add_product(k * NB + 1, 1)
                with pe.Fori(1, NB // 2 - 1) as it:
                    for q in range(2):
                        add_product(it * 2 + (k * NB + q), q)
                add_product((k + 1) * NB - 2, 0)
                add_product((k + 1) * NB - 1, 1, last=True)

            pe.wait_ge(s_moved, 1)
            mm(ps[:, 4, 0:1], ones[0:EP, :], moved[0:EP, :], start=True, stop=True).then_inc(s_moved, 1)

            pe.wait_ge(s_flag, 1)
            pe.wait_ge(s_w0, 16)
            for ic in range(2):
                for oc in range(2):
                    i = 2 * ic + oc
                    ins = turn(ps[:, 7, i * P:(i + 1) * P], tr2[:, oc, ic * P:(ic + 1) * P])
            ins.then_inc(s_w0t, 1)
            pe.wait_ge(s_mapld, 32)
            pe.wait_ge(s_x, 32)
            pe.sem_inc(m_oht, HEAD)
            with pe.Fori(0, NG // 4) as it:
                nt = tiles_of(ENG.PE, 0, it * 4, 4)
                for u in range(4):
                    g, q = it * 4 + u, u % 2
                    pe.wait_ge(m_oh, nth(g))
                    for j in range(G):
                        ins = turn(ps[:, q, j * P:(j + 1) * P], oh[:, q, j * P:(j + 1) * P])
                    ins.then_inc(m_oht, 1)
                    pe.wait_ge(m_ohts, nth(g))
                    for j in range(G):
                        pe.wait_ge(m_msg, nth((g - 1) * 4 + j, HEAD))
                        mm(ps[:, 2 + j, 0:D], oh_t[:, q, j * P:(j + 1) * P], at(x_all, nt[u], D, MSG),
                           start=True, stop=True).then_inc(m_x, 1)

            pe.sem_inc(a_sum, HEAD)
            with pe.Fori(0, NG // 4) as it:
                for u in range(4):
                    g, q = it * 4 + u, u % 2
                    pe.wait_ge(a_oh, nth(g))
                    pe.wait_ge(a_add, nth(g - 2, HEAD))
                    for j in range(G):
                        ins = mm(ps[:, q, 0:D], oh[:, q, j * P:(j + 1) * P], msgs[:, u, j, 0:D],
                                 start=(j == 0), stop=(j == G - 1))
                    ins.then_inc(a_sum, 1)

            pe.wait_ge(s_wt, 16 * 17)
            pe.wait_ge(s_wzero, 1)
            pe.wait_ge(act_steps, 1)
            with pe.Fori(0, NT) as t:
                pe.wait_ge(n_agg, nth(t))
                for c in range(2):
                    ins = turn(ps[:, 0, c * P:(c + 1) * P], y_sb[:, c * P:(c + 1) * P])
                ins.then_inc(n_t, 1)
                pe.wait_ge(n_ts, nth(t * 2))
                for c in range(2):
                    ins = mm(ps[:, 2, 0:D], tr2[:, 0, c * P:(c + 1) * P], w0_t[:, c * D:(c + 1) * D],
                             start=(c == 0), stop=(c == 1))
                ins.then_inc(n_lin, 1)
                pe.wait_ge(n_x1, nth(t))
                for c in range(2):
                    ins = turn(ps[:, 1, c * P:(c + 1) * P], x1_sb[:, c * P:(c + 1) * P])
                ins.then_inc(n_t, 1)
                pe.wait_ge(n_ts, nth(t * 2 + 1))
                pe.wait_ge(n_hv, nth(t - 1, HEAD))
                mm(ps[:, 3, 0:ROW], ones[0:1, :], wt_b[:, :], start=True, stop=False)
                for c in range(2):
                    ins = mm(ps[:, 3, 0:ROW], tr2[:, 1, c * P:(c + 1) * P], wt[:, c, :],
                             start=False, stop=(c == 1))
                ins.then_inc(n_tab, 1)

            for s in (k_t, k_h, k_seg, l_ctx):
                pe.sem_inc(s, HEAD)

            def turn_products(tau, j):
                pe.wait_ge(k_kron, nth(tau))
                pe.wait_ge(k_ts, nth(tau - 2, HEAD))
                for c in range(4):
                    ins = turn(ps[0:KC, j % 2, c * P:(c + 1) * P], kron[:, j, c * KC:(c + 1) * KC])
                ins.then_inc(k_t, 1)

            def linear(tau, j):
                pe.wait_ge(k_ts, nth(tau, HEAD))
                pe.wait_ge(k_n, nth(tau - 2, HEAD))
                for c in range(4):
                    ins = mm(ps[:, 2 + j % 2, 0:HC], kron_t[0:KC, j % 2, c * P:(c + 1) * P], wk[0:KC, c, :],
                             start=(c == 0), stop=(c == 3))
                ins.then_inc(k_h, 1)

            def onehot_of(u, j):
                return oh_r[:, u, j * P:(j + 1) * P]

            def sum_kron(g, u, j):
                pe.wait_ge(k_lo, nth(g * 4 + j, HEAD))
                if j == 0:
                    pe.wait_ge(l_ksum, nth(g - 1, HEAD))
                mm(ps[:, 4, 0:RC], onehot_of(u, j), chi[:, j % 2, :], start=(j == 0), stop=False)
                mm(ps[:, 4, 0:D], onehot_of(u, j), clo[:, j % 2, :], start=False, stop=(j == G - 1)).then_inc(k_seg, 1)

            def turn_onehot(g, u):
                pe.wait_ge(l_oh, nth(g))
                pe.wait_ge(l_mg, nth(g - 1, HEAD))
                for j in range(G):
                    ins = turn(ps[:, 6, j * P:(j + 1) * P], oh[:, u, j * P:(j + 1) * P])
                ins.then_inc(l_oht, 1)

            def dst_rows(g, q, nt):
                pe.wait_ge(l_ohts, nth(g))
                pe.wait_ge(l_dd, nth(g - 1, HEAD))
                for j in range(G):
                    ins = mm(ps[:, 7, j * (K + 1):(j + 1) * (K + 1)], oh_t[:, q, j * P:(j + 1) * P], node_of(nt),
                             start=True, stop=True)
                ins.then_inc(l_d, 1)

            def turn_logits(g):
                pe.wait_ge(l_ohl, nth(g))
                for j in range(G):
                    ins = turn(ps[:, 6, j * P:(j + 1) * P], ohl[:, j * P:(j + 1) * P])
                ins.then_inc(l_ohlt, 1)

            def edge_max(g, q):
                pe.wait_ge(l_mg, nth(g, HEAD))
                for j in range(G):
                    ins = mm(ps[:, 7, P + j:P + j + 1], oh_t[:, q, j * P:(j + 1) * P], mg[:, q:q + 1],
                             start=True, stop=True)
                ins.then_inc(l_me, 1)

            def context(g, u, j):
                pe.wait_ge(l_lo, nth(g * 4 + j))
                if j == 0:
                    pe.wait_ge(l_comb, nth(g - 1, HEAD))
                mm(ps[:, 5, 0:RC], onehot_of(u, j), whi[:, j % 2, :], start=(j == 0), stop=False)
                mm(ps[:, 5, 0:RC], onehot_of(u, j), wlo[:, j % 2, :], start=False, stop=(j == G - 1)).then_inc(l_ctx, 1)

            first = tiles_of(ENG.PE, 0, 0, 1)
            pe.wait_ge(n_row, nth(NT - 1, HEAD))
            turn_onehot(0, 0)
            dst_rows(0, 0, first[0])
            turn_logits(0)
            edge_max(0, 0)
            turn_products(0, 0)

            def edge_groups(it):
                nt = tiles_of(ENG.PE, 0, it * 4, 5)
                for u in range(4):
                    g, q, q1 = it * 4 + u, u % 2, 1 - u % 2
                    before, u_before = g - 1, (u + 3) % 4
                    started = u > 0 or not is_zero(it)
                    turn_products(g * 4 + 1, 1)
                    if started:
                        context(before, u_before, 2)
                    linear(g * 4, 0)
                    turn_onehot(g + 1, (u + 1) % 4)
                    if started:
                        sum_kron(before, u_before, 1)

                    turn_products(g * 4 + 2, 2)
                    if started:
                        context(before, u_before, 3)
                    dst_rows(g + 1, q1, nt[u + 1])
                    linear(g * 4 + 1, 1)
                    if started:
                        sum_kron(before, u_before, 2)

                    turn_products(g * 4 + 3, 3)
                    turn_logits(g + 1)
                    linear(g * 4 + 2, 2)
                    context(g, u, 0)
                    if started:
                        sum_kron(before, u_before, 3)

                    turn_products(g * 4 + 4, 0)
                    context(g, u, 1)
                    linear(g * 4 + 3, 3)
                    edge_max(g + 1, q1)
                    sum_kron(g, u, 0)

            edge_groups(0)
            with pe.Fori(1, NG // 4) as it:
                edge_groups(it)
            for j in (2, 3):
                context(NG - 1, 3, j)
            for j in (1, 2, 3):
                sum_kron(NG - 1, 3, j)

            pe.wait_ge(f_w, 16 * 10)
            pe.wait_ge(l_comb, nth(NG - 1, HEAD))
            for b in range(6):
                for r in range(4):
                    c, o = divmod((b % 3) * 4 + r, 6)
                    ins = turn(ps[:, b, r * P:(r + 1) * P], raw_w[:, 6 * (b // 3) + o, c * P:(c + 1) * P])
                ins.then_inc(f_wp, 1)
            pe.wait_ge(f_ws, 6)

            def gates(out, lo, n, parts):
                both = ((bih_r, wih_t, 0), (bhh_r, whh_t, 2))
                both = [both[i] for i in parts]
                first = True
                for b, _, _ in both:
                    mm(out, ones[0:1, :], b[0:1, lo:lo + n], start=first, stop=False)
                    first = False
                for i, (_, w, x) in enumerate(both):
                    for c in range(2):
                        ins = mm(out, tr4[:, (x + c) * P:(x + c + 1) * P], w[:, c * 3 * D + lo:c * 3 * D + lo + n],
                                 start=False, stop=(i == len(both) - 1 and c == 1))
                return ins

            def gate_products(t, q):
                pe.wait_ge(f_pre, nth(t))
                pe.wait_ge(f_x, 16 * (t + 1))
                for c in range(2):
                    turn(ps[:, 0, c * P:(c + 1) * P], cx[:, c * P:(c + 1) * P])
                for c in range(2):
                    ins = turn(ps[:, 0, (2 + c) * P:(3 + c) * P], xf[q][:, c * P:(c + 1) * P])
                ins.then_inc(f_t, 1)
                pe.wait_ge(f_ts, nth(t))
                gates(ps[:, 1 + 4 * q, :], 0, 2 * D, (0, 1))
                gates(ps[:, 2 + 4 * q, 0:D], 2 * D, D, (0,))
                gates(ps[:, 2 + 4 * q, D:2 * D], 2 * D, D, (1,)).then_inc(f_gate, 1)

            def last_products(t, q):
                if is_tile(t + 1):
                    gate_products(t + 1, 1 - q)
                pe.wait_ge(f_cat, nth(t))
                for c in range(4):
                    ins = turn(ps[:, 3, c * P:(c + 1) * P], cat[:, c * P:(c + 1) * P])
                ins.then_inc(f_ct, 1)
                pe.wait_ge(f_cts, nth(t))
                out = ps[:, 4 + 3 * q, 0:D]
                mm(out, ones[0:1, :], bcr_r[0:1, :], start=True, stop=False)
                for c in range(4):
                    ins = mm(out, cat_t[:, c * P:(c + 1) * P], wc[:, c, :], start=False, stop=(c == 3))
                ins.then_inc(f_lin, 1)

            gate_products(0, 0)
            last_loop(pe, last_products)


INPUTS = ["x", "src", "dst", "edge_weight", "L0_gnn_W"] + ["L1_gnn_" + n for n in (
    "Wp", "bp", "gp", "betap", "Wk", "bk", "gk", "betak", "We", "be", "Wn", "bn", "W_ih", "W_hh", "b_ih", "b_hh",
    "g_ln", "beta_ln", "Wc", "bc", "gc", "betac")]


def kernel(**inputs):
    import numpy as _np
    import concourse.bacc as _bacc
    from concourse import mybir as _mybir
    from concourse.bass_utils import run_bass_kernel_spmd as _run

    nc = _bacc.Bacc("TRN2", target_bir_lowering=False, num_devices=1)
    arrays, io = {}, {}
    for name in INPUTS:
        a = _np.ascontiguousarray(inputs[name])
        arrays["in_" + name] = a
        io[name] = nc.dram_tensor("in_" + name, a.shape, _mybir.dt.from_np(a.dtype), kind="ExternalInput").ap()
    V, E = inputs["x"].shape[0], inputs["src"].shape[0]
    io["out"] = nc.dram_tensor("out", (V, D), F32, kind="ExternalOutput").ap()
    gnn_program(nc, io, V, E, 125)
    r = _run(nc, [arrays], core_ids=[0])
    return r.results[0]["out"]
```
